# Optimizing a Trainium2 kernel written in Bass

```python
import numpy as np
import jax
import jax.numpy as jnp

def _softmax(x, axis=-1):
    return jax.nn.softmax(x, axis=axis)

def _gelu(x):
    return jax.nn.gelu(x, approximate=True)

def _silu(x):
    return jax.nn.silu(x)

def _sigmoid(x):
    return jax.nn.sigmoid(x)

def _layernorm(x, axis=-1, eps=1e-05):
    m = jnp.mean(x, axis=axis, keepdims=True)
    v = jnp.var(x, axis=axis, keepdims=True)
    return (x - m) / jnp.sqrt(v + eps)

def _scatter_add(tgt, idx, src, axis=0):
    return tgt.at[idx].add(src)

def _segment_sum(src, seg, n):
    return jax.ops.segment_sum(src, seg, n)
kernel_name = 'mk_gnn_preln_d4_gnn_r8_0593c1'

def setup_inputs(seed: int=0):
    np.random.seed(seed)
    _w = jnp.asarray

    def _rec_inputs():
        import jax
        import jax.numpy as jnp
        _gk = jax.random.key(seed)
        x = -0.0006008 + 1.001 * jax.random.normal(jax.random.fold_in(_gk, 1), (6250, 128), jnp.float32)
        _s = jax.random.randint(jax.random.fold_in(_gk, 2), (50000,), 0, 6250, jnp.int32)
        _d = jax.random.randint(jax.random.fold_in(_gk, 3), (50000,), 0, 6250, jnp.int32)
        _loop = jnp.arange(6250, dtype=jnp.int32)
        src = jnp.concatenate([_s, _d, _loop])
        dst = jnp.concatenate([_d, _s, _loop])
        _o = jnp.argsort(dst, stable=True)
        src = src[_o]
        dst = dst[_o]
        edge_attr_128 = 2.93046e-05 + 1.00006 * jax.random.normal(jax.random.fold_in(_gk, 12), (106250, 128), jnp.float32)
        node_type_3 = jax.random.randint(jax.random.fold_in(_gk, 14), (6250,), 0, 3, jnp.int32)
        return (x, src, dst, edge_attr_128, node_type_3)
    x, src, dst, edge_attr_128, node_type_3 = _rec_inputs()

    def _L0_gnn_setup():
        import jax, jax.numpy as jnp
        import numpy as np
        EPS = 1e-05

        def typed_linear(x, types, W):
            out = jnp.zeros((x.shape[0], W.shape[2]), x.dtype)
            for t in range(W.shape[0]):
                out = jnp.where((types == t)[:, None], x @ W[t], out)
            return out

        def layer_norm(x, g, b):
            mu = jnp.mean(x, axis=-1, keepdims=True)
            var = jnp.mean((x - mu) ** 2, axis=-1, keepdims=True)
            return (x - mu) * jax.lax.rsqrt(var + EPS) * g + b
        key = jax.random.key(seed)
        ks = jax.random.split(key, 16)
        N, E, D, H, Dh, T, C = (2500, 40000, 128, 8, 16, 3, 64)
        s = 0.05
        return {'x': jax.random.normal(ks[0], (N, D), jnp.float32), 'global_context': jax.random.normal(ks[1], (C,), jnp.float32), 'Wk': jax.random.normal(ks[2], (T, D, H * Dh), jnp.float32) * s, 'Wq': jax.random.normal(ks[3], (T, D, H * Dh), jnp.float32) * s, 'Wv': jax.random.normal(ks[4], (T, D, H * Dh), jnp.float32) * s, 'rel_att': jax.random.normal(ks[5], (H, Dh, Dh), jnp.float32) * s, 'rel_msg': jax.random.normal(ks[6], (H, Dh, Dh), jnp.float32) * s, 'rel_pri': jnp.ones((H,), jnp.float32), 'Wa': jax.random.normal(ks[7], (T, H * Dh, H * Dh), jnp.float32) * s, 'skip': jnp.ones((T,), jnp.float32), 'ln_g': jnp.ones((H * Dh,), jnp.float32), 'ln_b': jnp.zeros((H * Dh,), jnp.float32), 'film_w': jax.random.normal(ks[8], (C, 2 * D), jnp.float32) * s, 'film_b': jnp.zeros((2 * D,), jnp.float32), 'ntype': jax.random.randint(ks[9], (N,), 0, T, jnp.int32), 'src': jax.random.randint(ks[10], (E,), 0, N, jnp.int32), 'dst': jax.random.randint(ks[11], (E,), 0, N, jnp.int32)}
    _L0_gnn_all = _L0_gnn_setup()
    _L0_gnn_in = {k: v for k, v in _L0_gnn_all.items() if k in ('global_context', 'Wk', 'Wq', 'Wv', 'rel_att', 'rel_msg', 'rel_pri', 'Wa', 'skip', 'ln_g', 'ln_b', 'film_w', 'film_b')}
    del _L0_gnn_all

    def _L1_gnn_setup():
        import jax, jax.numpy as jnp
        import numpy as np
        key = jax.random.key(seed)
        k1, k2, k3 = jax.random.split(key, 3)
        N, E, D = (6250, 75000, 128)
        x = jax.random.normal(k1, (N, D), dtype=jnp.float32)
        src = jax.random.randint(k2, (E,), 0, N, dtype=jnp.int64)
        dst = jax.random.randint(k3, (E,), 0, N, dtype=jnp.int64)
        return {'x': x, 'src': src, 'dst': dst}
    _L1_gnn_all = _L1_gnn_setup()
    _L1_gnn_in = {k: v for k, v in _L1_gnn_all.items() if k in ()}
    del _L1_gnn_all

    def _L2_gnn_setup():
        import jax, jax.numpy as jnp
        import numpy as np
        N_NODES = 2500
        N_EDGES = 80000
        D = 128
        key = jax.random.key(seed)
        ks = jax.random.split(key, 9)
        s = 1.0 / np.sqrt(D)
        return {'x': jax.random.normal(ks[0], (N_NODES, D), dtype=jnp.float32), 'edge_index': jax.random.randint(ks[1], (2, N_EDGES), 0, N_NODES, dtype=jnp.int64), 'edge_attr': jax.random.normal(ks[2], (N_EDGES, D), dtype=jnp.float32), 'W_root': jax.random.normal(ks[3], (D, D), dtype=jnp.float32) * s, 'b_root': jax.random.normal(ks[4], (D,), dtype=jnp.float32) * s, 'W_msg': jax.random.normal(ks[5], (D, D), dtype=jnp.float32) * s, 'W_src': jax.random.normal(ks[6], (D, D), dtype=jnp.float32) * s, 'W_dst': jax.random.normal(ks[7], (D, D), dtype=jnp.float32) * s, 'W_edge': jax.random.normal(ks[8], (D, D), dtype=jnp.float32) * s}
    _L2_gnn_all = _L2_gnn_setup()
    _L2_gnn_in = {k: v for k, v in _L2_gnn_all.items() if k in ('W_root', 'b_root', 'W_msg', 'W_src', 'W_dst', 'W_edge')}
    del _L2_gnn_all

    def _L3_gnn_setup():
        import jax, jax.numpy as jnp
        import numpy as np
        N = 12500
        E = 400000
        D_IN = 128
        D_OUT = 128
        EPS = 1e-05
        key = jax.random.key(seed)
        ks = jax.random.split(key, 8)
        x = jax.random.normal(ks[0], (N, D_IN), dtype=jnp.float32)
        edge_index = jax.random.randint(ks[1], (2, E), 0, N, dtype=jnp.int32)
        s = 1.0 / np.sqrt(D_IN)
        W_l = jax.random.uniform(ks[2], (D_IN, D_OUT), jnp.float32, -s, s)
        b_l = jax.random.uniform(ks[3], (D_OUT,), jnp.float32, -s, s)
        W_r = jax.random.uniform(ks[4], (D_IN, D_OUT), jnp.float32, -s, s)
        gamma = jnp.ones((D_OUT,), jnp.float32)
        beta = jnp.zeros((D_OUT,), jnp.float32)
        return {'x': x, 'edge_index': edge_index, 'W_l': W_l, 'b_l': b_l, 'W_r': W_r, 'gamma': gamma, 'beta': beta}
    _L3_gnn_all = _L3_gnn_setup()
    _L3_gnn_in = {k: v for k, v in _L3_gnn_all.items() if k in ('W_l', 'b_l', 'W_r', 'gamma', 'beta')}
    del _L3_gnn_all
    return {'x': x, 'src': src, 'dst': dst, 'edge_attr_128': edge_attr_128, 'node_type_3': node_type_3, 'L0_gnn_global_context': _L0_gnn_in['global_context'], 'L0_gnn_Wk': _L0_gnn_in['Wk'], 'L0_gnn_Wq': _L0_gnn_in['Wq'], 'L0_gnn_Wv': _L0_gnn_in['Wv'], 'L0_gnn_rel_att': _L0_gnn_in['rel_att'], 'L0_gnn_rel_msg': _L0_gnn_in['rel_msg'], 'L0_gnn_rel_pri': _L0_gnn_in['rel_pri'], 'L0_gnn_Wa': _L0_gnn_in['Wa'], 'L0_gnn_skip': _L0_gnn_in['skip'], 'L0_gnn_ln_g': _L0_gnn_in['ln_g'], 'L0_gnn_ln_b': _L0_gnn_in['ln_b'], 'L0_gnn_film_w': _L0_gnn_in['film_w'], 'L0_gnn_film_b': _L0_gnn_in['film_b'], 'L2_gnn_W_root': _L2_gnn_in['W_root'], 'L2_gnn_b_root': _L2_gnn_in['b_root'], 'L2_gnn_W_msg': _L2_gnn_in['W_msg'], 'L2_gnn_W_src': _L2_gnn_in['W_src'], 'L2_gnn_W_dst': _L2_gnn_in['W_dst'], 'L2_gnn_W_edge': _L2_gnn_in['W_edge'], 'L3_gnn_W_l': _L3_gnn_in['W_l'], 'L3_gnn_b_l': _L3_gnn_in['b_l'], 'L3_gnn_W_r': _L3_gnn_in['W_r'], 'L3_gnn_gamma': _L3_gnn_in['gamma'], 'L3_gnn_beta': _L3_gnn_in['beta']}

def reference(x, src, dst, edge_attr_128, node_type_3, L0_gnn_global_context, L0_gnn_Wk, L0_gnn_Wq, L0_gnn_Wv, L0_gnn_rel_att, L0_gnn_rel_msg, L0_gnn_rel_pri, L0_gnn_Wa, L0_gnn_skip, L0_gnn_ln_g, L0_gnn_ln_b, L0_gnn_film_w, L0_gnn_film_b, L2_gnn_W_root, L2_gnn_b_root, L2_gnn_W_msg, L2_gnn_W_src, L2_gnn_W_dst, L2_gnn_W_edge, L3_gnn_W_l, L3_gnn_b_l, L3_gnn_W_r, L3_gnn_gamma, L3_gnn_beta):
    import jax
    import jax.numpy as jnp

    def _L0_gnn_ref(x, global_context, Wk, Wq, Wv, rel_att, rel_msg, rel_pri, Wa, skip, ln_g, ln_b, film_w, film_b, ntype, src, dst):
        import jax, jax.numpy as jnp
        import numpy as np
        EPS = 1e-05

        def typed_linear(x, types, W):
            out = jnp.zeros((x.shape[0], W.shape[2]), x.dtype)
            for t in range(W.shape[0]):
                out = jnp.where((types == t)[:, None], x @ W[t], out)
            return out

        def layer_norm(x, g, b):
            mu = jnp.mean(x, axis=-1, keepdims=True)
            var = jnp.mean((x - mu) ** 2, axis=-1, keepdims=True)
            return (x - mu) * jax.lax.rsqrt(var + EPS) * g + b
        N, D = x.shape
        H, Dh, _ = rel_att.shape
        inv_sqrt_d = 1.0 / jnp.sqrt(jnp.asarray(Dh, x.dtype))
        k = typed_linear(x, ntype, Wk).reshape(N, H, Dh)
        q = typed_linear(x, ntype, Wq).reshape(N, H, Dh)
        v = typed_linear(x, ntype, Wv).reshape(N, H, Dh)
        kw = jnp.einsum('ehd,hdo->eho', k[src], rel_att)
        a = jnp.einsum('eho,eho->eh', kw, q[dst]) * rel_pri * inv_sqrt_d
        m = jnp.einsum('ehd,hdo->eho', v[src], rel_msg)
        amax = jax.ops.segment_max(a, dst, num_segments=N)
        ae = jnp.exp(a - amax[dst])
        asum = jax.ops.segment_sum(ae, dst, num_segments=N)
        attn = ae / asum[dst]
        h_agg = jax.ops.segment_sum(m * attn[..., None], dst, num_segments=N).reshape(N, H * Dh)
        h = typed_linear(h_agg, ntype, Wa)
        alpha = jax.nn.sigmoid(skip)[ntype][:, None]
        h = h * alpha + x * (1.0 - alpha)
        h = layer_norm(h, ln_g, ln_b)
        h = h + x
        gb = global_context @ film_w + film_b
        gamma, beta = (gb[:D], gb[D:])
        return gamma[None, :] * h + beta[None, :]

    def _L1_gnn_ref(x, src, dst):
        import jax, jax.numpy as jnp
        import numpy as np
        N = x.shape[0]
        loop = jnp.arange(N, dtype=src.dtype)
        s = jnp.concatenate([src, loop])
        d = jnp.concatenate([dst, loop])
        ones = jnp.ones(s.shape[0], dtype=x.dtype)
        in_deg = jax.ops.segment_sum(ones, d, num_segments=N)
        out_deg = jax.ops.segment_sum(ones, s, num_segments=N)
        norm_in = jnp.clip(in_deg, 1.0) ** (-0.5)
        norm_out = jnp.clip(out_deg, 1.0) ** (-0.5)
        xs = x * norm_in[:, None]
        h = jax.ops.segment_sum(xs[s], d, num_segments=N)
        return h * norm_out[:, None]

    def _L2_gnn_ref(x, edge_index, edge_attr, W_root, b_root, W_msg, W_src, W_dst, W_edge):
        import jax, jax.numpy as jnp
        import numpy as np
        N_NODES = 2500
        N_EDGES = 80000
        D = 128
        row, col = (edge_index[0], edge_index[1])
        n = x.shape[0]
        x_row = x[row]
        x_col = x[col]
        gates = jax.nn.sigmoid(x_row @ W_src + x_col @ W_dst + edge_attr @ W_edge)
        messages = x_row @ W_msg * gates
        out = jax.ops.segment_sum(messages, col, num_segments=n)
        normalizer = jax.ops.segment_sum(gates, col, num_segments=n)
        out = out / jnp.maximum(normalizer, 1e-06)
        out = out + (x @ W_root + b_root)
        out = out + x
        return out

    def _L3_gnn_ref(x, edge_index, W_l, b_l, W_r, gamma, beta):
        import jax, jax.numpy as jnp
        import numpy as np
        N = 12500
        E = 400000
        D_IN = 128
        D_OUT = 128
        EPS = 1e-05
        src = edge_index[0]
        dst = edge_index[1]
        n = x.shape[0]
        summed = jax.ops.segment_sum(x[src], dst, num_segments=n)
        deg = jax.ops.segment_sum(jnp.ones((src.shape[0],), x.dtype), dst, num_segments=n)
        mean_neigh = summed / jnp.maximum(deg, 1.0)[:, None]
        h = mean_neigh @ W_l + b_l + x @ W_r
        mu = jnp.mean(h, axis=-1, keepdims=True)
        var = jnp.mean(jnp.square(h - mu), axis=-1, keepdims=True)
        h = (h - mu) * jax.lax.rsqrt(var + EPS) * gamma + beta
        return jax.nn.gelu(h, approximate=False)
    edge_index = jnp.stack([src, dst])
    h = jnp.maximum(_layernorm(x, axis=-1), 0.0)
    x = x + _L0_gnn_ref(h, L0_gnn_global_context, L0_gnn_Wk, L0_gnn_Wq, L0_gnn_Wv, L0_gnn_rel_att, L0_gnn_rel_msg, L0_gnn_rel_pri, L0_gnn_Wa, L0_gnn_skip, L0_gnn_ln_g, L0_gnn_ln_b, L0_gnn_film_w, L0_gnn_film_b, node_type_3, src, dst)
    h = jnp.maximum(_layernorm(x, axis=-1), 0.0)
    x = x + _L1_gnn_ref(h, src, dst)
    h = jnp.maximum(_layernorm(x, axis=-1), 0.0)
    x = x + _L2_gnn_ref(h, edge_index, edge_attr_128, L2_gnn_W_root, L2_gnn_b_root, L2_gnn_W_msg, L2_gnn_W_src, L2_gnn_W_dst, L2_gnn_W_edge)
    h = jnp.maximum(_layernorm(x, axis=-1), 0.0)
    x = x + _L3_gnn_ref(h, edge_index, L3_gnn_W_l, L3_gnn_b_l, L3_gnn_W_r, L3_gnn_gamma, L3_gnn_beta)
    return x

_drawn_inputs = setup_inputs


def setup_inputs(seed=0):
    import zlib

    import numpy as np

    out = dict(_drawn_inputs(seed))
    spreads = {'L0_gnn_rel_pri': (1.0, 0.6),
     'L0_gnn_skip': (1.0, 0.6),
     'L0_gnn_ln_g': (1.0, 0.2),
     'L0_gnn_ln_b': (0.0, 0.1),
     'L0_gnn_film_b': (0.0, 0.1),
     'L3_gnn_gamma': (1.0, 0.2),
     'L3_gnn_beta': (0.0, 0.368)}
    factors = {'L0_gnn_Wk': 8.0,
     'L0_gnn_Wq': 8.0,
     'L0_gnn_rel_att': 8.0,
     'L2_gnn_W_src': 2.916,
     'L2_gnn_W_dst': 5.826}
    for name, (base, spread) in spreads.items():
        noise = np.random.default_rng([zlib.crc32(name.encode()), seed]).standard_normal(out[name].shape)
        drawn = base * np.exp(spread * noise) if base else spread * noise
        out[name] = jnp.asarray(drawn.astype(out[name].dtype))
    for name, factor in factors.items():
        out[name] = (out[name] * factor).astype(out[name].dtype)
    return out
```

```python
import numpy as np
import concourse.bass as bass
from concourse import mybir
from contextlib import ExitStack

F32 = mybir.dt.float32
BF16 = mybir.dt.bfloat16
I32 = mybir.dt.int32
ALU = mybir.AluOpType
ACT = mybir.ActivationFunctionType
AX = mybir.AxisListType

P = 128
D = 128
HEADS = 8
DH = D // HEADS
TYPES = 3
CTX = 64
EPS = 1e-5
ALIGN = 16
QUAD = 4
RING = 4
UNROLL = 8
GROUP = 16
NEG = -1e30
PAD_NODE = 1 << 20
EDGE_PARTS = 16


class Sizes:

    def __init__(self, nodes, edges):
        self.nodes, self.edges = nodes, edges
        self.blocks = -(-nodes // P)
        self.slots = self.blocks + 1
        self.slots += self.slots % 2
        most = (edges + self.blocks * (P - 1 + ALIGN - 1)) // P
        self.tiles = -(-most // P) * P
        self.edge_end = -(-edges // ALIGN) * ALIGN
        self.windows = self.edge_end // ALIGN + 1
        self.cols = self.tiles // P
        self.chunk = self.tiles // GROUP
        self.quads = self.tiles // QUAD
        self.groups = self.tiles // GROUP
        self.iters = self.quads // UNROLL
        self.span = self.chunk * P


def wait(eng, sem, value):
    if isinstance(value, int) and value <= 0:
        return
    eng.wait_ge(sem, value)


def build(nc, sz, a):
    NB, NS, T = sz.blocks, sz.slots, sz.tiles
    NQ = sz.quads
    ctx = ExitStack()
    with ctx:
        def sb(name, shape, dt=F32):
            return ctx.enter_context(nc.sbuf_tensor(name, shape, dt))

        def sem(name):
            return ctx.enter_context(nc.semaphore(name))

        def dram(name, shape, dt=F32):
            return nc.dram_tensor(name, shape, dt, kind="Internal").ap()

        tab2 = dram("tab2", (NS * P, 2 * D))
        tab1 = dram("tab1", (NS * P, D))
        mvd = dram("mvd", (NQ, P, QUAD * D))
        keyd = dram("keyd", (GROUP, sz.span))
        metad = dram("metad", (2, T), I32)

        X = sb("X", [P, NS, D])
        H = sb("H", [P, NS, D])
        QTR = sb("QTR", [P, max(NS * D, sz.span)])
        accw = NS * (D + HEADS + 1)
        ACCR = sb("ACCR", [P, max(NS * 2 * D, accw + sz.span + 2)])
        FLG = sb("FLG", [P, max(sz.span + 2, 2 * (2 * QUAD * 2 * D + T)) // 2 + 1])
        G = sb("G", [P, RING * QUAD * 2 * D])
        SCR = sb("SCR", [P, 3072])
        S = sb("S", [P, RING, QUAD, P])
        ST = sb("ST", [P, 2, QUAD, P])
        REL = sb("REL", [P, T])
        SRC = sb("SRC", [P, T], I32)
        ISLOT = sb("ISLOT", [P, RING, QUAD], I32)
        BROW = sb("BROW", [1, T], I32)
        W = sb("W", [P, TYPES * 3 * D])
        ROWS = sb("ROWS", [P, 5, D])
        ident = sb("ident", [P, P])
        identb = sb("identb", [P, P], BF16)
        iota = sb("iota", [P, P])
        MASK = sb("MASK", [P, NS, TYPES])
        ALPHA = sb("ALPHA", [P, NS])
        DEG = sb("DEG", [P, NS])
        OUTDEG = sb("OUTDEG", [P, NS])
        st1 = sb("st1", [P, NS])
        st2 = sb("st2", [P, NS])
        small = sb("small", [P, 16])

        QT = QTR[:, 0:NS * D].rearrange("p (b d) -> p b d", d=D)
        FMAX = QTR[:, 0:sz.span]
        acc0 = ACCR[:, 0:accw].rearrange("p (b d) -> p b d", d=D + HEADS + 1)
        acc1 = ACCR[:, 0:NS * D].rearrange("p (b d) -> p b d", d=D)
        acc2 = ACCR[:, 0:NS * 2 * D].rearrange("p (b d) -> p b d", d=2 * D)
        WIDE = acc1
        AT = ACCR[:, accw:accw + sz.span]
        KEY = ACCR[:, accw:accw + sz.span + 2]
        flags = FLG[:, :].bitcast(BF16)[:, 0:sz.span + 1]
        SROW = FLG[0:1, 2 * QUAD * 2 * D:2 * QUAD * 2 * D + T].bitcast(I32)
        RHS = FLG[:, 0:2 * QUAD * 2 * D].rearrange("p (r j d) -> p r j d", r=2, j=QUAD)
        G2 = G[:, :].rearrange("p (r j d) -> p r j d", r=RING, j=QUAD)
        G1 = G[:, 0:RING * QUAD * D].rearrange("p (r j d) -> p r j d", r=RING, j=QUAD)

        PSA = ctx.enter_context(nc.psum_tensor("PSA", [P, 2, QUAD, 2 * D], F32))
        PB = [ctx.enter_context(nc.psum_tensor(f"PB{i}", [P, 512], F32)) for i in range(4)]
        STP = [PB[r][:, 0:QUAD * P // 2].bitcast(BF16).rearrange("p (j e) -> p j e", j=QUAD) for r in range(2)]
        QD = [PB[2 + r][:, :].rearrange("p (j d) -> p j d", j=QUAD) for r in range(2)]

        dve_done = sem("dve_done")
        consts = sem("consts")

        def edge_sems(n):
            s = {"onehot_ready": sem(f"onehot_ready_{n}")}
            if n != "scores":
                s |= {k: sem(f"{k}_{n}") for k in ("agg_done", "rows_added")}
            if n != "messages":
                s |= {k: [sem(f"{k}{r}_{n}") for r in range(RING)] for k in ("idx_filled", "gathered")}
            return s

        block = ctx.enter_context(nc.Block())
        reg_note = "computed on the chip from the tile's position, always in range"

        def at(i, u, d):
            v = u + d
            i = i + v // UNROLL if v // UNROLL else i
            v %= UNROLL
            return i * UNROLL + v, v % RING, i * (UNROLL // RING) + v // RING, v

        def valid(q):
            return not isinstance(q, int) or 0 <= q < NQ

        def steps(eng, fn, trailing):
            for u in range(UNROLL):
                fn(0, u)
            if sz.iters > 2:
                with eng.Fori(1, sz.iters - 1) as i:
                    for u in range(UNROLL):
                        fn(i, u)
            for u in range(UNROLL):
                fn(sz.iters - 1, u)
            for u in range(trailing):
                fn(sz.iters, u)

        def pairs(eng, fn, trailing):
            n = NS // 2
            for r in range(2):
                fn(r, r)
            if n > 2:
                with eng.Fori(1, n - 1) as i:
                    for r in range(2):
                        fn(i * 2 + r, r)
            for r in range(2):
                fn(NS - 2 + r, r)
            for r in range(trailing):
                fn(NS + r, r)

        def group_of(i, u, d):
            v = u + d
            i = i + v // UNROLL if v // UNROLL else i
            return i * (UNROLL * QUAD // GROUP) + (v % UNROLL) // QUAD

        def CLINE(k):
            return SCR[0:1, k * P:(k + 1) * P]

        def has_block(b):
            return not isinstance(b, int) or 0 <= b < NS

        class Chain:

            def __init__(self, eng, s):
                self.eng, self.sem, self.n = eng, s, 0

            def __call__(self, ins):
                ins.then_inc(self.sem, 1)
                self.n += 1
                self.eng.wait_ge(self.sem, self.n)

        def bc(ap, shape, dim):
            return ap.unsqueeze(dim).to_broadcast(shape)


        c_ready = sem("consts_ready")
        dst_loaded = sem("dst_loaded")
        x_loaded = sem("x_loaded")
        w_loaded = sem("w_loaded")
        counted = sem("counted")
        totals = sem("totals")
        windows_known = sem("windows_known")
        windows_in = sem("windows_in")
        tiles_masked = sem("tiles_masked")
        tiles_turned = sem("tiles_turned")
        keys_stored = sem("keys_stored")
        keys_in = sem("keys_in")
        rows_in = sem("rows_in")
        w_combined = sem("w_combined")
        sig_in = sem("sig_in")
        sig_out = sem("sig_out")
        film_in = sem("film_in")
        centred = sem("centred")
        squared = sem("squared")
        root_in = sem("root_in")
        root_out = sem("root_out")
        carry_in = sem("carry_in")
        carry_row = sem("carry_row")
        carry_rows = sem("carry_rows")
        carry_col = sem("carry_col")
        exp_in = sem("exp_in")
        exp_out = sem("exp_out")
        w_free = sem("w_free")
        w_next = sem("w_next")
        hist_in = sem("hist_in")
        table_made = sem("table_made")
        table_out = sem("table_out")
        srow_in = sem("srow_in")
        gelu_in = sem("gelu_in")
        gelu_out = sem("gelu_out")
        x_final = sem("x_final")
        out_stored = sem("out_stored")

        NE = NB + 1
        NC = sz.cols
        WK = 3 * D

        DSTI = G[:, 0:T].bitcast(I32)
        DSTF = G[:, T:2 * T]
        SRCW = G[:, 2 * T:3 * T].bitcast(I32).rearrange("p (c e) -> p c e", c=NC)
        DSTW = G[:, 3 * T:4 * T].bitcast(I32).rearrange("p (c e) -> p c e", c=NC)
        SRCF = SCR[:, 0:T].rearrange("p (c e) -> p c e", c=NC)
        RELF = SCR[:, T:2 * T].rearrange("p (c e) -> p c e", c=NC)
        JUNK = SCR[:, 2 * T:3 * T]
        VAL = JUNK.rearrange("p (c e) -> p c e", c=NC)
        DKF = DSTF.rearrange("p (c e) -> p c e", c=NC)
        KEYW = G[:, 0:T].rearrange("p (c e) -> p c e", c=NC)
        q0 = [0]

        def cut(n, dt=F32):
            v = QTR[:, q0[0]:q0[0] + n]
            q0[0] += n
            return v if dt == F32 else v.bitcast(dt)

        thr, cnt, bf, b16f, tiles_f, zer, cum, rel0, delta = (cut(NE) for _ in range(9))
        bi = cut(NE, I32)
        ti32 = cut(NE, I32)
        ones = cut(P)
        pI, p15, p4 = (cut(1, I32) for _ in range(3))
        p15f, p4f, tp = (cut(1) for _ in range(3))
        cI = cut(NC, I32)
        cF, tpos, bt, st, off = (cut(NC) for _ in range(5))
        bI, sI, wI = (cut(NC, I32) for _ in range(3))
        M = cut(NC * NE).rearrange("p (c b) -> p c b", c=NC)
        MD = cut(NC * NE).rearrange("p (c b) -> p c b", c=NC)
        thrI = cut(NE, I32)
        iotaI = cut(P, I32)
        NTI = cut(NS, I32)
        SKIP = cut(4)
        SIG = cut(4)
        PRI8 = cut(HEADS)
        SF = S[:, :, :, :].rearrange("p r j e -> p (r j e)")
        WKT = SF[:, 0:384].rearrange("p (t d) -> p t d", t=3)
        WVT = SF[:, 384:768].rearrange("p (t d) -> p t d", t=3)
        ATTB, MSGB = SF[:, 768:896], SF[:, 896:1024]
        FILMW = SF[0:CTX, 1024:1280]
        CTXB = SF[0:CTX, 1280:1408]
        CTXC = SF[0:CTX, 1408:1409]
        W3 = W[:, :].rearrange("p (t c) -> p t c", t=TYPES)
        WA = W[:, 0:TYPES * D].rearrange("p (t c) -> p t c", t=TYPES)
        PRI = ROWS[:, 0, :]

        MB = G[:, 0:2 * WK].rearrange("p (r t d) -> p r t d", r=2, t=3)
        HT = G[:, 2 * WK:4 * WK].rearrange("p (r t d) -> p r t d", r=2, t=3)
        STG = G[:, 4 * WK:4 * WK + 4 * D].rearrange("p (r d) -> p r d", r=2)

        def proj_sems(n):
            s = {k: sem(f"{k}_{n}") for k in ("placed", "turned", "copied", "multiplied", "evacuated", "inputs")}
            if n in ("typed_qkv", "gate_nodes"):
                s["stored"] = [sem(f"stored{r}_{n}") for r in range(2)]
            return s

        proj = [proj_sems(n) for n in ("typed_qkv", "typed_out", "gate_nodes", "sage")]
        proj_w = [
            (3, lambda t: W3[:, t, :], WK),
            (3, lambda t: WA[:, t, :], D),
            (1, lambda t: W[:, 0:4 * D], 4 * D),
            (2, lambda t: W[:, t * D:(t + 1) * D], D),
        ]

        def pe_proj(pe, n):
            s, (ni, w, cols) = proj[n], proj_w[n]
            pe.wait_ge(s["inputs"], 1)

            def step(b, r):
                if has_block(b):
                    pe.wait_ge(s["placed"], b + 1)
                    wait(pe, s["copied"], b - 1)
                    for t in range(ni):
                        last = nc.tensor.transpose(PB[r][:, t * P:(t + 1) * P], MB[:, r, t, :], ident[:, :])
                    last.then_inc(s["turned"], 1)
                m = b - 1
                if has_block(m):
                    pe.wait_ge(s["copied"], m + 1)
                    wait(pe, s["evacuated"], m - 1)
                    for t in range(ni):
                        last = nc.tensor.matmul(PB[2 + (1 - r)][:, 0:cols], HT[:, 1 - r, t, :], w(t),
                                                start=t == 0, stop=t == ni - 1)
                    last.then_inc(s["multiplied"], 1)
            pairs(pe, step, 1)

        def act_proj(act, n):
            s, (ni, w, cols) = proj[n], proj_w[n]

            def step(b, r):
                act.wait_ge(s["turned"], b + 1)
                wait(act, s["multiplied"], b - 1)
                nc.scalar.copy(HT[:, r, 0:ni, :].rearrange("p t d -> p (t d)"),
                               PB[r][:, 0:ni * P]).then_inc(s["copied"], 1)
            pairs(act, step, 0)

        def dve_proj(dve, n):
            s = proj[n]
            dve.sem_inc(s["inputs"], 1)

            def copy(dst, src):
                return nc.vector.tensor_scalar(dst, src, 1.0, None, ALU.mult)

            def step(b, r):
                if has_block(b):
                    wait(dve, s["turned"], b - 1)
                if n == 3 and has_block(b):
                    copy(MB[:, r, 0:1, :], QT[:, bass.ds(b, 1), :])
                if n in (2, 3) and has_block(b):
                    copy(MB[:, r, n - 2:n - 1, :], H[:, bass.ds(b, 1), :]).then_inc(s["placed"], 1)
                if n in (0, 1) and has_block(b):
                    src = H if n == 0 else QT
                    nc.vector.tensor_tensor(
                        MB[:, r, :, :], src[:, bass.ds(b, 1), :].to_broadcast([P, 3, D]),
                        MASK[:, bass.ds(b, 1), :].rearrange("p o t -> p (o t)").unsqueeze(2).to_broadcast([P, 3, D]),
                        ALU.mult).then_inc(s["placed"], 1)
                m, rm = b - 1, 1 - r
                if has_block(m):
                    dve.wait_ge(s["multiplied"], m + 1)
                    ps = PB[2 + rm]
                    row = lambda tab: tab[:, bass.ds(m, 1), :].rearrange("p o d -> p (o d)")
                    if n in (1, 3):
                        copy(row(QT), ps[:, 0:D]).then_inc(s["evacuated"], 1)
                        return
                    if n == 0:
                        nc.vector.tensor_tensor(row(QT), ps[:, 2 * D:3 * D], PRI, ALU.mult)
                    else:
                        copy(row(QT), ps[:, 2 * D:3 * D])
                        nc.vector.tensor_tensor(row(H), row(H), ps[:, 3 * D:4 * D], ALU.add)
                    half = m // 2 if isinstance(m, int) else None
                    if isinstance(m, int):
                        wait(dve, s["stored"][rm], half * 16)
                    else:
                        dve.wait_ge(s["stored"][rm], (m - rm) * 8)
                    copy(STG[:, rm, :], ps[:, 0:2 * D]).then_inc(s["evacuated"], 1)
            pairs(dve, step, 1)
            dve.wait_ge(s["evacuated"], NS)

        def sp_proj(sp, n):
            s = proj[n]

            def step(b, r):
                sp.wait_ge(s["evacuated"], b + 1)
                sp.dma_start(tab2[bass.ds(b * P, P), :], STG[:, r, :]).then_inc(s["stored"][r], 16)
            pairs(sp, step, 0)

        names = ("scores", "messages", "degree", "gated", "mean")
        ps = [edge_sems(n) for n in names]
        scored = {k: sem(k + "_scores") for k in ("st_turned", "st_copied", "q_spread", "multiplied", "reduced", "grp_turned", "grp_copied")}
        mv_stored = [sem(f"mv_stored{r}") for r in range(RING)]
        mv_loaded = [sem(f"mv_loaded{r}") for r in range(RING)]
        weighted = {k: sem(k + "_messages") for k in ("ones_set", "grp_staged", "grp_turned", "grp_copied", "prob_put", "weighted", "hist_ready")}
        gated = {k: sem(k + "_gated") for k in ("st_turned", "st_copied", "pre_done", "summed", "gate_done", "multiplied")}
        ea_loaded = [sem(f"ea_loaded{r}") for r in range(RING)]
        may_gather = sem("may_gather")
        rows_read = {0: scored["multiplied"], 2: ps[2]["agg_done"], 3: gated["multiplied"], 4: ps[4]["agg_done"]}

        PROD = SCR[:, 0:1024].rearrange("p (r j d) -> p r j d", r=2, j=QUAD)
        ABUF = SCR[:, 1024:1280].rearrange("p (r c) -> p r c", r=2)
        WMW = D + HEADS + 1
        WM = SCR[:, 0:2 * QUAD * WMW].rearrange("p (r j d) -> p r j d", r=2, j=QUAD)
        AE = SCR[:, 1096:1352].rearrange("p (r c) -> p r c", r=2)
        LOH = SCR[:, 1352:2376].bitcast(BF16).rearrange("p (r j c) -> p r j c", r=RING, j=QUAD)
        HIH = SCR[:, 2376:2376 + RING * QUAD * NS // 2].bitcast(BF16).rearrange("p (r j c) -> p r j c", r=RING, j=QUAD)
        LO = FLG[:, 0:T // 2].bitcast(BF16)
        HI = FLG[:, T // 2:T].bitcast(BF16)
        SRCPM = FLG[:, T:2 * T].bitcast(I32)
        SRCTMP = FLG[:, 2 * T:3 * T].bitcast(I32)
        PRE = SCR[:, 0:1024].rearrange("p (r j d) -> p r j d", r=2, j=QUAD)
        EA = SCR[:, 1024:3072].rearrange("p (r j e) -> p r j e", r=RING, j=QUAD)
        ATS = SCR[:, 2776:3032].rearrange("p (r e) -> p r e", r=2)
        ATP = PSA[:, 0, 0, 0:P]
        AEP = [PB[r][:, 0:P] for r in range(2)]
        HISTP = PB[2][:, 0:NS]

        def block_of(eng, q, j):
            return nc.values_load(BROW[0:1, bass.ds(q * QUAD + j, 1)], engines=[eng.engine], min_val=0,
                                  max_val=NB, skip_runtime_bounds_check_because=reg_note)

        def pool_gathers(pool, n, rows, table):
            s = ps[n]

            def step(i, u):
                q, slot, turn, _ = at(i, u, 0)
                pool.wait_ge(s["idx_filled"][slot], (turn + 1) * 16)
                wait(pool, rows_read[n], q - RING + 1)
                if n == 0:
                    wait(pool, mv_stored[slot], turn * 16)
                pool.sem_inc(may_gather, 1)
                for j in range(QUAD):
                    nc.gpsimd.indirect_dma_start(
                        out=rows[:, slot, j, :], out_offset=None, in_=table,
                        in_offset=bass.IndirectOffsetOnAxis(ap=ISLOT[:, slot, j:j + 1], axis=0),
                    ).then_inc(s["gathered"][slot], 16)
            steps(pool, step, 0)

        @block.gpsimd
        def _(pool):
            nc.gpsimd.memset(ident[:, :], 0.0).then_inc(consts, 1)
            pool.wait_ge(consts, 1)
            nc.gpsimd.affine_select(out=ident[:, :], in_=ident[:, :], compare_op=ALU.not_equal, fill=1.0,
                                    base=0, pattern=[[-1, P]], channel_multiplier=1)
            nc.gpsimd.iota(iotaI, pattern=[[1, P]], base=0, channel_multiplier=0)
            nc.gpsimd.iota(thrI, pattern=[[P, NE]], base=0, channel_multiplier=0)
            nc.gpsimd.iota(pI, pattern=[[0, 1]], base=0, channel_multiplier=1)
            nc.gpsimd.iota(cI, pattern=[[8, NC]], base=0, channel_multiplier=0).then_inc(c_ready, 1)
            pool.wait_ge(windows_known, 1)
            pool.sem_inc(may_gather, 1)
            for c in range(NC):
                for src, dst in ((a["src_win"], SRCW), (a["dst_win"], DSTW)):
                    nc.gpsimd.indirect_dma_start(
                        out=dst[:, c, :], out_offset=None, in_=src,
                        in_offset=bass.IndirectOffsetOnAxis(ap=wI[:, c:c + 1], axis=0)).then_inc(windows_in, 16)
            for r in range(2):
                pool.wait_ge(proj[0]["stored"][r], 16 * NS // 2)
            pool_gathers(pool, 0, G2, tab2)

            def step(i, u):
                q, slot, turn, v = at(i, u, 0)
                w = v % 2
                pool.wait_ge(mv_loaded[slot], (turn + 1) * 16)
                pool.wait_ge(weighted["prob_put"], q + 1)
                wait(pool, ps[1]["agg_done"], q - 1)
                grp = (v // 4) % 2
                probs = AE[:, grp, (v % 4) * 32:(v % 4) * 32 + 32]
                nc.gpsimd.tensor_tensor(
                    WM[:, w, :, 0:D].rearrange("p j (h d) -> p j h d", h=HEADS),
                    G1[:, slot, :, :].rearrange("p j (h d) -> p j h d", h=HEADS),
                    probs.rearrange("p (j h) -> p j h", j=QUAD).unsqueeze(3).to_broadcast([P, QUAD, HEADS, DH]),
                    ALU.mult).then_inc(weighted["weighted"], 1)
            steps(pool, step, 0)

            pool.wait_ge(table_out, 16)
            pool_gathers(pool, 2, G1, tab1)
            for r in range(2):
                pool.wait_ge(proj[2]["stored"][r], 16 * NS // 2)
            pool_gathers(pool, 3, G2, tab2)
            pool.wait_ge(table_out, 32)
            pool_gathers(pool, 4, G1, tab1)

        def sp_edges(sp, n):
            s = ps[n]

            def step(i, u):
                q, slot, turn, _ = at(i, u, 0)
                if n != 1:
                    wait(sp, s["gathered"][slot], turn * 64 if not isinstance(turn, int) else turn * 64)
                if n == 0 and valid(q - RING) and not (isinstance(q, int) and q < RING):
                    sp.dma_start(mvd[bass.ds(q - RING, 1), :, :].rearrange("o p (j d) -> (o p) j d", j=QUAD),
                                 G2[:, slot, :, D:2 * D]).then_inc(mv_stored[slot], 16)
                if not valid(q):
                    return
                if n == 1:
                    wait(sp, weighted["weighted"], q - RING + 1)
                    sp.dma_start(G1[:, slot, :, :].rearrange("p j d -> p (j d)"),
                                 mvd[bass.ds(q, 1), :, :].rearrange("o p f -> (o p) f")).then_inc(mv_loaded[slot], 16)
                    return
                sp.dma_start(ISLOT[:, slot, :], SRC[:, bass.ds(q * QUAD, QUAD)]).then_inc(s["idx_filled"][slot], 16)
                if n == 3:
                    wait(sp, gated["pre_done"], q - RING + 1)
                    for j in range(QUAD):
                        first = nc.values_load(SROW[0:1, bass.ds(q * QUAD + j, 1)], engines=[sp.engine], min_val=0,
                                               max_val=sz.edge_end, skip_runtime_bounds_check_because=reg_note)
                        sp.dma_start(EA[:, slot, j, :], a["ea_t"][:, bass.ds(first, P)]).then_inc(ea_loaded[slot], 16)
            steps(sp, step, RING if n == 0 else 0)
            if n == 0:
                for r in range(RING):
                    sp.wait_ge(mv_stored[r], 16 * NQ // RING)

        def row_bc(v, n):
            return v.rearrange("(o n) -> o n", o=1).to_broadcast([P, n])

        @block.sync
        def _(sp):
            sp.dma_start(DSTI, a["dst_pm"]).then_inc(dst_loaded, 16)
            sp.dma_start(X[:, :, :], a["x"].rearrange("(b p) d -> p b d", p=P)).then_inc(x_loaded, 16)
            loads = [
                (WKT, a["wk_t"].rearrange("t m i -> m t i")), (WVT, a["wv_t"].rearrange("t m i -> m t i")),
                (W3[:, :, 2 * D:3 * D], a["wq"].rearrange("t i o -> i t o")),
                (ATTB, a["att"]), (MSGB, a["msg"]), (FILMW, a["film_w"]),
                (CTXC, a["ctx"].rearrange("(c o) -> c o", o=1)), (NTI, a["ntype"]),
                (SKIP[:, 0:3], row_bc(a["skip"], 3)), (PRI8, row_bc(a["pri"], HEADS)),
                (ROWS[:, 1, :], row_bc(a["ln_g"], D)), (ROWS[:, 2, :], row_bc(a["ln_b"], D)),
                (ROWS[:, 3:5, :].rearrange("p a d -> p (a d)"), row_bc(a["film_b"], 2 * D)),
            ]
            with nc.allow_non_contiguous_dma(reason="columns of a few words"):
                for dst, src in loads:
                    sp.dma_start(dst, src).then_inc(w_loaded, 16)
                sp.wait_ge(tiles_masked, 1)
                sp.dma_start(keyd.rearrange("t (s e) -> (t s) e", e=P).rearrange("(c p) e -> p c e", p=P), KEYW).then_inc(keys_stored, 16)
                sp.dma_start(metad[0, :].rearrange("(c p) -> p c", p=P), bI).then_inc(keys_stored, 16)
                sp.dma_start(metad[1, :].rearrange("(c p) -> p c", p=P), sI).then_inc(keys_stored, 16)
                sp.wait_ge(keys_stored, 48)
                sp.dma_start(BROW[:, :], metad[0:1, :]).then_inc(rows_in, 16)
                keyk = keyd.rearrange("t (s e) -> (t s) e", e=P).rearrange("(g t) e -> t g e", t=GROUP)
                for h in range(HEADS):
                    sp.dma_start(KEY[h:P:HEADS, 1:1 + sz.span].rearrange("t (g e) -> t g e", e=P), keyk).then_inc(keys_in, 16)
                    sp.dma_start(KEY[HEADS + h:P:HEADS, 0:1], keyk[0:GROUP - 1, sz.chunk - 1, P - 1:P]).then_inc(keys_in, 16)
                    sp.dma_start(KEY[h:P - HEADS:HEADS, sz.span + 1:sz.span + 2], keyk[1:GROUP, 0, 0:1]).then_inc(keys_in, 16)
            sp_proj(sp, 0)
            sp_edges(sp, 0)
            sp.wait_ge(w_free, 1)
            sp.dma_start(WA, a["wa"].rearrange("t i o -> i t o")).then_inc(w_next, 16)
            sp.wait_ge(exp_in, 1)
            sp.dma_start(SRCPM, a["src_pm"]).then_inc(hist_in, 16)
            sp_edges(sp, 1)
            sp.wait_ge(table_made, 1)
            sp.dma_start(tab1.rearrange("(b p) d -> p b d", p=P), H[:, :, :]).then_inc(table_out, 16)
            sp.dma_start(ROWS[:, 0, :], row_bc(a["b_root"], D)).then_inc(w_next, 16)
            for k, name in enumerate(("w_src", "w_msg", "w_dst", "w_root", "w_edge")):
                sp.dma_start(W[:, k * D:(k + 1) * D], a[name]).then_inc(w_next, 16)
            sp.dma_start(SROW, metad[1:2, :]).then_inc(srow_in, 16)
            sp_edges(sp, 2)
            sp.wait_ge(srow_in, 16)
            sp_proj(sp, 2)
            sp_edges(sp, 3)
            sp.wait_ge(table_made, 2)
            sp.dma_start(tab1.rearrange("(b p) d -> p b d", p=P), H[:, :, :]).then_inc(table_out, 16)
            for k, name in enumerate(("w_l", "w_r")):
                sp.dma_start(W[:, k * D:(k + 1) * D], a[name]).then_inc(w_next, 16)
            for k, name in enumerate(("b_l", "gamma", "beta")):
                sp.dma_start(ROWS[:, k, :], row_bc(a[name], D)).then_inc(w_next, 16)
            sp_edges(sp, 4)
            sp.wait_ge(x_final, 1)
            whole = sz.nodes // P
            left = sz.nodes - whole * P
            sp.dma_start(a["out"][0:whole * P, :].rearrange("(b p) d -> p b d", p=P), X[:, 0:whole, :]).then_inc(out_stored, 16)
            if left:
                sp.dma_start(a["out"][whole * P:sz.nodes, :], X[0:left, whole, :]).then_inc(out_stored, 16)
            sp.wait_ge(out_stored, 32 if left else 16)

        def bf_view(slot, j):
            return S[:, slot, j, :].bitcast(BF16)[:, 1::2]

        def pe_turn_onehot(pe, s, onehot, q, slot, par):
            pe.wait_ge(onehot, q + 1)
            wait(pe, s["st_copied"], q - 1)
            for j in range(QUAD):
                last = nc.tensor.transpose(STP[par][:, j, :], bf_view(slot, j), identb[:, :])
            last.then_inc(s["st_turned"], 1)

        def pe_agg(pe, n, q, slot, par, rhs, width):
            s = ps[n]
            pe.wait_ge(s["onehot_ready"], q + 1)
            wait(pe, s["rows_added"], (q - 1) * QUAD)
            for j in range(QUAD):
                last = nc.tensor.matmul(PSA[:, par, j, 0:width], S[:, slot, j, :], rhs(j), start=True, stop=True)
            last.then_inc(s["agg_done"], 1)

        def pe_plain(pe, n):
            s = ps[n]

            def step(i, u):
                q, slot, turn, v = at(i, u, 0)
                pe.wait_ge(s["gathered"][slot], (turn + 1) * 64)
                pe_agg(pe, n, q, slot, v % 2, lambda j: G1[:, slot, j, :], D)
            steps(pe, step, 0)

        @block.tensor
        def _(pe):
            pe.wait_ge(counted, NE + 1)
            nc.tensor.matmul(PB[0][:, 0:NE], ones, cnt, start=True, stop=True).then_inc(totals, 1)
            pe.wait_ge(w_loaded, 16 * 13)
            for t in range(TYPES):
                nc.tensor.matmul(PB[1][:, t * D:(t + 1) * D], WKT[:, t, :], ATTB, start=True, stop=True)
                nc.tensor.matmul(PB[2][:, t * D:(t + 1) * D], WVT[:, t, :], MSGB, start=True, stop=True)
            pe.wait_ge(film_in, 1)
            nc.tensor.matmul(PB[3][:, 0:2 * D], CTXB, FILMW, start=True, stop=True).then_inc(w_combined, 1)
            pe.wait_ge(tiles_masked, 1)
            for c in range(NC):
                for k, f in enumerate((RELF, SRCF)):
                    last = nc.tensor.transpose(PB[2 * k + c // 4][:, (c % 4) * P:(c % 4 + 1) * P], f[:, c, :], ident[:, :])
            last.then_inc(tiles_turned, 1)
            pe_proj(pe, 0)

            pe.wait_ge(rows_in, 16)
            s = scored

            def step(i, u):
                q, slot, turn, v = at(i, u, 0)
                if valid(q):
                    pe_turn_onehot(pe, s, ps[0]["onehot_ready"], q, slot, v % 2)
                q, slot, turn, v = at(i, u, -1)
                if valid(q):
                    pe.wait_ge(s["st_copied"], q + 1)
                    wait(pe, s["multiplied"], q - 1)
                    for j in range(QUAD):
                        b = block_of(pe, q, j)
                        last = nc.tensor.matmul(QD[v % 2][:, j, :], ST[:, v % 2, j, :],
                                                QT[:, bass.ds(b, 1), :].rearrange("p o d -> p (o d)"), start=True, stop=True)
                    last.then_inc(s["q_spread"], 1)
                q, slot, turn, v = at(i, u, -3)
                if valid(q) and v % 4 == 3:
                    pe.wait_ge(s["reduced"], q + 1)
                    g = group_of(i, u, -3)
                    wait(pe, s["grp_copied"], g)
                    nc.tensor.transpose(ATP, ABUF[:, (v // 4) % 2, :], ident[:, :]).then_inc(s["grp_turned"], 1)
            steps(pe, step, 3)

            for k in range(2):
                pe.wait_ge(carry_in, k + 1)
                nc.tensor.matmul(PB[0][0:1, 0:P], small[:, 0:1], ident[:, :], start=True, stop=True)
                nc.tensor.matmul(PB[0][0:1, P:2 * P], small[:, 1:2], ident[:, :], start=True, stop=True).then_inc(carry_rows, 1)
                pe.wait_ge(carry_row, k + 1)
                nc.tensor.matmul(PB[1][:, 0:1], CLINE(3), small[0:1, 3:4], start=True, stop=True).then_inc(carry_col, 1)

            pe.wait_ge(exp_out, 1)
            w = weighted

            def step(i, u):
                q, slot, turn, v = at(i, u, 0)
                if valid(q) and v % 4 == 0:
                    g = group_of(i, u, 0)
                    pe.wait_ge(w["grp_staged"], g + 1)
                    wait(pe, w["prob_put"], (g - 1) * (GROUP // QUAD))
                    nc.tensor.transpose(AEP[(v // 4) % 2], ATS[:, (v // 4) % 2, :], ident[:, :]).then_inc(w["grp_turned"], 1)
                q, slot, turn, v = at(i, u, -2)
                if valid(q):
                    pe.wait_ge(w["hist_ready"], q + 1)
                    for j in range(QUAD):
                        first = isinstance(q, int) and q == 0 and j == 0
                        final = isinstance(q, int) and q == NQ - 1 and j == QUAD - 1
                        nc.tensor.matmul(HISTP, LOH[:, slot, j, :], HIH[:, slot, j, :], start=first, stop=final,
                                         skip_group_check=True)
                    pe.wait_ge(w["weighted"], q + 1)
                    pe_agg(pe, 1, q, slot, v % 2, lambda j: WM[:, v % 2, j, :], WMW)
            steps(pe, step, 2)
            pe_proj(pe, 1)
            pe_plain(pe, 2)
            pe_proj(pe, 2)

            s = gated

            def step(i, u):
                q, slot, turn, v = at(i, u, 0)
                if valid(q):
                    pe_turn_onehot(pe, s, ps[3]["onehot_ready"], q, slot, v % 2)
                q, slot, turn, v = at(i, u, -1)
                if valid(q):
                    pe.wait_ge(s["st_copied"], q + 1)
                    pe.wait_ge(ea_loaded[slot], (turn + 1) * 64)
                    wait(pe, s["summed"], q - 1)
                    for j in range(QUAD):
                        b = block_of(pe, q, j)
                        nc.tensor.matmul(QD[v % 2][:, j, :], EA[:, slot, j, :], W[:, 4 * D:5 * D], start=True, stop=False)
                        last = nc.tensor.matmul(QD[v % 2][:, j, :], ST[:, v % 2, j, :],
                                                QT[:, bass.ds(b, 1), :].rearrange("p o d -> p (o d)"), start=False, stop=True)
                    last.then_inc(s["pre_done"], 1)
                q, slot, turn, v = at(i, u, -3)
                if valid(q):
                    pe.wait_ge(s["multiplied"], q + 1)
                    pe_agg(pe, 3, q, slot, v % 2, lambda j: RHS[:, v % 2, j, :], 2 * D)
            steps(pe, step, 3)
            pe_plain(pe, 4)
            pe_proj(pe, 3)

        def act_copy_onehot(act, s, q, par, used):
            act.wait_ge(s["st_turned"], q + 1)
            wait(act, used, q - 1)
            nc.scalar.copy(ST[:, par, :, :], STP[par]).then_inc(s["st_copied"], 1)

        @block.scalar
        def _(act):
            turn_no = [0]

            roots = [0]

            def root(t):
                roots[0] += 1
                act.wait_ge(root_in, roots[0])
                nc.scalar.activation(t[:, :], t[:, :], ACT.Sqrt).then_inc(root_out, 1)

            def square():
                turn_no[0] += 1
                act.wait_ge(centred, turn_no[0])
                src = QT if turn_no[0] in (2, 6) else H
                nc.scalar.activation(WIDE, src[:, :, :], ACT.Square).then_inc(squared, 1)
                root(st2)

            act.wait_ge(sig_in, 1)
            nc.scalar.activation(SIG[:, 0:3], SKIP[:, 0:3], ACT.Sigmoid).then_inc(sig_out, 1)
            square()
            act_proj(act, 0)
            s = scored

            def step(i, u):
                q, slot, turn, v = at(i, u, 0)
                if valid(q):
                    act_copy_onehot(act, s, q, v % 2, s["q_spread"])
                q, slot, turn, v = at(i, u, -3)
                if valid(q) and v % 4 == 3:
                    g = group_of(i, u, -3)
                    act.wait_ge(s["grp_turned"], g + 1)
                    nc.scalar.copy(AT[:, bass.ds(g * P, P)], ATP).then_inc(s["grp_copied"], 1)
            steps(act, step, 3)
            act.wait_ge(exp_in, 1)
            nc.scalar.activation(AT, FMAX, ACT.Exp).then_inc(exp_out, 1)
            w = weighted
            act.wait_ge(exp_out, 1)
            act.wait_ge(w["ones_set"], 1)

            def step(i, u):
                q, slot, turn, v = at(i, u, 0)
                grp = (v // 4) % 2
                if v % 4 == 0:
                    g = group_of(i, u, 0)
                    wait(act, w["grp_turned"], g - 1)
                    nc.scalar.copy(ATS[:, grp, :], AT[:, bass.ds(g * P, P)]).then_inc(w["grp_staged"], 1)
                    act.wait_ge(w["grp_turned"], g + 1)
                    wait(act, w["weighted"], q - QUAD)
                    nc.scalar.copy(AE[:, grp, :], AEP[grp]).then_inc(w["grp_copied"], 1)
                wait(act, ps[1]["agg_done"], q - 1)
                nc.scalar.copy(WM[:, v % 2, :, D:D + HEADS],
                               AEP[grp][:, (v % 4) * 32:(v % 4) * 32 + 32].rearrange("p (j h) -> p j h", j=QUAD)
                               ).then_inc(w["prob_put"], 1)
            steps(act, step, 0)
            act_proj(act, 1)
            square()
            square()
            root(st1)
            root(OUTDEG)
            square()
            act_proj(act, 2)
            s = gated

            def step(i, u):
                q, slot, turn, v = at(i, u, 0)
                if valid(q):
                    act_copy_onehot(act, s, q, v % 2, s["pre_done"])
                q, slot, turn, v = at(i, u, -2)
                if valid(q):
                    act.wait_ge(s["summed"], q + 1)
                    wait(act, ps[3]["agg_done"], q - 1)
                    nc.scalar.activation(RHS[:, v % 2, :, D:2 * D], PRE[:, v % 2, :, :], ACT.Sigmoid).then_inc(s["gate_done"], 1)
            steps(act, step, 2)
            square()
            act_proj(act, 3)
            square()
            act.wait_ge(gelu_in, 1)
            nc.scalar.activation(QT, QT, ACT.Gelu).then_inc(gelu_out, 1)

        def plain(dve, n, onehot, add_rows):
            def step(i, u):
                q, slot, turn, v = at(i, u, 0)
                if valid(q):
                    onehot(n, q, slot)
                q, slot, turn, v = at(i, u, -2)
                if valid(q):
                    add_rows(n, acc1, D, q, v % 2)
            steps(dve, step, 2)
            dve.wait_ge(ps[n]["rows_added"], T)

        @block.vector
        def _(dve):
            c = Chain(dve, dve_done)
            v_ = nc.vector

            def onehot(n, q, slot):
                wait(dve, scored["st_turned"] if n == 0 else ps[n]["agg_done"], q - RING + 1)
                return v_.tensor_tensor(S[:, slot, :, :], bc(iota[:, :], [P, QUAD, P], 1),
                                        REL[:, bass.ds(q * QUAD, QUAD)].unsqueeze(2).to_broadcast([P, QUAD, P]),
                                        ALU.is_equal).then_inc(ps[n]["onehot_ready"], 1)

            def add_rows(n, acc, width, q, par):
                s = ps[n]
                dve.wait_ge(s["agg_done"], q + 1)
                for j in range(QUAD):
                    b = block_of(dve, q, j)
                    rows = acc[:, bass.ds(b, 1), :].rearrange("p o d -> p (o d)")
                    wait(dve, s["rows_added"], q * QUAD + j)
                    v_.tensor_tensor(rows, rows, PSA[:, par, j, 0:width], ALU.add).then_inc(s["rows_added"], 1)

            def layer_norm(src, dst):
                c(v_.tensor_reduce(st1[:, :], src[:, :, :], AX.X, ALU.add))
                c(v_.tensor_scalar(st1[:, :], st1[:, :], -1.0 / D, None, ALU.mult))
                c(v_.tensor_tensor(dst[:, :, :], src[:, :, :], st1[:, :].unsqueeze(2).to_broadcast([P, NS, D]), ALU.add))
                dve.sem_inc(centred, 1)
                norms[0] += 1
                dve.wait_ge(squared, norms[0])
                c(v_.tensor_reduce(st2[:, :], WIDE, AX.X, ALU.add))
                c(v_.tensor_scalar(st2[:, :], st2[:, :], 1.0 / D, EPS, ALU.mult, ALU.add))
                root(st2)

            norms, roots = [0], [0]
            node = [P, NS, D]

            def root(t):
                dve.sem_inc(root_in, 1)
                roots[0] += 1
                dve.wait_ge(root_out, roots[0])
                c(v_.reciprocal(t[:, :], t[:, :]))

            def relu_scaled(dst):
                c(v_.scalar_tensor_tensor(dst[:, :, :], dst[:, :, :], 0.0, st2[:, :].unsqueeze(2).to_broadcast(node),
                                          ALU.max, ALU.mult))

            def over(ap):
                return ap.unsqueeze(2).to_broadcast(node)

            def vec(k):
                return bc(ROWS[:, k, :], node, 1)

            dve.wait_ge(c_ready, 1)
            c(v_.tensor_copy(iota[:, :], iotaI))
            c(v_.tensor_copy(thr, thrI))
            c(v_.tensor_copy(identb[:, :], ident[:, :]))
            c(v_.memset(ones, 1.0))
            c(v_.memset(zer, 0.0))
            c(v_.memset(small[:, :], 1.0))
            c(v_.memset(cnt, 0.0))
            c(v_.memset(cum, 0.0))
            dve.wait_ge(dst_loaded, 16)
            v_.tensor_copy(DSTF, DSTI).then_inc(counted, 1)
            with dve.Fori(0, NE) as b:
                dve.wait_ge(counted, b + 1)
                v_.tensor_scalar(JUNK, DSTF, thr[:, bass.ds(b, 1)], 0.0, ALU.is_lt, ALU.add,
                                 accum_out=cnt[:, bass.ds(b, 1)]).then_inc(counted, 1)
            dve.wait_ge(totals, 1)
            c(v_.tensor_copy(bf, PB[0][:, 0:NE]))
            c(v_.tensor_copy(bi, bf))
            c(v_.tensor_scalar(bi, bi, 4, 4, ALU.logical_shift_right, ALU.logical_shift_left))
            c(v_.tensor_copy(b16f, bi))
            c(v_.tensor_tensor(tiles_f[:, 0:NB], bf[:, 1:NE], b16f[:, 0:NB], ALU.subtract))
            c(v_.tensor_scalar(tiles_f[:, 0:NB], tiles_f[:, 0:NB], float(P - 1), None, ALU.add))
            c(v_.tensor_copy(ti32[:, 0:NB], tiles_f[:, 0:NB]))
            c(v_.tensor_scalar(ti32[:, 0:NB], ti32[:, 0:NB], 7, None, ALU.logical_shift_right))
            c(v_.tensor_copy(tiles_f[:, 0:NB], ti32[:, 0:NB]))
            c(v_.tensor_tensor_scan(cum[:, 1:NE], tiles_f[:, 0:NB], zer[:, 0:NB], 0.0, ALU.add, ALU.add))
            c(v_.scalar_tensor_tensor(rel0, cum, -float(P), b16f, ALU.mult, ALU.add))
            c(v_.tensor_copy(delta[:, 0:1], rel0[:, 0:1]))
            c(v_.tensor_tensor(delta[:, 1:NE], rel0[:, 1:NE], rel0[:, 0:NE - 1], ALU.subtract))
            c(v_.tensor_scalar(p15, pI, GROUP - 1, None, ALU.bitwise_and))
            c(v_.tensor_scalar(p4, pI, 4, None, ALU.logical_shift_right))
            c(v_.tensor_copy(p15f, p15))
            c(v_.tensor_copy(p4f, p4))
            c(v_.tensor_copy(cF, cI))
            c(v_.scalar_tensor_tensor(tp, p15f, float(sz.chunk), p4f, ALU.mult, ALU.add))
            c(v_.tensor_scalar(tpos, cF, tp, None, ALU.add))
            c(v_.tensor_tensor(M, bc(cum, [P, NC, NE], 1), tpos.unsqueeze(2).to_broadcast([P, NC, NE]), ALU.is_le))
            c(v_.tensor_reduce(bt, M, AX.X, ALU.add))
            c(v_.tensor_scalar(bt, bt, -1.0, None, ALU.add))
            c(v_.tensor_tensor(MD, M, bc(delta, [P, NC, NE], 1), ALU.mult))
            c(v_.tensor_reduce(st, MD, AX.X, ALU.add))
            c(v_.scalar_tensor_tensor(st, tpos, float(P), st, ALU.mult, ALU.add))
            c(v_.tensor_scalar(st, st, float(sz.edge_end), None, ALU.min))
            c(v_.tensor_copy(bI, bt))
            c(v_.tensor_copy(sI, st))
            c(v_.tensor_scalar(wI, sI, 4, None, ALU.logical_shift_right))
            dve.sem_inc(windows_known, 1)
            c(v_.tensor_scalar(off, bt, -float(P), None, ALU.mult))
            dve.wait_ge(w_loaded, 16 * 13)
            dve.sem_inc(sig_in, 1)
            c(v_.tensor_copy(CTXB, CTXC.to_broadcast([CTX, P])))
            dve.sem_inc(film_in, 1)
            ntf = st1
            c(v_.tensor_copy(ntf[:, :], NTI))
            dve.wait_ge(sig_out, 1)
            c(v_.memset(ALPHA[:, :], 0.0))
            for t in range(TYPES):
                c(v_.tensor_scalar(MASK[:, :, t], ntf[:, :], float(t), None, ALU.is_equal))
                c(v_.scalar_tensor_tensor(ALPHA[:, :], MASK[:, :, t], SIG[:, t:t + 1], ALPHA[:, :], ALU.mult, ALU.add))
            c(v_.tensor_scalar(PRI.rearrange("p (h d) -> p h d", h=HEADS), PRI8.unsqueeze(2).to_broadcast([P, HEADS, DH]),
                               float(DH) ** -0.5, None, ALU.mult))
            dve.wait_ge(w_combined, 1)
            c(v_.tensor_copy(W3[:, :, 0:D], PB[1][:, 0:3 * D].rearrange("p (t d) -> p t d", t=3)))
            c(v_.tensor_copy(W3[:, :, D:2 * D], PB[2][:, 0:3 * D].rearrange("p (t d) -> p t d", t=3)))
            c(v_.tensor_tensor(ROWS[:, 3:5, :].rearrange("p a d -> p (a d)"), ROWS[:, 3:5, :].rearrange("p a d -> p (a d)"),
                               PB[3][:, 0:2 * D], ALU.add))
            dve.wait_ge(windows_in, 32 * NC)
            c(v_.tensor_copy(SRCF, SRCW))
            c(v_.tensor_copy(DKF, DSTW))
            c(v_.tensor_tensor(RELF, DKF, off.unsqueeze(2).to_broadcast([P, NC, P]), ALU.add))
            c(v_.tensor_scalar(VAL, RELF, 0.0, None, ALU.is_ge))
            c(v_.scalar_tensor_tensor(VAL, RELF, float(P), VAL, ALU.is_lt, ALU.mult))
            c(v_.scalar_tensor_tensor(KEYW, DKF, 1.0, VAL, ALU.add, ALU.mult))
            c(v_.tensor_scalar(KEYW, KEYW, -1.0, None, ALU.add))
            c(v_.memset(KEY[:, 0:1], -2.0))
            c(v_.memset(KEY[:, sz.span + 1:sz.span + 2], -3.0))
            dve.sem_inc(tiles_masked, 1)
            dve.wait_ge(tiles_turned, 1)
            for k, dst in enumerate((REL, SRC)):
                for h in range(-(-NC // 4)):
                    n = min(4, NC - 4 * h) * P
                    c(v_.tensor_copy(dst[:, 4 * h * P:4 * h * P + n], PB[2 * k + h][:, 0:n]))
            dve.wait_ge(keys_in, 16 * 24)
            c(v_.tensor_tensor(KEY[:, 0:sz.span + 1], KEY[:, 1:sz.span + 2], KEY[:, 0:sz.span + 1], ALU.not_equal))
            c(v_.tensor_scalar(flags, KEY[:, 0:sz.span + 1], NEG, None, ALU.mult))

            dve.wait_ge(x_loaded, 16)
            layer_norm(X, H)
            relu_scaled(H)
            dve_proj(dve, 0)
            s = scored

            def step(i, u):
                q, slot, turn, v = at(i, u, 0)
                if valid(q):
                    onehot(0, q, slot)
                q, slot, turn, v = at(i, u, -2)
                if valid(q):
                    par = v % 2
                    dve.wait_ge(s["q_spread"], q + 1)
                    dve.wait_ge(ps[0]["gathered"][slot], (turn + 1) * 64)
                    v_.tensor_tensor(PROD[:, par, :, :], G2[:, slot, :, 0:D], QD[par], ALU.mult).then_inc(s["multiplied"], 1)
                    dve.wait_ge(s["multiplied"], q + 1)
                    if v % 4 == 0:
                        wait(dve, s["grp_turned"], group_of(i, u, -2) - 1)
                    v_.tensor_reduce(ABUF[:, (v // 4) % 2, (v % 4) * 32:(v % 4) * 32 + 32].rearrange("p (j h) -> p j h", j=QUAD),
                                     PROD[:, par, :, :].rearrange("p j (h d) -> p j h d", h=HEADS), AX.X, ALU.add
                                     ).then_inc(s["reduced"], 1)
            steps(dve, step, 2)
            dve.sem_inc(w_free, 1)

            dve.wait_ge(s["grp_copied"], sz.groups)
            back = slice(None, None, -1)
            for k in range(2):
                if k == 0:
                    fl, data, out = flags[:, 0:sz.span], AT, FMAX
                else:
                    fl, data, out = flags[:, 1:sz.span + 1][:, ::-1], FMAX[:, ::-1], FMAX[:, ::-1]
                c(v_.tensor_tensor_scan(out, fl, data, 2 * NEG, ALU.add, ALU.max))
                c(v_.tensor_copy(small[:, 0:1], FMAX[:, sz.span - 1:sz.span] if k == 0 else FMAX[:, 0:1]))
                c(v_.tensor_reduce(small[:, 1:2], fl if k == 0 else flags[:, 1:sz.span + 1], AX.X, ALU.min))
                dve.sem_inc(carry_in, 1)
                dve.wait_ge(carry_rows, k + 1)
                hc = lambda r: CLINE(r).rearrange("o (h t) -> o h t", h=HEADS)
                th = lambda r: CLINE(r).rearrange("o (t h) -> o h t", h=HEADS)
                edge = 0 if k == 0 else GROUP - 1
                c(v_.tensor_copy(hc(0), PB[0][0:1, 0:P].rearrange("o (t h) -> o h t", h=HEADS)))
                c(v_.tensor_copy(hc(1), PB[0][0:1, P:2 * P].rearrange("o (t h) -> o h t", h=HEADS)))
                c(v_.memset(hc(1)[:, :, edge:edge + 1], NEG))
                if k == 0:
                    c(v_.tensor_tensor_scan(CLINE(2), CLINE(1), CLINE(0), 2 * NEG, ALU.add, ALU.max))
                    c(v_.memset(CLINE(3), 2 * NEG))
                    c(v_.tensor_copy(th(3)[:, :, 1:GROUP], hc(2)[:, :, 0:GROUP - 1]))
                else:
                    c(v_.tensor_tensor_scan(CLINE(2)[:, ::-1], CLINE(1)[:, ::-1], CLINE(0)[:, ::-1], 2 * NEG, ALU.add, ALU.max))
                    c(v_.memset(CLINE(3), 2 * NEG))
                    c(v_.tensor_copy(th(3)[:, :, 0:GROUP - 1], hc(2)[:, :, 1:GROUP]))
                dve.sem_inc(carry_row, 1)
                dve.wait_ge(carry_col, k + 1)
                c(v_.tensor_copy(small[:, 2:3], PB[1][:, 0:1]))
                out = FMAX if k == 0 else FMAX[:, ::-1]
                c(v_.tensor_tensor_scan(out, fl, out, small[:, 2:3], ALU.add, ALU.max))
            c(v_.tensor_tensor(FMAX, AT, FMAX, ALU.subtract))
            dve.sem_inc(exp_in, 1)
            dve.wait_ge(hist_in, 16)
            c(v_.tensor_scalar(SRCTMP, SRCPM, P - 1, None, ALU.bitwise_and))
            c(v_.tensor_copy(LO, SRCTMP))
            c(v_.tensor_scalar(SRCTMP, SRCPM, 7, None, ALU.logical_shift_right))
            c(v_.tensor_copy(HI, SRCTMP))
            c(v_.memset(acc0, 0.0))
            c(v_.memset(WM[:, :, :, D + HEADS:D + HEADS + 1], 1.0))
            dve.sem_inc(weighted["ones_set"], 1)

            def step(i, u):
                q, slot, turn, v = at(i, u, 0)
                if valid(q):
                    onehot(1, q, slot)
                    cols = bass.ds(q * QUAD, QUAD)
                    v_.tensor_tensor(LOH[:, slot, :, :], bc(iota[:, :], [P, QUAD, P], 1),
                                     LO[:, cols].unsqueeze(2).to_broadcast([P, QUAD, P]), ALU.is_equal)
                    v_.tensor_tensor(HIH[:, slot, :, :], bc(iota[:, 0:NS], [P, QUAD, NS], 1),
                                     HI[:, cols].unsqueeze(2).to_broadcast([P, QUAD, NS]), ALU.is_equal
                                     ).then_inc(weighted["hist_ready"], 1)
                q, slot, turn, v = at(i, u, -3)
                if valid(q):
                    add_rows(1, acc0, WMW, q, v % 2)
            steps(dve, step, 3)
            dve.wait_ge(ps[1]["rows_added"], T)
            c(v_.tensor_copy(OUTDEG[:, :], HISTP))
            c(v_.tensor_copy(DEG[:, :], acc0[:, :, D + HEADS:D + HEADS + 1].rearrange("p b o -> p (b o)")))
            probs = acc0[:, :, D:D + HEADS]
            c(v_.tensor_scalar(probs, probs, 0.5, None, ALU.max))
            c(v_.reciprocal(probs, probs))
            for h in range(HEADS):
                c(v_.tensor_tensor(QT[:, :, h * DH:(h + 1) * DH], acc0[:, :, h * DH:(h + 1) * DH],
                                   acc0[:, :, D + h:D + h + 1].to_broadcast([P, NS, DH]), ALU.mult))
            dve.wait_ge(w_next, 16)
            dve_proj(dve, 1)
            c(v_.tensor_tensor(QT, QT, H[:, :, :], ALU.subtract))
            c(v_.tensor_tensor(QT, QT, over(ALPHA[:, :]), ALU.mult))
            c(v_.tensor_tensor(QT, QT, H[:, :, :], ALU.add))
            layer_norm(QT, QT)
            c(v_.tensor_tensor(QT, QT, over(st2[:, :]), ALU.mult))
            c(v_.tensor_tensor(QT, QT, vec(1), ALU.mult))
            c(v_.tensor_tensor(QT, QT, vec(2), ALU.add))
            c(v_.tensor_tensor(QT, QT, H[:, :, :], ALU.add))
            c(v_.tensor_tensor(QT, QT, vec(3), ALU.mult))
            c(v_.tensor_tensor(QT, QT, vec(4), ALU.add))
            c(v_.tensor_tensor(X[:, :, :], X[:, :, :], QT, ALU.add))

            layer_norm(X, H)
            relu_scaled(H)
            for deg in (DEG, OUTDEG):
                c(v_.tensor_scalar(st1[:, :] if deg is DEG else OUTDEG[:, :], deg[:, :], 1.0, 1.0, ALU.add, ALU.max))
                d2 = st1 if deg is DEG else OUTDEG
                root(d2)
            c(v_.tensor_tensor(H[:, :, :], H[:, :, :], over(st1[:, :]), ALU.mult))
            dve.sem_inc(table_made, 1)
            c(v_.memset(acc1, 0.0))
            plain(dve, 2, onehot, add_rows)
            c(v_.tensor_tensor(acc1, acc1, H[:, :, :], ALU.add))
            c(v_.tensor_tensor(acc1, acc1, over(OUTDEG[:, :]), ALU.mult))
            c(v_.tensor_tensor(X[:, :, :], X[:, :, :], acc1, ALU.add))

            layer_norm(X, H)
            relu_scaled(H)
            dve.wait_ge(w_next, 16 * 7)
            dve_proj(dve, 2)
            c(v_.tensor_tensor(H[:, :, :], H[:, :, :], vec(0), ALU.add))
            c(v_.memset(acc2, 0.0))
            s = gated

            def step(i, u):
                q, slot, turn, v = at(i, u, 0)
                if valid(q):
                    onehot(3, q, slot)
                q, slot, turn, v = at(i, u, -2)
                if valid(q):
                    dve.wait_ge(s["pre_done"], q + 1)
                    dve.wait_ge(ps[3]["gathered"][slot], (turn + 1) * 64)
                    wait(dve, s["gate_done"], q - 1)
                    v_.tensor_tensor(PRE[:, v % 2, :, :], QD[v % 2], G2[:, slot, :, 0:D], ALU.add).then_inc(s["summed"], 1)
                q, slot, turn, v = at(i, u, -3)
                if valid(q):
                    dve.wait_ge(s["gate_done"], q + 1)
                    v_.tensor_tensor(RHS[:, v % 2, :, 0:D], G2[:, slot, :, D:2 * D], RHS[:, v % 2, :, D:2 * D],
                                     ALU.mult).then_inc(s["multiplied"], 1)
                q, slot, turn, v = at(i, u, -4)
                if valid(q):
                    add_rows(3, acc2, 2 * D, q, v % 2)
            steps(dve, step, 4)
            dve.wait_ge(ps[3]["rows_added"], T)
            norm, summed = acc2[:, :, D:2 * D], acc2[:, :, 0:D]
            c(v_.tensor_scalar(norm, norm, 1e-6, None, ALU.max))
            c(v_.reciprocal(norm, norm))
            c(v_.tensor_tensor(summed, summed, norm, ALU.mult))
            c(v_.tensor_tensor(summed, summed, H[:, :, :], ALU.add))
            c(v_.tensor_tensor(X[:, :, :], X[:, :, :], summed, ALU.add))

            layer_norm(X, H)
            relu_scaled(H)
            dve.sem_inc(table_made, 1)
            c(v_.memset(acc1, 0.0))
            plain(dve, 4, onehot, add_rows)
            c(v_.tensor_scalar(st1[:, :], DEG[:, :], 1.0, None, ALU.max))
            c(v_.reciprocal(st1[:, :], st1[:, :]))
            c(v_.tensor_tensor(QT, acc1, over(st1[:, :]), ALU.mult))
            dve.wait_ge(w_next, 16 * 12)
            dve_proj(dve, 3)
            c(v_.tensor_tensor(QT, QT, vec(0), ALU.add))
            layer_norm(QT, QT)
            c(v_.tensor_tensor(QT, QT, over(st2[:, :]), ALU.mult))
            c(v_.tensor_tensor(QT, QT, vec(1), ALU.mult))
            c(v_.tensor_tensor(QT, QT, vec(2), ALU.add))
            dve.sem_inc(gelu_in, 1)
            dve.wait_ge(gelu_out, 1)
            c(v_.tensor_tensor(X[:, :, :], X[:, :, :], QT, ALU.add))
            dve.sem_inc(x_final, 1)


def kernel(x, src, dst, edge_attr_128, node_type_3, **w):
    import concourse.bacc as _bacc
    from concourse.bass_utils import run_bass_kernel_spmd as _run

    x, src, dst, ea, ntype = (np.asarray(v) for v in (x, src, dst, edge_attr_128, node_type_3))
    w = {k: np.asarray(v) for k, v in w.items()}
    sz = Sizes(x.shape[0], src.shape[0])
    rows = sz.slots * P
    cont = np.ascontiguousarray

    def padded(v, n, value):
        out = np.full((n,) + v.shape[1:], value, v.dtype)
        out[:v.shape[0]] = v
        return out

    def windows(v, value):
        v = padded(v, sz.edge_end + P, value)
        return cont(np.lib.stride_tricks.sliding_window_view(v, P)[::ALIGN])

    def by_head(m):
        out = np.zeros((D, D), m.dtype)
        for h in range(HEADS):
            out[h * DH:(h + 1) * DH, h * DH:(h + 1) * DH] = m[h]
        return out

    arrays = {
        "x": padded(x, rows, 0),
        "src_win": windows(src, 0), "dst_win": windows(dst, PAD_NODE),
        "src_pm": padded(src, P * sz.tiles, sz.blocks * P).reshape(P, sz.tiles),
        "dst_pm": padded(dst, P * sz.tiles, PAD_NODE).reshape(P, sz.tiles),
        "ea_t": cont(padded(ea, sz.edge_end + P, 0).T),
        "ntype": cont(padded(ntype, rows, 0).reshape(sz.slots, P).T),
        "ctx": w["L0_gnn_global_context"],
        "wk_t": cont(w["L0_gnn_Wk"].transpose(0, 2, 1)), "wv_t": cont(w["L0_gnn_Wv"].transpose(0, 2, 1)),
        "wq": w["L0_gnn_Wq"], "att": by_head(w["L0_gnn_rel_att"]), "msg": by_head(w["L0_gnn_rel_msg"]),
        "pri": w["L0_gnn_rel_pri"], "wa": w["L0_gnn_Wa"], "skip": w["L0_gnn_skip"],
        "ln_g": w["L0_gnn_ln_g"], "ln_b": w["L0_gnn_ln_b"], "film_w": w["L0_gnn_film_w"], "film_b": w["L0_gnn_film_b"],
        "w_root": w["L2_gnn_W_root"], "b_root": w["L2_gnn_b_root"], "w_msg": w["L2_gnn_W_msg"],
        "w_src": w["L2_gnn_W_src"], "w_dst": w["L2_gnn_W_dst"], "w_edge": w["L2_gnn_W_edge"],
        "w_l": w["L3_gnn_W_l"], "b_l": w["L3_gnn_b_l"], "w_r": w["L3_gnn_W_r"],
        "gamma": w["L3_gnn_gamma"], "beta": w["L3_gnn_beta"],
    }
    nc = _bacc.Bacc("TRN2", target_bir_lowering=False, num_devices=1)
    a, feeds = {}, {}
    for name, v in arrays.items():
        feeds[f"in_{name}"] = cont(v)
        a[name] = nc.dram_tensor(f"in_{name}", v.shape, mybir.dt.from_np(v.dtype), kind="ExternalInput").ap()
    a["out"] = nc.dram_tensor("out_x", (sz.nodes, D), F32, kind="ExternalOutput").ap()
    build(nc, sz, a)
    return _run(nc, [feeds], core_ids=[0]).results[0]["out_x"]
```

```python
import numpy as np
import concourse.bass as bass
from concourse import mybir
from contextlib import ExitStack

F32 = mybir.dt.float32
BF16 = mybir.dt.bfloat16
I32 = mybir.dt.int32
ALU = mybir.AluOpType
ACT = mybir.ActivationFunctionType
AX = mybir.AxisListType

P = 128
D = 128
HEADS = 8
DH = D // HEADS
TYPES = 3
CTX = 64
EPS = 1e-5
ALIGN = 16
QUAD = 4
RING = 4
UNROLL = 8
GROUP = 16
NEG = -1e30
PAD_NODE = 1 << 20
PARTS = 4


class Sizes:

    def __init__(self, nodes, edges):
        self.nodes, self.edges = nodes, edges
        self.blocks = -(-nodes // P)
        self.slots = self.blocks + 1
        self.slots += self.slots % 2
        most = (edges + self.blocks * (P - 1 + ALIGN - 1)) // P
        self.tiles = -(-most // P) * P
        self.edge_end = -(-edges // ALIGN) * ALIGN
        self.windows = self.edge_end // ALIGN + 1
        self.cols = self.tiles // P
        self.chunk = self.tiles // GROUP // PARTS
        self.quads = self.tiles // QUAD
        self.groups = self.tiles // GROUP
        self.iters = self.quads // UNROLL
        self.span = self.chunk * P
        self.part_iters = self.iters // PARTS
        assert self.iters % PARTS == 0


def wait(eng, sem, value):
    if isinstance(value, int) and value <= 0:
        return
    eng.wait_ge(sem, value)


def build(nc, sz, a):
    NB, NS, T = sz.blocks, sz.slots, sz.tiles
    NQ = sz.quads
    ctx = ExitStack()
    with ctx:
        def sb(name, shape, dt=F32):
            return ctx.enter_context(nc.sbuf_tensor(name, shape, dt))

        def sem(name):
            return ctx.enter_context(nc.semaphore(name))

        def dram(name, shape, dt=F32):
            return nc.dram_tensor(name, shape, dt, kind="Internal").ap()

        tab2 = dram("tab2", (NS * P, 2 * D))
        tab1 = dram("tab1", (NS * P, D))
        mvd = dram("mvd", (NQ, P, QUAD * D))
        keyd = dram("keyd", (T, P))
        metad = dram("metad", (2, T), I32)

        X = sb("X", [P, NS, D])
        H = sb("H", [P, NS, D])
        QTR = sb("QTR", [P, NS * D])
        accw = NS * (D + HEADS + 1)
        fw = sz.span + 2
        ACCR = sb("ACCR", [P, max(NS * 2 * D, accw + 3 * sz.span, PARTS * fw)])
        FLG = sb("FLG", [P, max(PARTS * fw // 2, 2 * QUAD * 2 * D + T, 3 * T)])
        MV = sb("MV", [P, RING, QUAD, D])
        G = sb("G", [P, RING * QUAD * 2 * D])
        SCR = sb("SCR", [P, 3072])
        S = sb("S", [P, RING, QUAD, P])
        ST = sb("ST", [P, 2, QUAD, P])
        REL = sb("REL", [P, T])
        SRC = sb("SRC", [P, T], I32)
        ISLOT = sb("ISLOT", [P, RING, QUAD], I32)
        BROW = sb("BROW", [1, T], I32)
        W = sb("W", [P, TYPES * 3 * D])
        ROWS = sb("ROWS", [P, 5, D])
        ident = sb("ident", [P, P])
        identb = sb("identb", [P, P], BF16)
        iota = sb("iota", [P, P])
        MASK = sb("MASK", [P, NS, TYPES])
        ALPHA = sb("ALPHA", [P, NS])
        DEG = sb("DEG", [P, NS])
        OUTDEG = sb("OUTDEG", [P, NS])
        st1 = sb("st1", [P, NS])
        st2 = sb("st2", [P, NS])
        small = sb("small", [P, 16])
        LASTK = sb("LASTK", [1, 8])

        QT = QTR[:, 0:NS * D].rearrange("p (b d) -> p b d", d=D)
        acc0 = ACCR[:, 0:accw].rearrange("p (b d) -> p b d", d=D + HEADS + 1)
        acc1 = ACCR[:, 0:NS * D].rearrange("p (b d) -> p b d", d=D)
        acc2 = ACCR[:, 0:NS * 2 * D].rearrange("p (b d) -> p b d", d=2 * D)
        WIDE = acc1
        AT = ACCR[:, accw:accw + 2 * sz.span].rearrange("p (r g e) -> p r g e", r=2, e=P)
        FMAX = ACCR[:, accw + 2 * sz.span:accw + 3 * sz.span]
        KEY = ACCR[:, 0:PARTS * fw].rearrange("p (m j) -> p m j", m=PARTS)
        flags = FLG[:, 0:PARTS * fw // 2].bitcast(BF16).rearrange("p (m j) -> p m j", m=PARTS)
        SROW = FLG[0:1, 2 * QUAD * 2 * D:2 * QUAD * 2 * D + T].bitcast(I32)
        RHS = FLG[:, 0:2 * QUAD * 2 * D].rearrange("p (r j d) -> p r j d", r=2, j=QUAD)
        G2 = G[:, :].rearrange("p (r j d) -> p r j d", r=RING, j=QUAD)
        G1 = G[:, 0:RING * QUAD * D].rearrange("p (r j d) -> p r j d", r=RING, j=QUAD)

        PSA = ctx.enter_context(nc.psum_tensor("PSA", [P, 2, QUAD, 2 * D], F32))
        PB = [ctx.enter_context(nc.psum_tensor(f"PB{i}", [P, 512], F32)) for i in range(4)]
        STP = [PB[3 * r][:, 0:256].bitcast(BF16).rearrange("p (j e) -> p j e", j=QUAD) for r in range(2)]
        QD = [PB[1 + r][:, :].rearrange("p (j d) -> p j d", j=QUAD) for r in range(2)]
        HOP = PB[3][:, 3 * P:4 * P]

        dve_done = sem("dve_done")
        consts = sem("consts")

        def edge_sems(n):
            s = {"onehot_ready": sem(f"onehot_ready_{n}")}
            if n != "scores":
                s |= {k: sem(f"{k}_{n}") for k in ("agg_done", "rows_added")}
            if n != "messages":
                s |= {k: [sem(f"{k}{r}_{n}") for r in range(RING)] for k in ("idx_filled", "gathered")}
            return s

        block = ctx.enter_context(nc.Block())
        reg_note = "computed on the chip from the tile's position, always in range"

        def at(i, u, d):
            v = u + d
            i = i + v // UNROLL if v // UNROLL else i
            v %= UNROLL
            return i * UNROLL + v, v % RING, i * (UNROLL // RING) + v // RING, v

        def valid(q):
            return not isinstance(q, int) or 0 <= q < NQ

        def steps(eng, fn, trailing):
            for u in range(UNROLL):
                fn(0, u)
            if sz.iters > 2:
                with eng.Fori(1, sz.iters - 1) as i:
                    for u in range(UNROLL):
                        fn(i, u)
            for u in range(UNROLL):
                fn(sz.iters - 1, u)
            for u in range(trailing):
                fn(sz.iters, u)

        LAG = sz.part_iters + 1
        hooks = [m * sz.part_iters + LAG for m in range(PARTS)]

        def layer0_steps(eng, fn, hook=None):
            last = sz.iters + LAG
            at_edge = {0, sz.iters - 1, sz.iters, LAG, last - 1, last} | set(hooks)
            i = 0
            while i <= last:
                if i in hooks and hook:
                    hook(hooks.index(i))
                on = (i <= sz.iters, i >= LAG)
                if i in at_edge:
                    for u in range(UNROLL):
                        fn(i, u, *on)
                    i += 1
                    continue
                j = i
                while j not in at_edge:
                    j += 1
                with eng.Fori(i, j) as r:
                    for u in range(UNROLL):
                        fn(r, u, *on)
                i = j

        def pairs(eng, fn, trailing):
            n = NS // 2
            for r in range(4):
                fn(r, r % 2)
            if n > 3:
                with eng.Fori(2, n - 1) as i:
                    for r in range(2):
                        fn(i * 2 + r, r)
            for r in range(2):
                fn(NS - 2 + r, r)
            for r in range(trailing):
                fn(NS + r, r)

        def group_of(i, u, d):
            v = u + d
            i = i + v // UNROLL if v // UNROLL else i
            return i * (UNROLL * QUAD // GROUP) + (v % UNROLL) // QUAD

        def CLINE(k):
            return W[0:1, TYPES * D + k * P:TYPES * D + (k + 1) * P]

        def has_block(b):
            return not isinstance(b, int) or 0 <= b < NS

        class Chain:

            def __init__(self, eng, s):
                self.eng, self.sem, self.n = eng, s, 0

            def __call__(self, ins):
                ins.then_inc(self.sem, 1)
                self.n += 1
                self.eng.wait_ge(self.sem, self.n)

        def bc(ap, shape, dim):
            return ap.unsqueeze(dim).to_broadcast(shape)


        c_ready = sem("consts_ready")
        dst_loaded = sem("dst_loaded")
        x_loaded = sem("x_loaded")
        w_loaded = sem("w_loaded")
        counted = sem("counted")
        totals = sem("totals")
        windows_known = sem("windows_known")
        windows_in = sem("windows_in")
        tiles_masked = sem("tiles_masked")
        tiles_turned = sem("tiles_turned")
        keys_stored = sem("keys_stored")
        keys_in = sem("keys_in")
        scale_in = sem("scale_in")
        scale_out = sem("scale_out")
        rescaled = sem("rescaled")
        rows_in = sem("rows_in")
        w_combined = sem("w_combined")
        sig_in = sem("sig_in")
        sig_out = sem("sig_out")
        film_in = sem("film_in")
        centred = sem("centred")
        squared = sem("squared")
        root_in = sem("root_in")
        root_out = sem("root_out")
        hop_in = sem("hop_in")
        hop_out = sem("hop_out")
        exp_in = sem("exp_in")
        exp_out = sem("exp_out")
        w_free = sem("w_free")
        w_next = sem("w_next")
        hist_in = sem("hist_in")
        table_made = sem("table_made")
        table_out = sem("table_out")
        srow_in = sem("srow_in")
        gelu_in = sem("gelu_in")
        gelu_out = sem("gelu_out")
        x_final = sem("x_final")
        out_stored = sem("out_stored")

        NE = NB + 1
        keys_dmas = PARTS * HEADS * 3 + (PARTS - 1) * (HEADS + 1)
        NC = sz.cols
        WK = 3 * D

        DSTI = G[:, 0:T].bitcast(I32)
        DSTF = G[:, T:2 * T]
        SRCW = G[:, 2 * T:3 * T].bitcast(I32).rearrange("p (c e) -> p c e", c=NC)
        DSTW = G[:, 3 * T:4 * T].bitcast(I32).rearrange("p (c e) -> p c e", c=NC)
        SRCF = SCR[:, 0:T].rearrange("p (c e) -> p c e", c=NC)
        RELF = SCR[:, T:2 * T].rearrange("p (c e) -> p c e", c=NC)
        JUNK = SCR[:, 2 * T:3 * T]
        VAL = JUNK.rearrange("p (c e) -> p c e", c=NC)
        DKF = DSTF.rearrange("p (c e) -> p c e", c=NC)
        KEYW = G[:, 0:T].rearrange("p (c e) -> p c e", c=NC)
        q0 = [0]

        def cut(n, dt=F32):
            v = QTR[:, q0[0]:q0[0] + n]
            q0[0] += n
            return v if dt == F32 else v.bitcast(dt)

        thr, cnt, bf, b16f, tiles_f, zer, cum, rel0, delta = (cut(NE) for _ in range(9))
        bi = cut(NE, I32)
        ti32 = cut(NE, I32)
        ones = cut(P)
        pI, p15, p4 = (cut(1, I32) for _ in range(3))
        p15f, p4f, tp = (cut(1) for _ in range(3))
        cI = cut(NC, I32)
        cF, tpos, bt, st, off = (cut(NC) for _ in range(5))
        bI, sI, wI = (cut(NC, I32) for _ in range(3))
        M = cut(NC * NE).rearrange("p (c b) -> p c b", c=NC)
        MD = cut(NC * NE).rearrange("p (c b) -> p c b", c=NC)
        thrI = cut(NE, I32)
        iotaI = cut(P, I32)
        NTI = cut(NS, I32)
        SKIP = cut(4)
        SIG = cut(4)
        PRI8 = cut(HEADS)
        SF = S[:, :, :, :].rearrange("p r j e -> p (r j e)")
        WKT = SF[:, 0:384].rearrange("p (t d) -> p t d", t=3)
        WVT = SF[:, 384:768].rearrange("p (t d) -> p t d", t=3)
        ATTB, MSGB = SF[:, 768:896], SF[:, 896:1024]
        FILMW = SF[0:CTX, 1024:1280]
        CTXB = SF[0:CTX, 1280:1408]
        CTXC = SF[0:CTX, 1408:1409]
        W3 = W[:, :].rearrange("p (t c) -> p t c", t=TYPES)
        WA = W[:, 0:TYPES * D].rearrange("p (t c) -> p t c", t=TYPES)
        PRI = ROWS[:, 0, :]

        MB = G[:, 0:2 * WK].rearrange("p (r t d) -> p r t d", r=2, t=3)
        HT = G[:, 2 * WK:4 * WK].rearrange("p (r t d) -> p r t d", r=2, t=3)
        STG = G[:, 4 * WK:4 * WK + 4 * D].rearrange("p (r d) -> p r d", r=2)

        def proj_sems(n):
            s = {k: sem(f"{k}_{n}") for k in ("placed", "turned", "copied", "multiplied", "evacuated", "inputs")}
            if n in ("typed_qkv", "gate_nodes"):
                s["stored"] = [sem(f"stored{r}_{n}") for r in range(2)]
            return s

        proj = [proj_sems(n) for n in ("typed_qkv", "typed_out", "gate_nodes", "sage")]
        proj_w = [
            (3, lambda t: W3[:, t, :], WK),
            (3, lambda t: WA[:, t, :], D),
            (1, lambda t: W[:, 0:4 * D], 4 * D),
            (2, lambda t: W[:, t * D:(t + 1) * D], D),
        ]

        def pe_proj(pe, n):
            s, (ni, w, cols) = proj[n], proj_w[n]
            pe.wait_ge(s["inputs"], 1)

            def step(b, r):
                if has_block(b):
                    pe.wait_ge(s["placed"], b + 1)
                    wait(pe, s["copied"], b - 1)
                    for t in range(ni):
                        last = nc.tensor.transpose(PB[r][:, t * P:(t + 1) * P], MB[:, r, t, :], ident[:, :])
                    last.then_inc(s["turned"], 1)
                m = b - 1
                if has_block(m):
                    pe.wait_ge(s["copied"], m + 1)
                    wait(pe, s["evacuated"], m - 1)
                    for t in range(ni):
                        last = nc.tensor.matmul(PB[2 + (1 - r)][:, 0:cols], HT[:, 1 - r, t, :], w(t),
                                                start=t == 0, stop=t == ni - 1)
                    last.then_inc(s["multiplied"], 1)
            pairs(pe, step, 1)

        def act_proj(act, n):
            s, (ni, w, cols) = proj[n], proj_w[n]

            def step(b, r):
                act.wait_ge(s["turned"], b + 1)
                wait(act, s["multiplied"], b - 1)
                nc.scalar.copy(HT[:, r, 0:ni, :].rearrange("p t d -> p (t d)"),
                               PB[r][:, 0:ni * P]).then_inc(s["copied"], 1)
            pairs(act, step, 0)

        def dve_proj(dve, n):
            s = proj[n]
            dve.sem_inc(s["inputs"], 1)

            def copy(dst, src):
                return nc.vector.tensor_scalar(dst, src, 1.0, None, ALU.mult)

            def step(b, r):
                if has_block(b):
                    wait(dve, s["turned"], b - 1)
                if n == 3 and has_block(b):
                    copy(MB[:, r, 0:1, :], QT[:, bass.ds(b, 1), :])
                if n in (2, 3) and has_block(b):
                    copy(MB[:, r, n - 2:n - 1, :], H[:, bass.ds(b, 1), :]).then_inc(s["placed"], 1)
                if n in (0, 1) and has_block(b):
                    src = H if n == 0 else QT
                    nc.vector.tensor_tensor(
                        MB[:, r, :, :], src[:, bass.ds(b, 1), :].to_broadcast([P, 3, D]),
                        MASK[:, bass.ds(b, 1), :].rearrange("p o t -> p (o t)").unsqueeze(2).to_broadcast([P, 3, D]),
                        ALU.mult).then_inc(s["placed"], 1)
                m, rm = b - 2, r
                if has_block(m):
                    dve.wait_ge(s["multiplied"], m + 1)
                    ps = PB[2 + rm]
                    row = lambda tab: tab[:, bass.ds(m, 1), :].rearrange("p o d -> p (o d)")
                    if n in (1, 3):
                        copy(row(QT), ps[:, 0:D]).then_inc(s["evacuated"], 1)
                        return
                    if n == 0:
                        nc.vector.tensor_tensor(row(QT), ps[:, 2 * D:3 * D], PRI, ALU.mult)
                    else:
                        copy(row(QT), ps[:, 2 * D:3 * D])
                        nc.vector.tensor_tensor(row(H), row(H), ps[:, 3 * D:4 * D], ALU.add)
                    half = m // 2 if isinstance(m, int) else None
                    if isinstance(m, int):
                        wait(dve, s["stored"][rm], half * 16)
                    else:
                        dve.wait_ge(s["stored"][rm], (m - rm) * 8)
                    copy(STG[:, rm, :], ps[:, 0:2 * D]).then_inc(s["evacuated"], 1)
            pairs(dve, step, 2)
            dve.wait_ge(s["evacuated"], NS)

        def sp_proj(sp, n):
            s = proj[n]

            def step(b, r):
                sp.wait_ge(s["evacuated"], b + 1)
                sp.dma_start(tab2[bass.ds(b * P, P), :], STG[:, r, :]).then_inc(s["stored"][r], 16)
            pairs(sp, step, 0)

        names = ("scores", "messages", "degree", "gated", "mean")
        ps = [edge_sems(n) for n in names]
        scored = {k: sem(k + "_scores") for k in ("st_turned", "st_copied", "q_spread", "multiplied", "reduced", "grp_turned", "grp_copied")}
        mv_stored = [sem(f"mv_stored{r}") for r in range(RING)]
        mv_loaded = [sem(f"mv_loaded{r}") for r in range(RING)]
        weighted = {k: sem(k + "_messages") for k in ("grp_staged", "grp_turned", "grp_copied", "prob_put", "weighted")}
        hist_ready = sem("hist_ready")
        gated = {k: sem(k + "_gated") for k in ("st_turned", "st_copied", "pre_done", "summed", "gate_done", "multiplied")}
        ea_loaded = [sem(f"ea_loaded{r}") for r in range(RING)]
        may_gather = sem("may_gather")
        may_move = sem("may_move")
        rows_read = {0: scored["multiplied"], 2: ps[2]["agg_done"], 3: gated["multiplied"], 4: ps[4]["agg_done"]}

        PROD = SCR[:, 0:1024].rearrange("p (r j d) -> p r j d", r=2, j=QUAD)
        ABUF = SCR[:, 1024:1280].rearrange("p (r c) -> p r c", r=2)
        WMW = D + HEADS + 1
        WM = SCR[:, 1280:1280 + 2 * QUAD * WMW].rearrange("p (r j d) -> p r j d", r=2, j=QUAD)
        AE = SCR[:, 2400:2656].rearrange("p (r c) -> p r c", r=2)
        ATS = SCR[:, 2656:2912].rearrange("p (r e) -> p r e", r=2)
        LOH = SCR[:, 0:1024].bitcast(BF16).rearrange("p (r j c) -> p r j c", r=RING, j=QUAD)
        HIH = SCR[:, 1024:1024 + RING * QUAD * NS // 2].bitcast(BF16).rearrange("p (r j c) -> p r j c", r=RING, j=QUAD)
        LO = FLG[:, 0:T // 2].bitcast(BF16)
        HI = FLG[:, T // 2:T].bitcast(BF16)
        SRCPM = FLG[:, T:2 * T].bitcast(I32)
        SRCTMP = FLG[:, 2 * T:3 * T].bitcast(I32)
        PRE = SCR[:, 0:1024].rearrange("p (r j d) -> p r j d", r=2, j=QUAD)
        EA = SCR[:, 1024:3072].rearrange("p (r j e) -> p r j e", r=RING, j=QUAD)
        ATP = PB[3][:, 0:P]
        AEP = PB[3][:, P:2 * P]
        HISTP = PB[2][:, 0:NS]

        def registers(eng, row, q, most):
            _, values = nc.values_load_multi_w_load_instructions(
                row[0:1, bass.ds(q * QUAD, QUAD)], engines=[eng.engine], min_val=0, max_val=most,
                skip_runtime_bounds_check_because=reg_note)
            return values

        def pool_gathers(pool, n, rows, table):
            s = ps[n]

            def step(i, u):
                q, slot, turn, _ = at(i, u, 0)
                pool.wait_ge(s["idx_filled"][slot], (turn + 1) * 16)
                wait(pool, rows_read[n], q - RING + 1)
                if n == 0:
                    wait(pool, mv_stored[slot], turn * 16)
                pool.sem_inc(may_gather, 1)
                for j in range(QUAD):
                    nc.gpsimd.indirect_dma_start(
                        out=rows[:, slot, j, :], out_offset=None, in_=table,
                        in_offset=bass.IndirectOffsetOnAxis(ap=ISLOT[:, slot, j:j + 1], axis=0),
                    ).then_inc(s["gathered"][slot], 16)
            steps(pool, step, 0)

        @block.gpsimd
        def _(pool):
            nc.gpsimd.memset(ident[:, :], 0.0).then_inc(consts, 1)
            pool.wait_ge(consts, 1)
            nc.gpsimd.affine_select(out=ident[:, :], in_=ident[:, :], compare_op=ALU.not_equal, fill=1.0,
                                    base=0, pattern=[[-1, P]], channel_multiplier=1)
            nc.gpsimd.iota(iotaI, pattern=[[1, P]], base=0, channel_multiplier=0)
            nc.gpsimd.iota(thrI, pattern=[[P, NE]], base=0, channel_multiplier=0)
            nc.gpsimd.iota(pI, pattern=[[0, 1]], base=0, channel_multiplier=1)
            nc.gpsimd.iota(cI, pattern=[[8, NC]], base=0, channel_multiplier=0).then_inc(c_ready, 1)
            pool.wait_ge(windows_known, 1)
            pool.sem_inc(may_gather, 1)
            for c in range(NC):
                for src, dst in ((a["src_win"], SRCW), (a["dst_win"], DSTW)):
                    nc.gpsimd.indirect_dma_start(
                        out=dst[:, c, :], out_offset=None, in_=src,
                        in_offset=bass.IndirectOffsetOnAxis(ap=wI[:, c:c + 1], axis=0)).then_inc(windows_in, 16)
            for r in range(2):
                pool.wait_ge(proj[0]["stored"][r], 16 * NS // 2)
            pool_gathers(pool, 0, G2, tab2)

            pool.wait_ge(table_out, 16)
            pool_gathers(pool, 2, G1, tab1)
            for r in range(2):
                pool.wait_ge(proj[2]["stored"][r], 16 * NS // 2)
            pool_gathers(pool, 3, G2, tab2)
            pool.wait_ge(table_out, 32)
            pool_gathers(pool, 4, G1, tab1)

        def sp_edges(sp, n):
            s = ps[n]

            def step(i, u):
                q, slot, turn, _ = at(i, u, 0)
                wait(sp, s["gathered"][slot], turn * 64)
                sp.dma_start(ISLOT[:, slot, :], SRC[:, bass.ds(q * QUAD, QUAD)]).then_inc(s["idx_filled"][slot], 16)
                if n == 3:
                    wait(sp, gated["pre_done"], q - RING + 1)
                    for j, first in enumerate(registers(sp, SROW, q, sz.edge_end)):
                        sp.dma_start(EA[:, slot, j, :], a["ea_t"][:, bass.ds(first, P)]).then_inc(ea_loaded[slot], 16)
            steps(sp, step, 0)

        def sp_layer0(sp):
            s = ps[0]

            def step(i, u, scores, messages):
                q, slot, turn, _ = at(i, u, 0)
                if scores:
                    wait(sp, s["gathered"][slot], turn * 64)
                    if not isinstance(q, int) or RING <= q < NQ + RING:
                        sp.sem_inc(may_move, 1)
                        sp.dma_start(mvd[bass.ds(q - RING, 1), :, :].rearrange("o p (j d) -> (o p) j d", j=QUAD),
                                     G2[:, slot, :, D:2 * D]).then_inc(mv_stored[slot], 16)
                    if valid(q):
                        sp.dma_start(ISLOT[:, slot, :], SRC[:, bass.ds(q * QUAD, QUAD)]).then_inc(s["idx_filled"][slot], 16)
                if messages:
                    q, slot, turn, _ = at(i - LAG, u, 0)
                    if valid(q):
                        sp.wait_ge(mv_stored[slot], (turn + 1) * 16)
                        sp.sem_inc(may_move, 1)
                        wait(sp, weighted["weighted"], q - RING + 1)
                        sp.sem_inc(may_move, 1)
                        sp.dma_start(MV[:, slot, :, :].rearrange("p j d -> p (j d)"),
                                     mvd[bass.ds(q, 1), :, :].rearrange("o p f -> (o p) f")).then_inc(mv_loaded[slot], 16)

            def guarded(i, u, scores, messages):
                step(i, u, scores and not (isinstance(i, int) and i == sz.iters and u >= RING), messages)
            layer0_steps(sp, guarded)

        def row_bc(v, n):
            return v.rearrange("(o n) -> o n", o=1).to_broadcast([P, n])

        @block.sync
        def _(sp):
            sp.dma_start(DSTI, a["dst_pm"]).then_inc(dst_loaded, 16)
            sp.dma_start(X[:, :, :], a["x"].rearrange("(b p) d -> p b d", p=P)).then_inc(x_loaded, 16)
            loads = [
                (WKT, a["wk_t"].rearrange("t m i -> m t i")), (WVT, a["wv_t"].rearrange("t m i -> m t i")),
                (W3[:, :, 2 * D:3 * D], a["wq"].rearrange("t i o -> i t o")),
                (ATTB, a["att"]), (MSGB, a["msg"]), (FILMW, a["film_w"]),
                (CTXC, a["ctx"].rearrange("(c o) -> c o", o=1)), (NTI, a["ntype"]),
                (SKIP[:, 0:3], row_bc(a["skip"], 3)), (PRI8, row_bc(a["pri"], HEADS)),
                (ROWS[:, 1, :], row_bc(a["ln_g"], D)), (ROWS[:, 2, :], row_bc(a["ln_b"], D)),
                (ROWS[:, 3:5, :].rearrange("p a d -> p (a d)"), row_bc(a["film_b"], 2 * D)),
            ]
            with nc.allow_non_contiguous_dma(reason="columns of a few words"):
                for dst, src in loads:
                    sp.dma_start(dst, src).then_inc(w_loaded, 16)
                sp.wait_ge(tiles_masked, 1)
                sp.dma_start(keyd.rearrange("(c p) e -> p c e", p=P), KEYW).then_inc(keys_stored, 16)
                sp.dma_start(metad[0, :].rearrange("(c p) -> p c", p=P), bI).then_inc(keys_stored, 16)
                sp.dma_start(metad[1, :].rearrange("(c p) -> p c", p=P), sI).then_inc(keys_stored, 16)
                sp.wait_ge(keys_stored, 48)
                sp.dma_start(BROW[:, :], metad[0:1, :]).then_inc(rows_in, 16)
                keyk = keyd.rearrange("(m g t) e -> m t g e", m=PARTS, t=GROUP)
                for m in range(PARTS):
                    for h in range(HEADS):
                        sp.dma_start(KEY[h:P:HEADS, m, 1:1 + sz.span].rearrange("t (g e) -> t g e", e=P),
                                     keyk[m]).then_inc(keys_in, 16)
                        sp.dma_start(KEY[HEADS + h:P:HEADS, m, 0:1], keyk[m, 0:GROUP - 1, sz.chunk - 1, P - 1:P]).then_inc(keys_in, 16)
                        sp.dma_start(KEY[h:P - HEADS:HEADS, m, fw - 1:fw], keyk[m, 1:GROUP, 0, 0:1]).then_inc(keys_in, 16)
                        if m:
                            sp.dma_start(KEY[h:h + 1, m, 0:1], keyk[m - 1, GROUP - 1:GROUP, sz.chunk - 1, P - 1:P]).then_inc(keys_in, 16)
                    if m:
                        sp.dma_start(LASTK[0:1, m:m + 1], keyk[m - 1, GROUP - 1:GROUP, sz.chunk - 1, P - 1:P]).then_inc(keys_in, 16)
            sp_proj(sp, 0)
            sp_layer0(sp)
            sp.wait_ge(w_free, 1)
            sp.dma_start(WA, a["wa"].rearrange("t i o -> i t o")).then_inc(w_next, 16)
            sp.dma_start(SRCPM, a["src_pm"]).then_inc(hist_in, 16)
            sp.wait_ge(table_made, 1)
            sp.dma_start(tab1.rearrange("(b p) d -> p b d", p=P), H[:, :, :]).then_inc(table_out, 16)
            sp.dma_start(ROWS[:, 0, :], row_bc(a["b_root"], D)).then_inc(w_next, 16)
            for k, name in enumerate(("w_src", "w_msg", "w_dst", "w_root", "w_edge")):
                sp.dma_start(W[:, k * D:(k + 1) * D], a[name]).then_inc(w_next, 16)
            sp_edges(sp, 2)
            sp.wait_ge(hist_ready, NQ)
            sp.dma_start(SROW, metad[1:2, :]).then_inc(srow_in, 16)
            sp.wait_ge(srow_in, 16)
            sp_proj(sp, 2)
            sp_edges(sp, 3)
            sp.wait_ge(table_made, 2)
            sp.dma_start(tab1.rearrange("(b p) d -> p b d", p=P), H[:, :, :]).then_inc(table_out, 16)
            for k, name in enumerate(("w_l", "w_r")):
                sp.dma_start(W[:, k * D:(k + 1) * D], a[name]).then_inc(w_next, 16)
            for k, name in enumerate(("b_l", "gamma", "beta")):
                sp.dma_start(ROWS[:, k, :], row_bc(a[name], D)).then_inc(w_next, 16)
            sp_edges(sp, 4)
            sp.wait_ge(x_final, 1)
            whole = sz.nodes // P
            left = sz.nodes - whole * P
            sp.dma_start(a["out"][0:whole * P, :].rearrange("(b p) d -> p b d", p=P), X[:, 0:whole, :]).then_inc(out_stored, 16)
            if left:
                sp.dma_start(a["out"][whole * P:sz.nodes, :], X[0:left, whole, :]).then_inc(out_stored, 16)
            sp.wait_ge(out_stored, 32 if left else 16)

        def bf_view(slot, j):
            return S[:, slot, j, :].bitcast(BF16)[:, 1::2]

        def pe_turn_onehot(pe, s, onehot, q, slot, par, banks):
            pe.wait_ge(onehot, q + 1)
            wait(pe, s["st_copied"], q + 1 - banks)
            for j in range(QUAD):
                last = nc.tensor.transpose(STP[par][:, j, :], bf_view(slot, j), identb[:, :])
            last.then_inc(s["st_turned"], 1)

        def pe_agg(pe, n, q, slot, par, rhs, width):
            s = ps[n]
            pe.wait_ge(s["onehot_ready"], q + 1)
            wait(pe, s["rows_added"], (q - 1) * QUAD)
            for j in range(QUAD):
                last = nc.tensor.matmul(PSA[:, par, j, 0:width], S[:, slot, j, :], rhs(j), start=True, stop=True)
            last.then_inc(s["agg_done"], 1)

        def pe_plain(pe, n):
            s = ps[n]

            def step(i, u):
                q, slot, turn, v = at(i, u, 0)
                if n == 2:
                    pe.wait_ge(hist_ready, q + 1)
                    for j in range(QUAD):
                        first = isinstance(q, int) and q == 0 and j == 0
                        final = isinstance(q, int) and q == NQ - 1 and j == QUAD - 1
                        nc.tensor.matmul(HISTP, LOH[:, slot, j, :], HIH[:, slot, j, :], start=first, stop=final,
                                         skip_group_check=True)
                pe.wait_ge(s["gathered"][slot], (turn + 1) * 64)
                pe_agg(pe, n, q, slot, v % 2, lambda j: G1[:, slot, j, :], D)
            steps(pe, step, 0)

        @block.tensor
        def _(pe):
            pe.wait_ge(counted, NE + 1)
            nc.tensor.matmul(PB[0][:, 0:NE], ones, cnt, start=True, stop=True).then_inc(totals, 1)
            pe.wait_ge(w_loaded, 16 * 13)
            for t in range(TYPES):
                nc.tensor.matmul(PB[1][:, t * D:(t + 1) * D], WKT[:, t, :], ATTB, start=True, stop=True)
                nc.tensor.matmul(PB[2][:, t * D:(t + 1) * D], WVT[:, t, :], MSGB, start=True, stop=True)
            pe.wait_ge(film_in, 1)
            nc.tensor.matmul(PB[3][:, 0:2 * D], CTXB, FILMW, start=True, stop=True).then_inc(w_combined, 1)
            pe.wait_ge(tiles_masked, 1)
            for c in range(NC):
                for k, f in enumerate((RELF, SRCF)):
                    last = nc.tensor.transpose(PB[2 * k + c // 4][:, (c % 4) * P:(c % 4 + 1) * P], f[:, c, :], ident[:, :])
            last.then_inc(tiles_turned, 1)
            pe_proj(pe, 0)

            pe.wait_ge(rows_in, 16)
            s = scored

            w = weighted
            hops = [0]

            def hop(lhs, rhs, dst):
                hops[0] += 1
                pe.wait_ge(hop_in, hops[0])
                nc.tensor.matmul(dst, lhs, rhs, start=True, stop=True).then_inc(hop_out, 1)

            def carries(m):
                pe.wait_ge(s["grp_copied"], min((m + 1) * sz.chunk + 1, sz.groups))
                wait(pe, w["grp_copied"], m * sz.chunk)
                for _ in range(2):
                    for _ in range(2):
                        hop(small[:, 0:1], ident[:, :], HOP[0:1, :])
                    hop(CLINE(3), small[0:1, 3:4], HOP[:, 0:1])
                if m:
                    hop(small[:, 0:1], ident[:, :], HOP[0:1, :])
                pe.wait_ge(exp_in, m + 1)

            def step(i, u, scores, messages):
                q, slot, turn, v = at(i, u, 0)
                if scores and valid(q):
                    pe_turn_onehot(pe, s, ps[0]["onehot_ready"], q, v % 2, 0, 1)
                q, slot, turn, v = at(i, u, -1)
                if scores and valid(q):
                    pe.wait_ge(s["st_copied"], q + 1)
                    wait(pe, s["multiplied"], q - 1)
                    blocks = registers(pe, BROW, q, NB)
                    for j in range(QUAD):
                        last = nc.tensor.matmul(QD[v % 2][:, j, :], ST[:, v % 2, j, :],
                                                QT[:, bass.ds(blocks[j], 1), :].rearrange("p o d -> p (o d)"), start=True, stop=True)
                    last.then_inc(s["q_spread"], 1)
                q, slot, turn, v = at(i, u, -3)
                if scores and valid(q) and v % 4 == 3:
                    pe.wait_ge(s["reduced"], q + 1)
                    g = group_of(i, u, -3)
                    wait(pe, s["grp_copied"], g)
                    if messages:
                        wait(pe, w["grp_copied"], (i - LAG) * 2 + (1 if u == 2 else 2))
                    nc.tensor.transpose(ATP, ABUF[:, (v // 4) % 2, :], ident[:, :]).then_inc(s["grp_turned"], 1)
                q, slot, turn, v = at(i - LAG, u, 0)
                if isinstance(i, int) and i in hooks[1:] and u == 4:
                    pe.wait_ge(rescaled, hooks.index(i))
                if messages and valid(q) and v % 4 == 0:
                    g = group_of(i - LAG, u, 0)
                    pe.wait_ge(w["grp_staged"], g + 1)
                    wait(pe, w["grp_copied"], g)
                    if scores and not (isinstance(i, int) and i == sz.iters and u):
                        wait(pe, s["grp_copied"], i * 2 - 1 + (u > 0))
                    else:
                        wait(pe, s["grp_copied"], sz.groups)
                    nc.tensor.transpose(AEP, ATS[:, (v // 4) % 2, :], ident[:, :]).then_inc(w["grp_turned"], 1)
                q, slot, turn, v = at(i - LAG, u, -3)
                if messages and valid(q):
                    pe.wait_ge(w["weighted"], q + 1)
                    pe_agg(pe, 1, q, 2 + v % 2, v % 2, lambda j: WM[:, v % 2, j, :], WMW)
                if isinstance(i, int) and i in hooks[1:] and u == 3:
                    pe.wait_ge(w["grp_copied"], hooks.index(i) * sz.chunk + 1)
                    pe.wait_ge(s["grp_copied"], min(i * 2, sz.groups))
                    hop(CLINE(5), CLINE(4)[:, 24:24 + HEADS], HOP[:, 0:HEADS])
            layer0_steps(pe, step, carries)
            pe_proj(pe, 1)
            pe_plain(pe, 2)
            pe_proj(pe, 2)

            s = gated

            def step(i, u):
                q, slot, turn, v = at(i, u, -1)
                if valid(q):
                    blocks = registers(pe, BROW, q, NB)
                    pe.wait_ge(ea_loaded[slot], (turn + 1) * 64)
                    wait(pe, s["summed"], q - 1)
                    for j in range(QUAD):
                        nc.tensor.matmul(QD[v % 2][:, j, :], EA[:, slot, j, :], W[:, 4 * D:5 * D], start=j == 0, stop=False,
                                         skip_group_check=True)
                    pe.wait_ge(s["st_copied"], q + 1)
                    for j in range(QUAD):
                        last = nc.tensor.matmul(QD[v % 2][:, j, :], ST[:, v % 2, j, :],
                                                QT[:, bass.ds(blocks[j], 1), :].rearrange("p o d -> p (o d)"), start=False, stop=True,
                                                skip_group_check=True)
                    last.then_inc(s["pre_done"], 1)
                q, slot, turn, v = at(i, u, -3)
                if valid(q):
                    pe.wait_ge(s["multiplied"], q + 1)
                    pe_agg(pe, 3, q, slot, v % 2, lambda j: RHS[:, v % 2, j, :], 2 * D)
                q, slot, turn, v = at(i, u, 0)
                if valid(q):
                    pe_turn_onehot(pe, s, ps[3]["onehot_ready"], q, slot, v % 2, 2)
            steps(pe, step, 3)
            pe_plain(pe, 4)
            pe_proj(pe, 3)

        def act_copy_onehot(act, s, q, par, used, bank):
            act.wait_ge(s["st_turned"], q + 1)
            wait(act, used, q - 1)
            nc.scalar.copy(ST[:, par, :, :], STP[bank]).then_inc(s["st_copied"], 1)

        @block.scalar
        def _(act):
            turn_no = [0]

            roots = [0]

            def root(t):
                roots[0] += 1
                act.wait_ge(root_in, roots[0])
                nc.scalar.activation(t[:, :], t[:, :], ACT.Sqrt).then_inc(root_out, 1)

            def square():
                turn_no[0] += 1
                act.wait_ge(centred, turn_no[0])
                src = QT if turn_no[0] in (2, 6) else H
                nc.scalar.activation(WIDE, src[:, :, :], ACT.Square).then_inc(squared, 1)
                root(st2)

            act.wait_ge(sig_in, 1)
            nc.scalar.activation(SIG[:, 0:3], SKIP[:, 0:3], ACT.Sigmoid).then_inc(sig_out, 1)
            square()
            act_proj(act, 0)
            s, w = scored, weighted

            def exponentials(m):
                act.wait_ge(exp_in, m + 1)
                nc.scalar.activation(AT[:, m % 2, :, :], FMAX.rearrange("p (g e) -> p g e", e=P), ACT.Exp).then_inc(exp_out, 1)
                act.wait_ge(exp_out, m + 1)
                if m:
                    act.wait_ge(scale_in, m)
                    nc.scalar.activation(CLINE(4)[:, 24:24 + HEADS], CLINE(4)[:, 16:16 + HEADS], ACT.Exp).then_inc(scale_out, 1)

            def ring_group(g):
                flat = AT.rearrange("p r g e -> p (r g e)")
                return flat[:, bass.ds((g % (2 * sz.chunk)) * P, P)]

            def step(i, u, scores, messages):
                q, slot, turn, v = at(i - LAG, u, -1)
                if messages and valid(q) and v % 4 == 0:
                    act.wait_ge(w["grp_turned"], group_of(i - LAG, u, -1) + 1)
                    wait(act, w["weighted"], q - QUAD)
                    nc.scalar.copy(AE[:, (v // 4) % 2, :], AEP).then_inc(w["grp_copied"], 1)
                q, slot, turn, v = at(i - LAG, u, -2)
                if messages and valid(q):
                    wait(act, ps[1]["agg_done"], q - 1)
                    wait(act, w["grp_copied"], group_of(i - LAG, u, -2) + 1)
                    nc.scalar.copy(WM[:, v % 2, :, D:D + HEADS],
                                   AE[:, (v // 4) % 2, (v % 4) * 32:(v % 4) * 32 + 32].rearrange("p (j h) -> p j h", j=QUAD)
                                   ).then_inc(w["prob_put"], 1)
                q, slot, turn, v = at(i, u, 0)
                if scores and valid(q):
                    act_copy_onehot(act, s, q, v % 2, s["q_spread"], 0)
                q, slot, turn, v = at(i, u, -3)
                if scores and valid(q) and v % 4 == 3:
                    g = group_of(i, u, -3)
                    act.wait_ge(s["grp_turned"], g + 1)
                    nc.scalar.copy(ring_group(g), ATP).then_inc(s["grp_copied"], 1)
                q, slot, turn, v = at(i - LAG, u, 0)
                if messages and valid(q) and v % 4 == 0:
                    g = group_of(i - LAG, u, 0)
                    wait(act, w["grp_turned"], g - 1)
                    nc.scalar.copy(ATS[:, (v // 4) % 2, :], ring_group(g)).then_inc(w["grp_staged"], 1)
            layer0_steps(act, step, exponentials)
            act_proj(act, 1)
            square()
            square()
            root(st1)
            root(OUTDEG)
            square()
            act_proj(act, 2)
            s = gated

            def step(i, u):
                q, slot, turn, v = at(i, u, 0)
                if valid(q):
                    act_copy_onehot(act, s, q, v % 2, s["pre_done"], v % 2)
                q, slot, turn, v = at(i, u, -2)
                if valid(q):
                    act.wait_ge(s["summed"], q + 1)
                    wait(act, ps[3]["agg_done"], q - 1)
                    nc.scalar.activation(RHS[:, v % 2, :, D:2 * D], PRE[:, v % 2, :, :], ACT.Sigmoid).then_inc(s["gate_done"], 1)
            steps(act, step, 2)
            square()
            act_proj(act, 3)
            square()
            act.wait_ge(gelu_in, 1)
            nc.scalar.activation(QT, QT, ACT.Gelu).then_inc(gelu_out, 1)

        def plain(dve, n, onehot, row_adder):
            def step(i, u):
                q, slot, turn, v = at(i, u, -2)
                add = row_adder(n, acc1, D, q, v % 2)
                add(0)
                q, slot, turn, v = at(i, u, 0)
                if valid(q):
                    onehot(n, q, slot)
                add(1)
                if valid(q) and n == 2:
                    cols = bass.ds(q * QUAD, QUAD)
                    nc.vector.tensor_tensor(LOH[:, slot, :, :], bc(iota[:, :], [P, QUAD, P], 1),
                                            LO[:, cols].unsqueeze(2).to_broadcast([P, QUAD, P]), ALU.is_equal)
                add(2)
                if valid(q) and n == 2:
                    nc.vector.tensor_tensor(HIH[:, slot, :, :], bc(iota[:, 0:NS], [P, QUAD, NS], 1),
                                            HI[:, cols].unsqueeze(2).to_broadcast([P, QUAD, NS]), ALU.is_equal
                                            ).then_inc(hist_ready, 1)
                add(3)
            steps(dve, step, 2)
            dve.wait_ge(ps[n]["rows_added"], T)

        @block.vector
        def _(dve):
            c = Chain(dve, dve_done)
            v_ = nc.vector

            def onehot(n, q, slot):
                if n == 0:
                    wait(dve, scored["st_turned"], q - 1)
                elif n == 1:
                    wait(dve, ps[1]["agg_done"], q - 1)
                else:
                    wait(dve, ps[n]["agg_done"], q - RING + 1)
                return v_.tensor_tensor(S[:, slot, :, :], bc(iota[:, :], [P, QUAD, P], 1),
                                        REL[:, bass.ds(q * QUAD, QUAD)].unsqueeze(2).to_broadcast([P, QUAD, P]),
                                        ALU.is_equal).then_inc(ps[n]["onehot_ready"], 1)

            def row_adder(n, acc, width, q, par, on=True):
                s = ps[n]
                if not (on and valid(q)):
                    return lambda j: None
                blocks = registers(dve, BROW, q, NB)

                def add(j):
                    rows = acc[:, bass.ds(blocks[j], 1), :].rearrange("p o d -> p (o d)")
                    if j == 0:
                        dve.wait_ge(s["agg_done"], q + 1)
                    wait(dve, s["rows_added"], q * QUAD + j)
                    v_.tensor_tensor(rows, rows, PSA[:, par, j, 0:width], ALU.add).then_inc(s["rows_added"], 1)
                return add

            def layer_norm(src, dst):
                c(v_.tensor_reduce(st1[:, :], src[:, :, :], AX.X, ALU.add))
                c(v_.tensor_scalar(st1[:, :], st1[:, :], -1.0 / D, None, ALU.mult))
                c(v_.tensor_tensor(dst[:, :, :], src[:, :, :], st1[:, :].unsqueeze(2).to_broadcast([P, NS, D]), ALU.add))
                dve.sem_inc(centred, 1)
                norms[0] += 1
                dve.wait_ge(squared, norms[0])
                c(v_.tensor_reduce(st2[:, :], WIDE, AX.X, ALU.add))
                c(v_.tensor_scalar(st2[:, :], st2[:, :], 1.0 / D, EPS, ALU.mult, ALU.add))
                root(st2)

            norms, roots = [0], [0]
            node = [P, NS, D]

            def root(t):
                dve.sem_inc(root_in, 1)
                roots[0] += 1
                dve.wait_ge(root_out, roots[0])
                c(v_.reciprocal(t[:, :], t[:, :]))

            def relu_scaled(dst):
                c(v_.scalar_tensor_tensor(dst[:, :, :], dst[:, :, :], 0.0, st2[:, :].unsqueeze(2).to_broadcast(node),
                                          ALU.max, ALU.mult))

            def over(ap):
                return ap.unsqueeze(2).to_broadcast(node)

            def vec(k):
                return bc(ROWS[:, k, :], node, 1)

            dve.wait_ge(c_ready, 1)
            c(v_.tensor_copy(iota[:, :], iotaI))
            c(v_.tensor_copy(thr, thrI))
            c(v_.tensor_copy(identb[:, :], ident[:, :]))
            c(v_.memset(ones, 1.0))
            c(v_.memset(zer, 0.0))
            c(v_.memset(small[:, :], 1.0))
            c(v_.memset(cnt, 0.0))
            c(v_.memset(cum, 0.0))
            dve.wait_ge(dst_loaded, 16)
            v_.tensor_copy(DSTF, DSTI).then_inc(counted, 1)
            with dve.Fori(0, NE) as b:
                dve.wait_ge(counted, b + 1)
                v_.tensor_scalar(JUNK, DSTF, thr[:, bass.ds(b, 1)], 0.0, ALU.is_lt, ALU.add,
                                 accum_out=cnt[:, bass.ds(b, 1)]).then_inc(counted, 1)
            dve.wait_ge(totals, 1)
            c(v_.tensor_copy(bf, PB[0][:, 0:NE]))
            c(v_.tensor_copy(bi, bf))
            c(v_.tensor_scalar(bi, bi, 4, 4, ALU.logical_shift_right, ALU.logical_shift_left))
            c(v_.tensor_copy(b16f, bi))
            c(v_.tensor_tensor(tiles_f[:, 0:NB], bf[:, 1:NE], b16f[:, 0:NB], ALU.subtract))
            c(v_.tensor_scalar(tiles_f[:, 0:NB], tiles_f[:, 0:NB], float(P - 1), None, ALU.add))
            c(v_.tensor_copy(ti32[:, 0:NB], tiles_f[:, 0:NB]))
            c(v_.tensor_scalar(ti32[:, 0:NB], ti32[:, 0:NB], 7, None, ALU.logical_shift_right))
            c(v_.tensor_copy(tiles_f[:, 0:NB], ti32[:, 0:NB]))
            c(v_.tensor_tensor_scan(cum[:, 1:NE], tiles_f[:, 0:NB], zer[:, 0:NB], 0.0, ALU.add, ALU.add))
            c(v_.scalar_tensor_tensor(rel0, cum, -float(P), b16f, ALU.mult, ALU.add))
            c(v_.tensor_copy(delta[:, 0:1], rel0[:, 0:1]))
            c(v_.tensor_tensor(delta[:, 1:NE], rel0[:, 1:NE], rel0[:, 0:NE - 1], ALU.subtract))
            c(v_.tensor_scalar(p15, pI, GROUP - 1, None, ALU.bitwise_and))
            c(v_.tensor_scalar(p4, pI, 4, None, ALU.logical_shift_right))
            c(v_.tensor_copy(p15f, p15))
            c(v_.tensor_copy(p4f, p4))
            c(v_.tensor_copy(cF, cI))
            c(v_.tensor_scalar(cF, cF, p4f, None, ALU.add))
            c(v_.tensor_scalar(tp, p15f, float(sz.chunk), None, ALU.mult))
            c(v_.tensor_scalar(tpos, cF, tp, None, ALU.add))
            for m in range(1, PARTS):
                c(v_.tensor_scalar(off, cF, float(m * sz.chunk), float((GROUP - 1) * sz.chunk), ALU.is_ge, ALU.mult))
                c(v_.tensor_tensor(tpos, tpos, off, ALU.add))
            c(v_.tensor_tensor(M, bc(cum, [P, NC, NE], 1), tpos.unsqueeze(2).to_broadcast([P, NC, NE]), ALU.is_le))
            c(v_.tensor_reduce(bt, M, AX.X, ALU.add))
            c(v_.tensor_scalar(bt, bt, -1.0, None, ALU.add))
            c(v_.tensor_tensor(MD, M, bc(delta, [P, NC, NE], 1), ALU.mult))
            c(v_.tensor_reduce(st, MD, AX.X, ALU.add))
            c(v_.scalar_tensor_tensor(st, tpos, float(P), st, ALU.mult, ALU.add))
            c(v_.tensor_scalar(st, st, float(sz.edge_end), None, ALU.min))
            c(v_.tensor_copy(bI, bt))
            c(v_.tensor_copy(sI, st))
            c(v_.tensor_scalar(wI, sI, 4, None, ALU.logical_shift_right))
            dve.sem_inc(windows_known, 1)
            c(v_.tensor_scalar(off, bt, -float(P), None, ALU.mult))
            dve.wait_ge(w_loaded, 16 * 13)
            dve.sem_inc(sig_in, 1)
            c(v_.tensor_copy(CTXB, CTXC.to_broadcast([CTX, P])))
            dve.sem_inc(film_in, 1)
            ntf = st1
            c(v_.tensor_copy(ntf[:, :], NTI))
            dve.wait_ge(sig_out, 1)
            c(v_.memset(ALPHA[:, :], 0.0))
            for t in range(TYPES):
                c(v_.tensor_scalar(MASK[:, :, t], ntf[:, :], float(t), None, ALU.is_equal))
                c(v_.scalar_tensor_tensor(ALPHA[:, :], MASK[:, :, t], SIG[:, t:t + 1], ALPHA[:, :], ALU.mult, ALU.add))
            c(v_.tensor_scalar(PRI.rearrange("p (h d) -> p h d", h=HEADS), PRI8.unsqueeze(2).to_broadcast([P, HEADS, DH]),
                               float(DH) ** -0.5, None, ALU.mult))
            dve.wait_ge(w_combined, 1)
            c(v_.tensor_copy(W3[:, :, 0:D], PB[1][:, 0:3 * D].rearrange("p (t d) -> p t d", t=3)))
            c(v_.tensor_copy(W3[:, :, D:2 * D], PB[2][:, 0:3 * D].rearrange("p (t d) -> p t d", t=3)))
            c(v_.tensor_tensor(ROWS[:, 3:5, :].rearrange("p a d -> p (a d)"), ROWS[:, 3:5, :].rearrange("p a d -> p (a d)"),
                               PB[3][:, 0:2 * D], ALU.add))
            dve.wait_ge(windows_in, 32 * NC)
            c(v_.tensor_copy(SRCF, SRCW))
            c(v_.tensor_copy(DKF, DSTW))
            c(v_.tensor_tensor(RELF, DKF, off.unsqueeze(2).to_broadcast([P, NC, P]), ALU.add))
            c(v_.tensor_scalar(VAL, RELF, 0.0, None, ALU.is_ge))
            c(v_.scalar_tensor_tensor(VAL, RELF, float(P), VAL, ALU.is_lt, ALU.mult))
            c(v_.scalar_tensor_tensor(KEYW, DKF, 1.0, VAL, ALU.add, ALU.mult))
            c(v_.tensor_scalar(KEYW, KEYW, -1.0, None, ALU.add))
            c(v_.memset(KEY[:, :, 0:1], -2.0))
            c(v_.memset(KEY[:, :, sz.span + 1:sz.span + 2], -3.0))
            dve.sem_inc(tiles_masked, 1)
            dve.wait_ge(tiles_turned, 1)
            for k, dst in enumerate((REL, SRC)):
                for h in range(-(-NC // 4)):
                    n = min(4, NC - 4 * h) * P
                    c(v_.tensor_copy(dst[:, 4 * h * P:4 * h * P + n], PB[2 * k + h][:, 0:n]))
            dve.wait_ge(keys_in, 16 * keys_dmas)
            c(v_.tensor_tensor(KEY[:, :, 0:fw - 1], KEY[:, :, 1:fw], KEY[:, :, 0:fw - 1], ALU.not_equal))
            c(v_.tensor_scalar(flags[:, :, 0:fw - 1], KEY[:, :, 0:fw - 1], NEG, None, ALU.mult))

            dve.wait_ge(x_loaded, 16)
            layer_norm(X, H)
            relu_scaled(H)
            dve_proj(dve, 0)
            s, w = scored, weighted
            c(v_.memset(acc0, 0.0))
            c(v_.memset(WM[:, :, :, D + HEADS:D + HEADS + 1], 1.0))
            hops = [0]

            def hop():
                dve.sem_inc(hop_in, 1)
                hops[0] += 1
                dve.wait_ge(hop_out, hops[0])

            def to_row(column, dst):
                c(v_.tensor_copy(small[:, 0:1], column))
                hop()
                c(v_.tensor_copy(dst, HOP[0:1, :].rearrange("o (t h) -> o h t", h=HEADS)))

            hc = lambda r: CLINE(r).rearrange("o (h t) -> o h t", h=HEADS)
            th = lambda r: CLINE(r).rearrange("o (t h) -> o h t", h=HEADS)
            carry = CLINE(4)[:, 0:HEADS].unsqueeze(2)
            before = CLINE(4)[:, 8:8 + HEADS]
            shift = CLINE(4)[:, 16:16 + HEADS]
            c(v_.memset(CLINE(4), 2 * NEG))

            def maxima(m):
                dve.wait_ge(s["grp_copied"], (m + 1) * sz.chunk)
                wait(dve, exp_out, m)
                at_m = AT[:, m % 2, :, :].rearrange("p g e -> p (g e)")
                ahead, behind = flags[:, m, 0:sz.span], flags[:, m, 1:sz.span + 1]
                c(v_.tensor_tensor_scan(FMAX, ahead, at_m, 2 * NEG, ALU.add, ALU.max))
                to_row(FMAX[:, sz.span - 1:sz.span], hc(0))
                c(v_.tensor_reduce(small[:, 1:2], ahead, AX.X, ALU.min))
                to_row(small[:, 1:2], hc(1))
                c(v_.tensor_copy(before, carry.rearrange("o h x -> o (h x)")))
                c(v_.tensor_tensor(hc(1)[:, :, 0:1], hc(1)[:, :, 0:1], carry, ALU.add))
                c(v_.tensor_tensor(hc(0)[:, :, 0:1], hc(0)[:, :, 0:1], hc(1)[:, :, 0:1], ALU.max))
                c(v_.memset(hc(1)[:, :, 0:1], 2 * NEG))
                c(v_.tensor_tensor_scan(CLINE(2), CLINE(1), CLINE(0), 4 * NEG, ALU.add, ALU.max))
                c(v_.tensor_copy(th(3)[:, :, 1:GROUP], hc(2)[:, :, 0:GROUP - 1]))
                c(v_.tensor_copy(th(3)[:, :, 0:1], carry))
                c(v_.tensor_copy(carry, hc(2)[:, :, GROUP - 1:GROUP]))
                hop()
                c(v_.tensor_copy(small[:, 2:3], HOP[:, 0:1]))
                c(v_.tensor_tensor_scan(FMAX, ahead, FMAX, small[:, 2:3], ALU.add, ALU.max))
                fb, bb = FMAX[:, ::-1], behind[:, ::-1]
                c(v_.tensor_tensor_scan(fb, bb, fb, 2 * NEG, ALU.add, ALU.max))
                to_row(FMAX[:, 0:1], hc(0))
                c(v_.tensor_reduce(small[:, 1:2], behind, AX.X, ALU.min))
                to_row(small[:, 1:2], hc(1))
                c(v_.memset(hc(1)[:, :, GROUP - 1:GROUP], 2 * NEG))
                c(v_.tensor_tensor_scan(CLINE(2)[:, ::-1], CLINE(1)[:, ::-1], CLINE(0)[:, ::-1], 4 * NEG, ALU.add, ALU.max))
                c(v_.memset(CLINE(3), 2 * NEG))
                c(v_.tensor_copy(th(3)[:, :, 0:GROUP - 1], hc(2)[:, :, 1:GROUP]))
                hop()
                c(v_.tensor_copy(small[:, 2:3], HOP[:, 0:1]))
                c(v_.tensor_tensor_scan(fb, bb, fb, small[:, 2:3], ALU.add, ALU.max))
                if m:
                    to_row(FMAX[:, 0:1], hc(0))
                    c(v_.tensor_tensor(shift, before, hc(0)[:, :, 0:1].rearrange("o h x -> o (h x)"), ALU.subtract))
                    c(v_.tensor_scalar(CLINE(4)[:, 32:33], flags[0:1, m, 0:1], -1.0, None, ALU.is_ge))
                    c(v_.tensor_scalar(shift, shift, CLINE(4)[:, 32:33], None, ALU.mult))
                    dve.sem_inc(scale_in, 1)
                c(v_.tensor_tensor(FMAX, at_m, FMAX, ALU.subtract))
                dve.sem_inc(exp_in, 1)

            def rescale(m):
                k = m * sz.chunk * GROUP - 1
                block_col = BROW[0:1, k:k + 1]
                c(v_.tensor_copy(CLINE(4)[:, 33:34], block_col))
                c(v_.scalar_tensor_tensor(CLINE(4)[:, 34:35], CLINE(4)[:, 33:34], -float(P), LASTK[0:1, m:m + 1], ALU.mult, ALU.add))
                c(v_.tensor_scalar(CLINE(5), iota[0:1, :], CLINE(4)[:, 34:35], None, ALU.is_equal))
                dve.wait_ge(scale_out, m)
                c(v_.tensor_scalar(CLINE(4)[:, 24:24 + HEADS], CLINE(4)[:, 24:24 + HEADS], -1.0, None, ALU.add))
                hop()
                c(v_.tensor_scalar(small[:, 4:4 + HEADS], HOP[:, 0:HEADS], 1.0, None, ALU.add))
                b = nc.values_load(block_col, engines=[dve.engine], min_val=0, max_val=NB,
                                   skip_runtime_bounds_check_because=reg_note)
                row = acc0[:, bass.ds(b, 1), :].rearrange("p o d -> p (o d)")
                sums = row[:, 0:D].rearrange("p (h d) -> p h d", h=HEADS)
                c(v_.tensor_tensor(sums, sums, small[:, 4:4 + HEADS].unsqueeze(2).to_broadcast([P, HEADS, DH]), ALU.mult))
                c(v_.tensor_tensor(row[:, D:D + HEADS], row[:, D:D + HEADS], small[:, 4:4 + HEADS], ALU.mult))

            def step(i, u, scores, messages):
                q, slot, turn, v = at(i, u, 0)
                if scores and valid(q):
                    onehot(0, q, v % 2)
                q, slot, turn, v = at(i - LAG, u, -4)
                add = row_adder(1, acc0, WMW, q, v % 2, messages)
                add(0)
                qm, mslot, mturn, mv = at(i - LAG, u, -2)
                weigh = messages and valid(qm)
                if weigh:
                    onehot(1, qm, 2 + mv % 2)
                add(1)
                q, slot, turn, v = at(i, u, -2)
                score = scores and valid(q)
                if score:
                    dve.wait_ge(s["q_spread"], q + 1)
                    dve.wait_ge(ps[0]["gathered"][slot], (turn + 1) * 64)
                    wait(dve, s["reduced"], q - 1)
                    v_.tensor_tensor(PROD[:, v % 2, :, :], G2[:, slot, :, 0:D], QD[v % 2], ALU.mult).then_inc(s["multiplied"], 1)
                add(2)
                if weigh:
                    dve.wait_ge(mv_loaded[mslot], (mturn + 1) * 16)
                    dve.wait_ge(w["prob_put"], qm + 1)
                    wait(dve, ps[1]["agg_done"], qm - 1)
                    probs = AE[:, (mv // 4) % 2, (mv % 4) * 32:(mv % 4) * 32 + 32]
                    v_.tensor_tensor(
                        WM[:, mv % 2, :, 0:D].rearrange("p j (h d) -> p j h d", h=HEADS),
                        MV[:, mslot, :, :].rearrange("p j (h d) -> p j h d", h=HEADS),
                        probs.rearrange("p (j h) -> p j h", j=QUAD).unsqueeze(3).to_broadcast([P, QUAD, HEADS, DH]),
                        ALU.mult).then_inc(w["weighted"], 1)
                add(3)
                if score:
                    dve.wait_ge(s["multiplied"], q + 1)
                    if v % 4 == 0:
                        wait(dve, s["grp_turned"], group_of(i, u, -2) - 1)
                    v_.tensor_reduce(ABUF[:, (v // 4) % 2, (v % 4) * 32:(v % 4) * 32 + 32].rearrange("p (j h) -> p j h", j=QUAD),
                                     PROD[:, v % 2, :, :].rearrange("p j (h d) -> p j h d", h=HEADS), AX.X, ALU.add
                                     ).then_inc(s["reduced"], 1)
                if isinstance(i, int) and i in hooks[1:] and u == 3:
                    dve.wait_ge(ps[1]["rows_added"], hooks.index(i) * sz.chunk * GROUP)
                    rescale(hooks.index(i))
                    dve.sem_inc(rescaled, 1)
            layer0_steps(dve, step, maxima)
            dve.sem_inc(w_free, 1)
            dve.wait_ge(ps[1]["rows_added"], T)
            c(v_.tensor_copy(DEG[:, :], acc0[:, :, D + HEADS:D + HEADS + 1].rearrange("p b o -> p (b o)")))
            probs = acc0[:, :, D:D + HEADS]
            c(v_.tensor_scalar(probs, probs, 0.5, None, ALU.max))
            c(v_.reciprocal(probs, probs))
            for h in range(HEADS):
                c(v_.tensor_tensor(QT[:, :, h * DH:(h + 1) * DH], acc0[:, :, h * DH:(h + 1) * DH],
                                   acc0[:, :, D + h:D + h + 1].to_broadcast([P, NS, DH]), ALU.mult))
            dve.wait_ge(w_next, 16)
            dve_proj(dve, 1)
            c(v_.tensor_tensor(QT, QT, H[:, :, :], ALU.subtract))
            c(v_.tensor_tensor(QT, QT, over(ALPHA[:, :]), ALU.mult))
            c(v_.tensor_tensor(QT, QT, H[:, :, :], ALU.add))
            layer_norm(QT, QT)
            c(v_.tensor_tensor(QT, QT, over(st2[:, :]), ALU.mult))
            c(v_.tensor_tensor(QT, QT, vec(1), ALU.mult))
            c(v_.tensor_tensor(QT, QT, vec(2), ALU.add))
            c(v_.tensor_tensor(QT, QT, H[:, :, :], ALU.add))
            c(v_.tensor_tensor(QT, QT, vec(3), ALU.mult))
            c(v_.tensor_tensor(QT, QT, vec(4), ALU.add))
            c(v_.tensor_tensor(X[:, :, :], X[:, :, :], QT, ALU.add))

            layer_norm(X, H)
            relu_scaled(H)
            c(v_.tensor_scalar(st1[:, :], DEG[:, :], 1.0, 1.0, ALU.add, ALU.max))
            root(st1)
            c(v_.tensor_tensor(H[:, :, :], H[:, :, :], over(st1[:, :]), ALU.mult))
            dve.sem_inc(table_made, 1)
            c(v_.memset(acc1, 0.0))
            dve.wait_ge(hist_in, 16)
            c(v_.tensor_scalar(SRCTMP, SRCPM, P - 1, None, ALU.bitwise_and))
            c(v_.tensor_copy(LO, SRCTMP))
            c(v_.tensor_scalar(SRCTMP, SRCPM, 7, None, ALU.logical_shift_right))
            c(v_.tensor_copy(HI, SRCTMP))
            plain(dve, 2, onehot, row_adder)
            c(v_.tensor_scalar(OUTDEG[:, :], HISTP, 1.0, 1.0, ALU.add, ALU.max))
            root(OUTDEG)
            c(v_.tensor_tensor(acc1, acc1, H[:, :, :], ALU.add))
            c(v_.tensor_tensor(acc1, acc1, over(OUTDEG[:, :]), ALU.mult))
            c(v_.tensor_tensor(X[:, :, :], X[:, :, :], acc1, ALU.add))

            layer_norm(X, H)
            relu_scaled(H)
            dve.wait_ge(w_next, 16 * 7)
            dve_proj(dve, 2)
            c(v_.tensor_tensor(H[:, :, :], H[:, :, :], vec(0), ALU.add))
            c(v_.memset(acc2, 0.0))
            s = gated

            def step(i, u):
                q, slot, turn, v = at(i, u, -4)
                add = row_adder(3, acc2, 2 * D, q, v % 2)
                q, slot, turn, v = at(i, u, -3)
                if valid(q):
                    dve.wait_ge(s["gate_done"], q + 1)
                    v_.tensor_tensor(RHS[:, v % 2, :, 0:D], G2[:, slot, :, D:2 * D], RHS[:, v % 2, :, D:2 * D],
                                     ALU.mult).then_inc(s["multiplied"], 1)
                add(0)
                q, slot, turn, v = at(i, u, -2)
                if valid(q):
                    dve.wait_ge(s["pre_done"], q + 1)
                    dve.wait_ge(ps[3]["gathered"][slot], (turn + 1) * 64)
                    wait(dve, s["gate_done"], q - 1)
                    v_.tensor_tensor(PRE[:, v % 2, :, :], QD[v % 2], G2[:, slot, :, 0:D], ALU.add).then_inc(s["summed"], 1)
                add(1)
                q, slot, turn, v = at(i, u, 0)
                if valid(q):
                    onehot(3, q, slot)
                add(2)
                add(3)
            steps(dve, step, 4)
            dve.wait_ge(ps[3]["rows_added"], T)
            norm, summed = acc2[:, :, D:2 * D], acc2[:, :, 0:D]
            c(v_.tensor_scalar(norm, norm, 1e-6, None, ALU.max))
            c(v_.reciprocal(norm, norm))
            c(v_.tensor_tensor(summed, summed, norm, ALU.mult))
            c(v_.tensor_tensor(summed, summed, H[:, :, :], ALU.add))
            c(v_.tensor_tensor(X[:, :, :], X[:, :, :], summed, ALU.add))

            layer_norm(X, H)
            relu_scaled(H)
            dve.sem_inc(table_made, 1)
            c(v_.memset(acc1, 0.0))
            plain(dve, 4, onehot, row_adder)
            c(v_.tensor_scalar(st1[:, :], DEG[:, :], 1.0, None, ALU.max))
            c(v_.reciprocal(st1[:, :], st1[:, :]))
            c(v_.tensor_tensor(QT, acc1, over(st1[:, :]), ALU.mult))
            dve.wait_ge(w_next, 16 * 12)
            dve_proj(dve, 3)
            c(v_.tensor_tensor(QT, QT, vec(0), ALU.add))
            layer_norm(QT, QT)
            c(v_.tensor_tensor(QT, QT, over(st2[:, :]), ALU.mult))
            c(v_.tensor_tensor(QT, QT, vec(1), ALU.mult))
            c(v_.tensor_tensor(QT, QT, vec(2), ALU.add))
            dve.sem_inc(gelu_in, 1)
            dve.wait_ge(gelu_out, 1)
            c(v_.tensor_tensor(X[:, :, :], X[:, :, :], QT, ALU.add))
            dve.sem_inc(x_final, 1)


def kernel(x, src, dst, edge_attr_128, node_type_3, **w):
    import concourse.bacc as _bacc
    from concourse.bass_utils import run_bass_kernel_spmd as _run

    x, src, dst, ea, ntype = (np.asarray(v) for v in (x, src, dst, edge_attr_128, node_type_3))
    w = {k: np.asarray(v) for k, v in w.items()}
    sz = Sizes(x.shape[0], src.shape[0])
    rows = sz.slots * P
    cont = np.ascontiguousarray

    def padded(v, n, value):
        out = np.full((n,) + v.shape[1:], value, v.dtype)
        out[:v.shape[0]] = v
        return out

    def windows(v, value):
        v = padded(v, sz.edge_end + P, value)
        return cont(np.lib.stride_tricks.sliding_window_view(v, P)[::ALIGN])

    def by_head(m):
        out = np.zeros((D, D), m.dtype)
        for h in range(HEADS):
            out[h * DH:(h + 1) * DH, h * DH:(h + 1) * DH] = m[h]
        return out

    arrays = {
        "x": padded(x, rows, 0),
        "src_win": windows(src, 0), "dst_win": windows(dst, PAD_NODE),
        "src_pm": padded(src, P * sz.tiles, sz.blocks * P).reshape(P, sz.tiles),
        "dst_pm": padded(dst, P * sz.tiles, PAD_NODE).reshape(P, sz.tiles),
        "ea_t": cont(padded(ea, sz.edge_end + P, 0).T),
        "ntype": cont(padded(ntype, rows, 0).reshape(sz.slots, P).T),
        "ctx": w["L0_gnn_global_context"],
        "wk_t": cont(w["L0_gnn_Wk"].transpose(0, 2, 1)), "wv_t": cont(w["L0_gnn_Wv"].transpose(0, 2, 1)),
        "wq": w["L0_gnn_Wq"], "att": by_head(w["L0_gnn_rel_att"]), "msg": by_head(w["L0_gnn_rel_msg"]),
        "pri": w["L0_gnn_rel_pri"], "wa": w["L0_gnn_Wa"], "skip": w["L0_gnn_skip"],
        "ln_g": w["L0_gnn_ln_g"], "ln_b": w["L0_gnn_ln_b"], "film_w": w["L0_gnn_film_w"], "film_b": w["L0_gnn_film_b"],
        "w_root": w["L2_gnn_W_root"], "b_root": w["L2_gnn_b_root"], "w_msg": w["L2_gnn_W_msg"],
        "w_src": w["L2_gnn_W_src"], "w_dst": w["L2_gnn_W_dst"], "w_edge": w["L2_gnn_W_edge"],
        "w_l": w["L3_gnn_W_l"], "b_l": w["L3_gnn_b_l"], "w_r": w["L3_gnn_W_r"],
        "gamma": w["L3_gnn_gamma"], "beta": w["L3_gnn_beta"],
    }
    nc = _bacc.Bacc("TRN2", target_bir_lowering=False, num_devices=1)
    a, feeds = {}, {}
    for name, v in arrays.items():
        feeds[f"in_{name}"] = cont(v)
        a[name] = nc.dram_tensor(f"in_{name}", v.shape, mybir.dt.from_np(v.dtype), kind="ExternalInput").ap()
    a["out"] = nc.dram_tensor("out_x", (sz.nodes, D), F32, kind="ExternalOutput").ap()
    build(nc, sz, a)
    return _run(nc, [feeds], core_ids=[0]).results[0]["out_x"]
```

```python
import numpy as np
import concourse.bass as bass
from concourse import mybir
from contextlib import ExitStack

F32 = mybir.dt.float32
BF16 = mybir.dt.bfloat16
I32 = mybir.dt.int32
ALU = mybir.AluOpType
ACT = mybir.ActivationFunctionType
AX = mybir.AxisListType

P = 128
D = 128
HEADS = 8
DH = D // HEADS
TYPES = 3
CTX = 64
EPS = 1e-5
ALIGN = 16
QUAD = 4
RING = 4
UNROLL = 8
GROUP = 16
NEG = -1e30
PAD_NODE = 1 << 20


class Sizes:

    def __init__(self, nodes, edges):
        self.nodes, self.edges = nodes, edges
        self.blocks = -(-nodes // P)
        self.slots = self.blocks + 1
        self.slots += self.slots % 2
        most = (edges + self.blocks * (P - 1 + ALIGN - 1)) // P
        self.tiles = -(-most // P) * P
        self.edge_end = -(-edges // ALIGN) * ALIGN
        self.windows = self.edge_end // ALIGN + 1
        self.cols = self.tiles // P
        self.quads = self.tiles // QUAD
        self.groups = self.tiles // GROUP
        self.iters = self.quads // UNROLL
        self.parts = max(p for p in range(1, 8) if self.iters % p == 0)
        self.chunk = self.groups // self.parts
        self.span = self.chunk * P
        self.part_iters = self.iters // self.parts


def wait(eng, sem, value):
    if isinstance(value, int) and value <= 0:
        return
    eng.wait_ge(sem, value)


def build(nc, sz, a):
    NB, NS, T = sz.blocks, sz.slots, sz.tiles
    NQ, PARTS = sz.quads, sz.parts
    ctx = ExitStack()
    with ctx:
        def sb(name, shape, dt=F32):
            return ctx.enter_context(nc.sbuf_tensor(name, shape, dt))

        def sem(name):
            return ctx.enter_context(nc.semaphore(name))

        def dram(name, shape, dt=F32):
            return nc.dram_tensor(name, shape, dt, kind="Internal").ap()

        tab2 = dram("tab2", (NS * P, 2 * D))
        tab1 = dram("tab1", (NS * P, D))
        mvd = dram("mvd", (NQ, P, QUAD * D))
        flagd = dram("flagd", (T, P), BF16)
        metad = dram("metad", (3, T), I32)

        X = sb("X", [P, NS, D])
        H = sb("H", [P, NS, D])
        QTR = sb("QTR", [P, NS * D])
        accw = NS * (D + HEADS + 1)
        fw = sz.span + 2
        ACCR = sb("ACCR", [P, max(NS * 2 * D, accw + 3 * sz.span)])
        FLG = sb("FLG", [P, max(PARTS * fw // 2, 2 * QUAD * 2 * D + T, 3 * T)])
        MV = sb("MV", [P, RING, QUAD, D])
        G = sb("G", [P, RING * QUAD * 2 * D])
        SCR = sb("SCR", [P, 3072])
        S = sb("S", [P, RING, QUAD, P])
        ST = sb("ST", [P, 2, QUAD, P])
        REL = sb("REL", [P, T])
        SRC = sb("SRC", [P, T], I32)
        ISLOT = sb("ISLOT", [P, RING, QUAD], I32)
        BROW = sb("BROW", [1, T], I32)
        W = sb("W", [P, TYPES * 3 * D])
        ROWS = sb("ROWS", [P, 5, D])
        ident = sb("ident", [P, P])
        identb = sb("identb", [P, P], BF16)
        iota = sb("iota", [P, P])
        MASK = sb("MASK", [P, NS, TYPES])
        ALPHA = sb("ALPHA", [P, NS])
        DEG = sb("DEG", [P, NS])
        OUTDEG = sb("OUTDEG", [P, NS])
        st1 = sb("st1", [P, NS])
        st2 = sb("st2", [P, NS])
        small = sb("small", [P, 16])
        LASTK = sb("LASTK", [1, 8], I32)

        QT = QTR[:, 0:NS * D].rearrange("p (b d) -> p b d", d=D)
        acc0 = ACCR[:, 0:accw].rearrange("p (b d) -> p b d", d=D + HEADS + 1)
        acc1 = ACCR[:, 0:NS * D].rearrange("p (b d) -> p b d", d=D)
        acc2 = ACCR[:, 0:NS * 2 * D].rearrange("p (b d) -> p b d", d=2 * D)
        STATS = ACCR[:, 0:NS * 6].rearrange("p (b k) -> p b k", k=6)
        AT = ACCR[:, accw:accw + 2 * sz.span].rearrange("p (r g e) -> p r g e", r=2, e=P)
        FMAX = ACCR[:, accw + 2 * sz.span:accw + 3 * sz.span]
        flags = FLG[:, 0:PARTS * fw // 2].bitcast(BF16).rearrange("p (m j) -> p m j", m=PARTS)
        SROW = FLG[0:1, 2 * QUAD * 2 * D:2 * QUAD * 2 * D + T].bitcast(I32)
        RHS = FLG[:, 0:2 * QUAD * 2 * D].rearrange("p (r j d) -> p r j d", r=2, j=QUAD)
        G2 = G[:, :].rearrange("p (r j d) -> p r j d", r=RING, j=QUAD)
        G1 = G[:, 0:RING * QUAD * D].rearrange("p (r j d) -> p r j d", r=RING, j=QUAD)

        PSA = ctx.enter_context(nc.psum_tensor("PSA", [P, 2, QUAD, 2 * D], F32))
        PB = [ctx.enter_context(nc.psum_tensor(f"PB{i}", [P, 512], F32)) for i in range(4)]
        STP = [PB[3 * r][:, 0:256].bitcast(BF16).rearrange("p (j e) -> p j e", j=QUAD) for r in range(2)]
        QD = [PB[1 + r][:, :].rearrange("p (j d) -> p j d", j=QUAD) for r in range(2)]
        HOP = PB[3][:, 3 * P:4 * P]

        dve_done = sem("dve_done")
        consts = sem("consts")

        def edge_sems(n):
            s = {"onehot_ready": sem(f"onehot_ready_{n}")}
            if n != "scores":
                s |= {k: sem(f"{k}_{n}") for k in ("agg_done", "rows_added")}
            if n != "messages":
                s |= {k: [sem(f"{k}{r}_{n}") for r in range(RING)] for k in ("idx_filled", "gathered")}
            return s

        block = ctx.enter_context(nc.Block())
        reg_note = "computed on the chip from the tile's position, always in range"

        def at(i, u, d):
            v = u + d
            i = i + v // UNROLL if v // UNROLL else i
            v %= UNROLL
            return i * UNROLL + v, v % RING, i * (UNROLL // RING) + v // RING, v

        def valid(q):
            return not isinstance(q, int) or 0 <= q < NQ

        def steps(eng, fn, trailing):
            for u in range(UNROLL):
                fn(0, u)
            if sz.iters > 2:
                with eng.Fori(1, sz.iters - 1) as i:
                    for u in range(UNROLL):
                        fn(i, u)
            for u in range(UNROLL):
                fn(sz.iters - 1, u)
            for u in range(trailing):
                fn(sz.iters, u)

        LAG = sz.part_iters + 1
        hooks = [m * sz.part_iters + LAG for m in range(PARTS)]

        def layer0_steps(eng, fn, hook=None):
            last = sz.iters + LAG
            at_edge = {0, sz.iters - 1, sz.iters, LAG, last - 1, last} | set(hooks)
            i = 0
            while i <= last:
                if i in hooks and hook:
                    hook(hooks.index(i))
                on = (i <= sz.iters, i >= LAG)
                if i in at_edge:
                    for u in range(UNROLL):
                        fn(i, u, *on)
                    i += 1
                    continue
                j = i
                while j not in at_edge:
                    j += 1
                with eng.Fori(i, j) as r:
                    for u in range(UNROLL):
                        fn(r, u, *on)
                i = j

        def pairs(eng, fn, trailing):
            n = NS // 2
            for r in range(4):
                fn(r, r % 2)
            if n > 3:
                with eng.Fori(2, n - 1) as i:
                    for r in range(2):
                        fn(i * 2 + r, r)
            for r in range(2):
                fn(NS - 2 + r, r)
            for r in range(trailing):
                fn(NS + r, r)

        def group_of(i, u, d):
            v = u + d
            i = i + v // UNROLL if v // UNROLL else i
            return i * (UNROLL * QUAD // GROUP) + (v % UNROLL) // QUAD

        def CLINE(k):
            return W[0:1, TYPES * D + k * P:TYPES * D + (k + 1) * P]

        def has_block(b):
            return not isinstance(b, int) or 0 <= b < NS

        class Chain:

            def __init__(self, eng, s):
                self.eng, self.sem, self.n = eng, s, 0

            def __call__(self, ins):
                ins.then_inc(self.sem, 1)
                self.n += 1
                self.eng.wait_ge(self.sem, self.n)

        def bc(ap, shape, dim):
            return ap.unsqueeze(dim).to_broadcast(shape)


        c_ready = sem("consts_ready")
        dst_loaded = sem("dst_loaded")
        x_loaded = sem("x_loaded")
        w_loaded = sem("w_loaded")
        counted = sem("counted")
        counted_too = sem("counted_too")
        totals = sem("totals")
        windows_known = sem("windows_known")
        windows_in = sem("windows_in")
        tiles_masked = sem("tiles_masked")
        tiles_turned = sem("tiles_turned")
        tiles_stored = sem("tiles_stored")
        flags_in = sem("flags_in")
        acc_cleared = sem("acc_cleared")
        pool_added = sem("pool_added")
        scale_in = sem("scale_in")
        scale_out = sem("scale_out")
        rescaled = sem("rescaled")
        rows_in = sem("rows_in")
        w_combined = sem("w_combined")
        sig_in = sem("sig_in")
        sig_out = sem("sig_out")
        film_in = sem("film_in")
        stats_taken = sem("stats_taken")
        factors_known = sem("factors_known")
        normed = sem("normed")
        normed_too = sem("normed_too")
        root_in = sem("root_in")
        root_out = sem("root_out")
        hop_in = sem("hop_in")
        hop_out = sem("hop_out")
        exp_in = sem("exp_in")
        exp_out = sem("exp_out")
        w_free = sem("w_free")
        w_next = sem("w_next")
        hist_in = sem("hist_in")
        table_made = sem("table_made")
        table_out = sem("table_out")
        srow_in = sem("srow_in")
        gelu_in = sem("gelu_in")
        gelu_out = sem("gelu_out")
        x_final = sem("x_final")
        out_stored = sem("out_stored")

        NE = NB + 1
        flag_dmas = HEADS * (PARTS + 1) + 1
        NC = sz.cols
        WK = 3 * D

        TC = -(-sz.edges // P)
        DSTI = G[:, 0:TC].bitcast(I32)
        DSTF = G[:, T:T + TC]
        DSTK = G[:, T:2 * T]
        SRCW = G[:, 2 * T:3 * T].bitcast(I32).rearrange("p (c e) -> p c e", c=NC)
        DSTW = G[:, 3 * T:3 * T + NC * (P + 1)].bitcast(I32).rearrange("p (c e) -> p c e", c=NC)
        SRCF = SCR[:, 0:T].rearrange("p (c e) -> p c e", c=NC)
        RELF = SCR[:, T:2 * T].rearrange("p (c e) -> p c e", c=NC)
        JUNK = SCR[:, 2 * T:2 * T + TC]
        JUNKA = G[:, 2 * T:2 * T + TC]
        VAL = SCR[:, 2 * T:3 * T].rearrange("p (c e) -> p c e", c=NC)
        STARTS = SCR[:, 2 * T:2 * T + T // 2].bitcast(BF16).rearrange("p (c e) -> p c e", c=NC)
        DKF = DSTK.rearrange("p (c e) -> p c e", c=NC)
        KEYW = G[:, 0:T].rearrange("p (c e) -> p c e", c=NC)
        q0 = [0]

        def cut(n, dt=F32):
            v = QTR[:, q0[0]:q0[0] + n]
            q0[0] += n
            return v if dt == F32 else v.bitcast(dt)

        ON_ACT = NS * 3 // 5
        half = NE // 2
        thr_half = cut(NE)
        thr, cnt, bf, b16f, tiles_f, zer, cum, rel0, delta = (cut(NE) for _ in range(9))
        bi = cut(NE, I32)
        ti32 = cut(NE, I32)
        ones = cut(P)
        pI, p15, p4 = (cut(1, I32) for _ in range(3))
        p15f, p4f, tp = (cut(1) for _ in range(3))
        cI = cut(NC, I32)
        grp, tpos, bt, st, off = (cut(NC) for _ in range(5))
        bI, sI, wI, kI = (cut(NC, I32) for _ in range(4))
        prev = cut(NC)
        M = cut(NC * NE).rearrange("p (c b) -> p c b", c=NC)
        MD = cut(NC * NE).rearrange("p (c b) -> p c b", c=NC)
        thrI = cut(NE, I32)
        iotaI = cut(P, I32)
        NTI = cut(NS, I32)
        SKIP = cut(4)
        SIG = cut(4)
        PRI8 = cut(HEADS)
        SF = S[:, :, :, :].rearrange("p r j e -> p (r j e)")
        WKT = SF[:, 0:384].rearrange("p (t d) -> p t d", t=3)
        WVT = SF[:, 384:768].rearrange("p (t d) -> p t d", t=3)
        ATTB, MSGB = SF[:, 768:896], SF[:, 896:1024]
        FILMW = SF[0:CTX, 1024:1280]
        CTXB = SF[0:CTX, 1280:1408]
        CTXC = SF[0:CTX, 1408:1409]
        W3 = W[:, :].rearrange("p (t c) -> p t c", t=TYPES)
        WA = W[:, 0:TYPES * D].rearrange("p (t c) -> p t c", t=TYPES)
        PRI = ROWS[:, 0, :]

        MB = G[:, 0:2 * WK].rearrange("p (r t d) -> p r t d", r=2, t=3)
        HT = G[:, 2 * WK:4 * WK].rearrange("p (r t d) -> p r t d", r=2, t=3)
        STG = G[:, 4 * WK:4 * WK + 4 * D].rearrange("p (r d) -> p r d", r=2)

        def proj_sems(n):
            s = {k: sem(f"{k}_{n}") for k in ("placed", "turned", "copied", "multiplied", "evacuated", "inputs")}
            if n in ("typed_qkv", "gate_nodes"):
                s["stored"] = [sem(f"stored{r}_{n}") for r in range(2)]
            return s

        proj = [proj_sems(n) for n in ("typed_qkv", "typed_out", "gate_nodes", "sage")]
        proj_w = [
            (3, lambda t: W3[:, t, :], WK),
            (3, lambda t: WA[:, t, :], D),
            (1, lambda t: W[:, 0:4 * D], 4 * D),
            (2, lambda t: W[:, t * D:(t + 1) * D], D),
        ]

        def pe_proj(pe, n):
            s, (ni, w, cols) = proj[n], proj_w[n]
            pe.wait_ge(s["inputs"], 1)

            def step(b, r):
                if has_block(b):
                    pe.wait_ge(s["placed"], b + 1)
                    wait(pe, s["copied"], b - 1)
                    for t in range(ni):
                        last = nc.tensor.transpose(PB[r][:, t * P:(t + 1) * P], MB[:, r, t, :], ident[:, :])
                    last.then_inc(s["turned"], 1)
                m = b - 1
                if has_block(m):
                    pe.wait_ge(s["copied"], m + 1)
                    wait(pe, s["evacuated"], m - 1)
                    for t in range(ni):
                        last = nc.tensor.matmul(PB[2 + (1 - r)][:, 0:cols], HT[:, 1 - r, t, :], w(t),
                                                start=t == 0, stop=t == ni - 1)
                    last.then_inc(s["multiplied"], 1)
            pairs(pe, step, 1)

        def act_proj(act, n):
            s, (ni, w, cols) = proj[n], proj_w[n]

            def step(b, r):
                act.wait_ge(s["turned"], b + 1)
                wait(act, s["multiplied"], b - 1)
                nc.scalar.copy(HT[:, r, 0:ni, :].rearrange("p t d -> p (t d)"),
                               PB[r][:, 0:ni * P]).then_inc(s["copied"], 1)
            pairs(act, step, 0)

        def dve_proj(dve, n):
            s = proj[n]
            dve.sem_inc(s["inputs"], 1)

            def copy(dst, src):
                return nc.vector.tensor_scalar(dst, src, 1.0, None, ALU.mult)

            def step(b, r):
                if has_block(b):
                    wait(dve, s["turned"], b - 1)
                if n == 3 and has_block(b):
                    copy(MB[:, r, 0:1, :], QT[:, bass.ds(b, 1), :])
                if n in (2, 3) and has_block(b):
                    copy(MB[:, r, n - 2:n - 1, :], H[:, bass.ds(b, 1), :]).then_inc(s["placed"], 1)
                if n in (0, 1) and has_block(b):
                    src = H if n == 0 else acc0
                    nc.vector.tensor_tensor(
                        MB[:, r, :, :], src[:, bass.ds(b, 1), 0:D].to_broadcast([P, 3, D]),
                        MASK[:, bass.ds(b, 1), :].rearrange("p o t -> p (o t)").unsqueeze(2).to_broadcast([P, 3, D]),
                        ALU.mult).then_inc(s["placed"], 1)
                m, rm = b - 2, r
                if has_block(m):
                    dve.wait_ge(s["multiplied"], m + 1)
                    ps = PB[2 + rm]
                    row = lambda tab: tab[:, bass.ds(m, 1), :].rearrange("p o d -> p (o d)")
                    if n == 1:
                        nc.vector.tensor_tensor(row(QT), row(QT), ps[:, 0:D], ALU.add).then_inc(s["evacuated"], 1)
                        return
                    if n == 3:
                        copy(row(QT), ps[:, 0:D]).then_inc(s["evacuated"], 1)
                        return
                    if n == 0:
                        nc.vector.tensor_tensor(row(QT), ps[:, 2 * D:3 * D], PRI, ALU.mult)
                    else:
                        copy(row(QT), ps[:, 2 * D:3 * D])
                        nc.vector.tensor_tensor(row(H), row(H), ps[:, 3 * D:4 * D], ALU.add)
                    half = m // 2 if isinstance(m, int) else None
                    if isinstance(m, int):
                        wait(dve, s["stored"][rm], half * 16)
                    else:
                        dve.wait_ge(s["stored"][rm], (m - rm) * 8)
                    copy(STG[:, rm, :], ps[:, 0:2 * D]).then_inc(s["evacuated"], 1)
            pairs(dve, step, 2)
            dve.wait_ge(s["evacuated"], NS)

        def sp_proj(sp, n):
            s = proj[n]

            def step(b, r):
                sp.wait_ge(s["evacuated"], b + 1)
                sp.dma_start(tab2[bass.ds(b * P, P), :], STG[:, r, :]).then_inc(s["stored"][r], 16)
            pairs(sp, step, 0)

        names = ("scores", "messages", "degree", "gated", "mean")
        ps = [edge_sems(n) for n in names]
        scored = {k: sem(k + "_scores") for k in ("st_turned", "st_copied", "q_spread", "multiplied", "reduced", "grp_turned", "grp_copied")}
        mv_stored = [sem(f"mv_stored{r}") for r in range(RING)]
        mv_loaded = [sem(f"mv_loaded{r}") for r in range(RING)]
        weighted = {k: sem(k + "_messages") for k in ("grp_staged", "grp_turned", "grp_copied", "prob_put", "weighted")}
        hist_ready = sem("hist_ready")
        gated = {k: sem(k + "_gated") for k in ("st_turned", "st_copied", "pre_done", "summed", "gate_done", "multiplied")}
        ea_loaded = [sem(f"ea_loaded{r}") for r in range(RING)]
        may_gather = sem("may_gather")
        may_move = sem("may_move")
        rows_read = {0: scored["multiplied"], 2: ps[2]["agg_done"], 3: gated["multiplied"], 4: ps[4]["agg_done"]}

        PROD = SCR[:, 0:1024].rearrange("p (r j d) -> p r j d", r=2, j=QUAD)
        ABUF = SCR[:, 1024:1280].rearrange("p (r c) -> p r c", r=2)
        WMW = D + HEADS + 1
        WM = SCR[:, 1280:1280 + 2 * QUAD * WMW].rearrange("p (r j d) -> p r j d", r=2, j=QUAD)
        AE = SCR[:, 2400:2656].rearrange("p (r c) -> p r c", r=2)
        ATS = SCR[:, 2656:2912].rearrange("p (r e) -> p r e", r=2)
        LOH = SCR[:, 0:1024].bitcast(BF16).rearrange("p (r j c) -> p r j c", r=RING, j=QUAD)
        HIH = SCR[:, 1024:1024 + RING * QUAD * NS // 2].bitcast(BF16).rearrange("p (r j c) -> p r j c", r=RING, j=QUAD)
        LO = FLG[:, 0:T // 2].bitcast(BF16)
        HI = FLG[:, T // 2:T].bitcast(BF16)
        SRCPM = FLG[:, T:2 * T].bitcast(I32)
        SRCTMP = FLG[:, 2 * T:3 * T].bitcast(I32)
        PRE = SCR[:, 0:1024].rearrange("p (r j d) -> p r j d", r=2, j=QUAD)
        EA = SCR[:, 1024:3072].rearrange("p (r j e) -> p r j e", r=RING, j=QUAD)
        ATP = PB[3][:, 0:P]
        AEP = PB[3][:, P:2 * P]
        HISTP = PB[2][:, 0:NS]

        def registers(eng, row, q, most):
            _, values = nc.values_load_multi_w_load_instructions(
                row[0:1, bass.ds(q * QUAD, QUAD)], engines=[eng.engine], min_val=0, max_val=most,
                skip_runtime_bounds_check_because=reg_note)
            return values

        def pool_gathers(pool, n, rows, table):
            s = ps[n]

            def step(i, u):
                q, slot, turn, _ = at(i, u, 0)
                pool.wait_ge(s["idx_filled"][slot], (turn + 1) * 16)
                wait(pool, rows_read[n], q - RING + 1)
                if n == 0:
                    wait(pool, mv_stored[slot], turn * 16)
                pool.sem_inc(may_gather, 1)
                for j in range(QUAD):
                    nc.gpsimd.indirect_dma_start(
                        out=rows[:, slot, j, :], out_offset=None, in_=table,
                        in_offset=bass.IndirectOffsetOnAxis(ap=ISLOT[:, slot, j:j + 1], axis=0),
                    ).then_inc(s["gathered"][slot], 16)
            steps(pool, step, 0)

        @block.gpsimd
        def _(pool):
            nc.gpsimd.memset(ident[:, :], 0.0).then_inc(consts, 1)
            pool.wait_ge(consts, 1)
            nc.gpsimd.affine_select(out=ident[:, :], in_=ident[:, :], compare_op=ALU.not_equal, fill=1.0,
                                    base=0, pattern=[[-1, P]], channel_multiplier=1)
            nc.gpsimd.iota(iotaI, pattern=[[1, P]], base=0, channel_multiplier=0)
            nc.gpsimd.iota(thrI, pattern=[[P, NE]], base=0, channel_multiplier=0)
            nc.gpsimd.iota(pI, pattern=[[0, 1]], base=0, channel_multiplier=1)
            nc.gpsimd.iota(cI, pattern=[[8, NC]], base=0, channel_multiplier=0).then_inc(c_ready, 1)
            pool.wait_ge(windows_known, 1)
            pool.sem_inc(may_gather, 1)
            for c in range(NC):
                for src, dst in ((a["src_win"], SRCW), (a["dst_win"], DSTW)):
                    nc.gpsimd.indirect_dma_start(
                        out=dst[:, c, :], out_offset=None, in_=src,
                        in_offset=bass.IndirectOffsetOnAxis(ap=wI[:, c:c + 1], axis=0)).then_inc(windows_in, 16)
            pool.wait_ge(tiles_stored, 64)
            starts = flagd.rearrange("(m g t) e -> t m g e", m=PARTS, t=GROUP)
            with nc.allow_non_contiguous_dma(reason="single flags"):
                for h in range(HEADS):
                    for m in range(PARTS):
                        nc.gpsimd.dma_start(flags[h:P:HEADS, m, 0:sz.span].rearrange("t (g e) -> t g e", e=P),
                                            starts[:, m]).then_inc(flags_in, 16)
                    nc.gpsimd.dma_start(flags[h:P - HEADS:HEADS, :, sz.span:sz.span + 1], starts[1:GROUP, :, 0, 0:1]).then_inc(flags_in, 16)
                run = sz.chunk * GROUP
                if PARTS > 1:
                    nc.gpsimd.dma_start(LASTK[0:1, 1:PARTS], metad[2:3, run - 1:(PARTS - 1) * run:run]).then_inc(flags_in, 16)
            nc.gpsimd.memset(acc0, 0.0).then_inc(acc_cleared, 1)
            for r in range(2):
                pool.wait_ge(proj[0]["stored"][r], 16 * NS // 2)
            pool_gathers(pool, 0, G2, tab2)

            pool.wait_ge(scored["multiplied"], NQ)
            node, steps_done = [P, NS, D], [0]

            def each(out, x, y, op):
                nc.gpsimd.tensor_tensor(out, x, y, op).then_inc(pool_added, 1)
                steps_done[0] += 1
                pool.wait_ge(pool_added, steps_done[0])
            each(QT, H[:, :, :], ALPHA[:, :].unsqueeze(2).to_broadcast(node), ALU.mult)
            each(H[:, :, :], H[:, :, :], bc(ROWS[:, 3, :], node, 1), ALU.mult)
            each(X[:, :, :], X[:, :, :], H[:, :, :], ALU.add)
            each(X[:, :, :], X[:, :, :], bc(ROWS[:, 2, :], node, 1), ALU.add)

            pool.wait_ge(table_out, 16)
            pool_gathers(pool, 2, G1, tab1)
            pool.wait_ge(proj[2]["inputs"], 1)
            each(X[:, :, :], X[:, :, :], bc(ROWS[:, 0, :], node, 1), ALU.add)
            nc.gpsimd.memset(acc2, 0.0).then_inc(acc_cleared, 1)
            for r in range(2):
                pool.wait_ge(proj[2]["stored"][r], 16 * NS // 2)
            pool_gathers(pool, 3, G2, tab2)
            pool.wait_ge(table_out, 32)
            pool_gathers(pool, 4, G1, tab1)

        def sp_edges(sp, n):
            s = ps[n]

            def step(i, u):
                q, slot, turn, _ = at(i, u, 0)
                wait(sp, s["gathered"][slot], turn * 64)
                sp.dma_start(ISLOT[:, slot, :], SRC[:, bass.ds(q * QUAD, QUAD)]).then_inc(s["idx_filled"][slot], 16)
                if n == 3:
                    wait(sp, gated["pre_done"], q - RING + 1)
                    for j, first in enumerate(registers(sp, SROW, q, sz.edge_end)):
                        sp.dma_start(EA[:, slot, j, :], a["ea_t"][:, bass.ds(first, P)]).then_inc(ea_loaded[slot], 16)
            steps(sp, step, 0)

        def sp_layer0(sp):
            s = ps[0]

            def step(i, u, scores, messages):
                q, slot, turn, _ = at(i, u, 0)
                if scores:
                    wait(sp, s["gathered"][slot], turn * 64)
                    if not isinstance(q, int) or RING <= q < NQ + RING:
                        sp.sem_inc(may_move, 1)
                        sp.dma_start(mvd[bass.ds(q - RING, 1), :, :].rearrange("o p (j d) -> (o p) j d", j=QUAD),
                                     G2[:, slot, :, D:2 * D]).then_inc(mv_stored[slot], 16)
                    if valid(q):
                        sp.dma_start(ISLOT[:, slot, :], SRC[:, bass.ds(q * QUAD, QUAD)]).then_inc(s["idx_filled"][slot], 16)
                if messages:
                    q, slot, turn, _ = at(i - LAG, u, 0)
                    if valid(q):
                        sp.wait_ge(mv_stored[slot], (turn + 1) * 16)
                        sp.sem_inc(may_move, 1)
                        wait(sp, weighted["weighted"], q - RING + 1)
                        sp.sem_inc(may_move, 1)
                        sp.dma_start(MV[:, slot, :, :].rearrange("p j d -> p (j d)"),
                                     mvd[bass.ds(q, 1), :, :].rearrange("o p f -> (o p) f")).then_inc(mv_loaded[slot], 16)

            def guarded(i, u, scores, messages):
                step(i, u, scores and not (isinstance(i, int) and i == sz.iters and u >= RING), messages)
            layer0_steps(sp, guarded)

        def row_bc(v, n):
            return v.rearrange("(o n) -> o n", o=1).to_broadcast([P, n])

        @block.sync
        def _(sp):
            sp.dma_start(DSTI, a["dst_pm"]).then_inc(dst_loaded, 16)
            sp.dma_start(X[:, :, :], a["x"].rearrange("(b p) d -> p b d", p=P)).then_inc(x_loaded, 16)
            loads = [
                (WKT, a["wk_t"].rearrange("t m i -> m t i")), (WVT, a["wv_t"].rearrange("t m i -> m t i")),
                (W3[:, :, 2 * D:3 * D], a["wq"].rearrange("t i o -> i t o")),
                (ATTB, a["att"]), (MSGB, a["msg"]), (FILMW, a["film_w"]),
                (CTXC, a["ctx"].rearrange("(c o) -> c o", o=1)), (NTI, a["ntype"]),
                (SKIP[:, 0:3], row_bc(a["skip"], 3)), (PRI8, row_bc(a["pri"], HEADS)),
                (ROWS[:, 1, :], row_bc(a["ln_g"], D)), (ROWS[:, 2, :], row_bc(a["ln_b"], D)),
                (ROWS[:, 3:5, :].rearrange("p a d -> p (a d)"), row_bc(a["film_b"], 2 * D)),
            ]
            with nc.allow_non_contiguous_dma(reason="columns of a few words"):
                for dst, src in loads:
                    sp.dma_start(dst, src).then_inc(w_loaded, 16)
                sp.wait_ge(tiles_masked, 1)
                sp.dma_start(flagd.rearrange("(c p) e -> p c e", p=P), STARTS).then_inc(tiles_stored, 16)
                sp.dma_start(metad[2, :].rearrange("(c p) -> p c", p=P), kI).then_inc(tiles_stored, 16)
                sp.dma_start(metad[0, :].rearrange("(c p) -> p c", p=P), bI).then_inc(tiles_stored, 16)
                sp.dma_start(metad[1, :].rearrange("(c p) -> p c", p=P), sI).then_inc(tiles_stored, 16)
                sp.wait_ge(tiles_stored, 64)
                sp.dma_start(BROW[:, :], metad[0:1, :]).then_inc(rows_in, 16)
            sp_proj(sp, 0)
            sp_layer0(sp)
            sp.wait_ge(w_free, 1)
            sp.dma_start(WA, a["wa"].rearrange("t i o -> i t o")).then_inc(w_next, 16)
            sp.dma_start(SRCPM, a["src_pm"]).then_inc(hist_in, 16)
            sp.wait_ge(table_made, 1)
            sp.dma_start(tab1.rearrange("(b p) d -> p b d", p=P), H[:, :, :]).then_inc(table_out, 16)
            sp.dma_start(ROWS[:, 0, :], row_bc(a["b_root"], D)).then_inc(w_next, 16)
            for k, name in enumerate(("w_src", "w_msg", "w_dst", "w_root", "w_edge")):
                sp.dma_start(W[:, k * D:(k + 1) * D], a[name]).then_inc(w_next, 16)
            sp_edges(sp, 2)
            sp.wait_ge(hist_ready, NQ)
            sp.dma_start(SROW, metad[1:2, :]).then_inc(srow_in, 16)
            sp.wait_ge(srow_in, 16)
            sp_proj(sp, 2)
            sp_edges(sp, 3)
            sp.wait_ge(table_made, 2)
            sp.dma_start(tab1.rearrange("(b p) d -> p b d", p=P), H[:, :, :]).then_inc(table_out, 16)
            for k, name in enumerate(("w_l", "w_r")):
                sp.dma_start(W[:, k * D:(k + 1) * D], a[name]).then_inc(w_next, 16)
            for k, name in enumerate(("b_l", "gamma", "beta")):
                sp.dma_start(ROWS[:, k, :], row_bc(a[name], D)).then_inc(w_next, 16)
            sp_edges(sp, 4)
            sp.wait_ge(x_final, 1)
            whole = sz.nodes // P
            left = sz.nodes - whole * P
            sp.dma_start(a["out"][0:whole * P, :].rearrange("(b p) d -> p b d", p=P), X[:, 0:whole, :]).then_inc(out_stored, 16)
            if left:
                sp.dma_start(a["out"][whole * P:sz.nodes, :], X[0:left, whole, :]).then_inc(out_stored, 16)
            sp.wait_ge(out_stored, 32 if left else 16)

        def bf_view(slot, j):
            return S[:, slot, j, :].bitcast(BF16)[:, 1::2]

        def pe_turn_onehot(pe, s, onehot, q, slot, par, banks):
            pe.wait_ge(onehot, q + 1)
            wait(pe, s["st_copied"], q + 1 - banks)
            for j in range(QUAD):
                last = nc.tensor.transpose(STP[par][:, j, :], bf_view(slot, j), identb[:, :])
            last.then_inc(s["st_turned"], 1)

        def pe_agg(pe, n, q, slot, par, rhs, width):
            s = ps[n]
            pe.wait_ge(s["onehot_ready"], q + 1)
            wait(pe, s["rows_added"], (q - 1) * QUAD)
            for j in range(QUAD):
                last = nc.tensor.matmul(PSA[:, par, j, 0:width], S[:, slot, j, :], rhs(j), start=True, stop=True)
            last.then_inc(s["agg_done"], 1)

        def pe_plain(pe, n):
            s = ps[n]

            def step(i, u):
                q, slot, turn, v = at(i, u, 0)
                if n == 2:
                    pe.wait_ge(hist_ready, q + 1)
                    for j in range(QUAD):
                        first = isinstance(q, int) and q == 0 and j == 0
                        final = isinstance(q, int) and q == NQ - 1 and j == QUAD - 1
                        nc.tensor.matmul(HISTP, LOH[:, slot, j, :], HIH[:, slot, j, :], start=first, stop=final,
                                         skip_group_check=True)
                pe.wait_ge(s["gathered"][slot], (turn + 1) * 64)
                pe_agg(pe, n, q, slot, v % 2, lambda j: G1[:, slot, j, :], D)
            steps(pe, step, 0)

        @block.tensor
        def _(pe):
            pe.wait_ge(counted, half + 1)
            pe.wait_ge(counted_too, NE - half)
            nc.tensor.matmul(PB[0][:, 0:NE], ones, cnt, start=True, stop=True).then_inc(totals, 1)
            pe.wait_ge(w_loaded, 16 * 13)
            for t in range(TYPES):
                nc.tensor.matmul(PB[1][:, t * D:(t + 1) * D], WKT[:, t, :], ATTB, start=True, stop=True)
                nc.tensor.matmul(PB[2][:, t * D:(t + 1) * D], WVT[:, t, :], MSGB, start=True, stop=True)
            pe.wait_ge(film_in, 1)
            nc.tensor.matmul(PB[3][:, 0:2 * D], CTXB, FILMW, start=True, stop=True).then_inc(w_combined, 1)
            pe.wait_ge(tiles_masked, 1)
            for c in range(NC):
                for k, f in enumerate((RELF, SRCF)):
                    last = nc.tensor.transpose(PB[2 * k + c // 4][:, (c % 4) * P:(c % 4 + 1) * P], f[:, c, :], ident[:, :])
            last.then_inc(tiles_turned, 1)
            pe_proj(pe, 0)

            pe.wait_ge(rows_in, 16)
            s = scored

            w = weighted
            hops = [0]

            def hop(lhs, rhs, dst):
                hops[0] += 1
                pe.wait_ge(hop_in, hops[0])
                nc.tensor.matmul(dst, lhs, rhs, start=True, stop=True).then_inc(hop_out, 1)

            def carries(m):
                pe.wait_ge(s["grp_copied"], min((m + 1) * sz.chunk + 1, sz.groups))
                wait(pe, w["grp_copied"], m * sz.chunk)
                for _ in range(2):
                    for _ in range(2):
                        hop(small[:, 0:1], ident[:, :], HOP[0:1, :])
                    hop(CLINE(3), small[0:1, 3:4], HOP[:, 0:1])
                if m:
                    hop(small[:, 0:1], ident[:, :], HOP[0:1, :])
                pe.wait_ge(exp_in, m + 1)

            def step(i, u, scores, messages):
                q, slot, turn, v = at(i, u, 0)
                if scores and valid(q):
                    pe_turn_onehot(pe, s, ps[0]["onehot_ready"], q, v % 2, 0, 1)
                q, slot, turn, v = at(i, u, -1)
                if scores and valid(q):
                    pe.wait_ge(s["st_copied"], q + 1)
                    wait(pe, s["multiplied"], q - 1)
                    blocks = registers(pe, BROW, q, NB)
                    for j in range(QUAD):
                        last = nc.tensor.matmul(QD[v % 2][:, j, :], ST[:, v % 2, j, :],
                                                QT[:, bass.ds(blocks[j], 1), :].rearrange("p o d -> p (o d)"), start=True, stop=True)
                    last.then_inc(s["q_spread"], 1)
                q, slot, turn, v = at(i, u, -3)
                if scores and valid(q) and v % 4 == 3:
                    pe.wait_ge(s["reduced"], q + 1)
                    g = group_of(i, u, -3)
                    wait(pe, s["grp_copied"], g)
                    if messages:
                        wait(pe, w["grp_copied"], (i - LAG) * 2 + (1 if u == 2 else 2))
                    nc.tensor.transpose(ATP, ABUF[:, (v // 4) % 2, :], ident[:, :]).then_inc(s["grp_turned"], 1)
                q, slot, turn, v = at(i - LAG, u, 0)
                if isinstance(i, int) and i in hooks[1:] and u == 4:
                    pe.wait_ge(rescaled, hooks.index(i))
                if messages and valid(q) and v % 4 == 0:
                    g = group_of(i - LAG, u, 0)
                    pe.wait_ge(w["grp_staged"], g + 1)
                    wait(pe, w["grp_copied"], g)
                    if scores and not (isinstance(i, int) and i == sz.iters and u):
                        wait(pe, s["grp_copied"], i * 2 - 1 + (u > 0))
                    else:
                        wait(pe, s["grp_copied"], sz.groups)
                    nc.tensor.transpose(AEP, ATS[:, (v // 4) % 2, :], ident[:, :]).then_inc(w["grp_turned"], 1)
                q, slot, turn, v = at(i - LAG, u, -3)
                if messages and valid(q):
                    pe.wait_ge(w["weighted"], q + 1)
                    pe_agg(pe, 1, q, 2 + v % 2, v % 2, lambda j: WM[:, v % 2, j, :], WMW)
                if isinstance(i, int) and i in hooks[1:] and u == 3:
                    pe.wait_ge(w["grp_copied"], hooks.index(i) * sz.chunk + 1)
                    pe.wait_ge(s["grp_copied"], min(i * 2, sz.groups))
                    hop(CLINE(5), CLINE(4)[:, 24:24 + HEADS], HOP[:, 0:HEADS])
            layer0_steps(pe, step, carries)
            pe_proj(pe, 1)
            pe_plain(pe, 2)
            pe_proj(pe, 2)

            s = gated

            def step(i, u):
                q, slot, turn, v = at(i, u, -1)
                if valid(q):
                    blocks = registers(pe, BROW, q, NB)
                    pe.wait_ge(ea_loaded[slot], (turn + 1) * 64)
                    wait(pe, s["summed"], q - 1)
                    for j in range(QUAD):
                        nc.tensor.matmul(QD[v % 2][:, j, :], EA[:, slot, j, :], W[:, 4 * D:5 * D], start=j == 0, stop=False,
                                         skip_group_check=True)
                    pe.wait_ge(s["st_copied"], q + 1)
                    for j in range(QUAD):
                        last = nc.tensor.matmul(QD[v % 2][:, j, :], ST[:, v % 2, j, :],
                                                QT[:, bass.ds(blocks[j], 1), :].rearrange("p o d -> p (o d)"), start=False, stop=True,
                                                skip_group_check=True)
                    last.then_inc(s["pre_done"], 1)
                q, slot, turn, v = at(i, u, -3)
                if valid(q):
                    pe.wait_ge(s["multiplied"], q + 1)
                    pe_agg(pe, 3, q, slot, v % 2, lambda j: RHS[:, v % 2, j, :], 2 * D)
                q, slot, turn, v = at(i, u, 0)
                if valid(q):
                    pe_turn_onehot(pe, s, ps[3]["onehot_ready"], q, slot, v % 2, 2)
            steps(pe, step, 3)
            pe_plain(pe, 4)
            pe_proj(pe, 3)

        def act_copy_onehot(act, s, q, par, used, bank):
            act.wait_ge(s["st_turned"], q + 1)
            wait(act, used, q - 1)
            nc.scalar.copy(ST[:, par, :, :], STP[bank]).then_inc(s["st_copied"], 1)

        @block.scalar
        def _(act):
            turn_no = [0]

            roots = [0]

            def root(t):
                roots[0] += 1
                act.wait_ge(root_in, roots[0])
                nc.scalar.activation(t[:, :], t[:, :], ACT.Sqrt).then_inc(root_out, 1)

            def normalise(src, dst, func):
                root(st2)
                turn_no[0] += 1
                act.wait_ge(factors_known, turn_no[0])

                for b in range(ON_ACT):
                    nc.scalar.activation(dst[:, b, :], src[:, b, :], func, bias=st1[:, b:b + 1],
                                         scale=st2[:, b:b + 1]).then_inc(normed, 1)

            act.wait_ge(counted, 1)
            def count(b):
                nc.scalar.activation(JUNKA, DSTF, ACT.Sign, bias=thr_half[:, bass.ds(b, 1)], scale=-1.0,
                                     accum_out=cnt[:, bass.ds(b, 1)]).then_inc(counted_too, 1)
            count(half)
            with act.Fori(half + 1, NE) as b:
                act.wait_ge(counted_too, b - half)
                count(b)
            act.wait_ge(sig_in, 1)
            nc.scalar.activation(SIG[:, 0:3], SKIP[:, 0:3], ACT.Sigmoid).then_inc(sig_out, 1)
            normalise(X, H, ACT.Relu)
            act_proj(act, 0)
            s, w = scored, weighted

            def exponentials(m):
                act.wait_ge(exp_in, m + 1)
                nc.scalar.activation(AT[:, m % 2, :, :], FMAX.rearrange("p (g e) -> p g e", e=P), ACT.Exp).then_inc(exp_out, 1)
                act.wait_ge(exp_out, m + 1)
                if m:
                    act.wait_ge(scale_in, m)
                    nc.scalar.activation(CLINE(4)[:, 24:24 + HEADS], CLINE(4)[:, 16:16 + HEADS], ACT.Exp).then_inc(scale_out, 1)

            def ring_group(g):
                flat = AT.rearrange("p r g e -> p (r g e)")
                return flat[:, bass.ds((g % (2 * sz.chunk)) * P, P)]

            def step(i, u, scores, messages):
                q, slot, turn, v = at(i - LAG, u, -1)
                if messages and valid(q) and v % 4 == 0:
                    act.wait_ge(w["grp_turned"], group_of(i - LAG, u, -1) + 1)
                    wait(act, w["weighted"], q - QUAD)
                    nc.scalar.copy(AE[:, (v // 4) % 2, :], AEP).then_inc(w["grp_copied"], 1)
                q, slot, turn, v = at(i - LAG, u, -2)
                if messages and valid(q):
                    wait(act, ps[1]["agg_done"], q - 1)
                    wait(act, w["grp_copied"], group_of(i - LAG, u, -2) + 1)
                    nc.scalar.copy(WM[:, v % 2, :, D:D + HEADS],
                                   AE[:, (v // 4) % 2, (v % 4) * 32:(v % 4) * 32 + 32].rearrange("p (j h) -> p j h", j=QUAD)
                                   ).then_inc(w["prob_put"], 1)
                q, slot, turn, v = at(i, u, 0)
                if scores and valid(q):
                    act_copy_onehot(act, s, q, v % 2, s["q_spread"], 0)
                q, slot, turn, v = at(i, u, -3)
                if scores and valid(q) and v % 4 == 3:
                    g = group_of(i, u, -3)
                    act.wait_ge(s["grp_turned"], g + 1)
                    nc.scalar.copy(ring_group(g), ATP).then_inc(s["grp_copied"], 1)
                q, slot, turn, v = at(i - LAG, u, 0)
                if messages and valid(q) and v % 4 == 0:
                    g = group_of(i - LAG, u, 0)
                    wait(act, w["grp_turned"], g - 1)
                    nc.scalar.copy(ATS[:, (v // 4) % 2, :], ring_group(g)).then_inc(w["grp_staged"], 1)
            layer0_steps(act, step, exponentials)
            act_proj(act, 1)
            normalise(QT, QT, ACT.Identity)
            root(ALPHA)
            normalise(X, H, ACT.Relu)
            root(OUTDEG)
            normalise(X, H, ACT.Relu)
            act_proj(act, 2)
            s = gated

            def step(i, u):
                q, slot, turn, v = at(i, u, 0)
                if valid(q):
                    act_copy_onehot(act, s, q, v % 2, s["pre_done"], v % 2)
                q, slot, turn, v = at(i, u, -2)
                if valid(q):
                    act.wait_ge(s["summed"], q + 1)
                    wait(act, ps[3]["agg_done"], q - 1)
                    nc.scalar.activation(RHS[:, v % 2, :, D:2 * D], PRE[:, v % 2, :, :], ACT.Sigmoid).then_inc(s["gate_done"], 1)
            steps(act, step, 2)
            normalise(X, H, ACT.Relu)
            act_proj(act, 3)
            normalise(QT, QT, ACT.Identity)
            act.wait_ge(gelu_in, 1)
            nc.scalar.activation(QT, QT, ACT.Gelu).then_inc(gelu_out, 1)

        def plain(dve, n, onehot, row_adder):
            def step(i, u):
                q, slot, turn, v = at(i, u, -2)
                add = row_adder(n, acc1, D, q, v % 2)
                add(0)
                q, slot, turn, v = at(i, u, 0)
                if valid(q):
                    onehot(n, q, slot)
                add(1)
                if valid(q) and n == 2:
                    cols = bass.ds(q * QUAD, QUAD)
                    nc.vector.tensor_tensor(LOH[:, slot, :, :], bc(iota[:, :], [P, QUAD, P], 1),
                                            LO[:, cols].unsqueeze(2).to_broadcast([P, QUAD, P]), ALU.is_equal)
                add(2)
                if valid(q) and n == 2:
                    nc.vector.tensor_tensor(HIH[:, slot, :, :], bc(iota[:, 0:NS], [P, QUAD, NS], 1),
                                            HI[:, cols].unsqueeze(2).to_broadcast([P, QUAD, NS]), ALU.is_equal
                                            ).then_inc(hist_ready, 1)
                add(3)
            steps(dve, step, 2)
            dve.wait_ge(ps[n]["rows_added"], T)

        @block.vector
        def _(dve):
            c = Chain(dve, dve_done)
            v_ = nc.vector

            def onehot(n, q, slot):
                if n == 0:
                    wait(dve, scored["st_turned"], q - 1)
                elif n == 1:
                    wait(dve, ps[1]["agg_done"], q - 1)
                else:
                    wait(dve, ps[n]["agg_done"], q - RING + 1)
                return v_.tensor_tensor(S[:, slot, :, :], bc(iota[:, :], [P, QUAD, P], 1),
                                        REL[:, bass.ds(q * QUAD, QUAD)].unsqueeze(2).to_broadcast([P, QUAD, P]),
                                        ALU.is_equal).then_inc(ps[n]["onehot_ready"], 1)

            def row_adder(n, acc, width, q, par, on=True):
                s = ps[n]
                if not (on and valid(q)):
                    return lambda j: None
                blocks = registers(dve, BROW, q, NB)

                def add(j):
                    rows = acc[:, bass.ds(blocks[j], 1), :].rearrange("p o d -> p (o d)")
                    if j == 0:
                        dve.wait_ge(s["agg_done"], q + 1)
                    wait(dve, s["rows_added"], q * QUAD + j)
                    v_.tensor_tensor(rows, rows, PSA[:, par, j, 0:width], ALU.add).then_inc(s["rows_added"], 1)
                return add

            def layer_norm(src, dst, relu=True, by=None):
                for b in range(NS):
                    v_.bn_stats(STATS[:, b, :], src[:, b, :]).then_inc(stats_taken, 1)
                norms[0] += 1
                dve.wait_ge(stats_taken, norms[0] * NS)
                mean0, sq0, mean1, sq1 = (STATS[:, :, k] for k in (1, 2, 4, 5))
                c(v_.tensor_tensor(st2[:, :], mean0, mean1, ALU.subtract))
                c(v_.tensor_tensor(st1[:, :], mean0, mean1, ALU.add))
                c(v_.tensor_tensor(sq0, sq0, sq1, ALU.add))
                c(v_.scalar_tensor_tensor(st2[:, :], st2[:, :], 0.25, st2[:, :], ALU.mult, ALU.mult))
                c(v_.scalar_tensor_tensor(st2[:, :], sq0, 1.0 / D, st2[:, :], ALU.mult, ALU.add))
                c(v_.tensor_scalar(st2[:, :], st2[:, :], EPS, None, ALU.add))
                root(st2)
                if by is not None:
                    c(v_.tensor_tensor(st2[:, :], st2[:, :], by[:, :], ALU.mult))
                c(v_.scalar_tensor_tensor(st1[:, :], st1[:, :], -0.5, st2[:, :], ALU.mult, ALU.mult))
                dve.sem_inc(factors_known, 1)
                for b in range(ON_ACT, NS):
                    v_.tensor_scalar(dst[:, b, :], src[:, b, :], st2[:, b:b + 1], st1[:, b:b + 1],
                                     ALU.mult, ALU.add).then_inc(normed_too, 1)
                dve.wait_ge(normed_too, norms[0] * (NS - ON_ACT))
                if relu:
                    c(v_.tensor_scalar(dst[:, ON_ACT:NS, :], dst[:, ON_ACT:NS, :], 0.0, None, ALU.max))
                dve.wait_ge(normed, norms[0] * ON_ACT)

            norms, roots = [0], [0]
            node = [P, NS, D]

            def root(t):
                dve.sem_inc(root_in, 1)
                roots[0] += 1
                dve.wait_ge(root_out, roots[0])
                c(v_.reciprocal(t[:, :], t[:, :]))

            def over(ap):
                return ap.unsqueeze(2).to_broadcast(node)

            def vec(k):
                return bc(ROWS[:, k, :], node, 1)

            dve.wait_ge(c_ready, 1)
            c(v_.tensor_copy(iota[:, :], iotaI))
            c(v_.tensor_copy(thr, thrI))
            c(v_.tensor_scalar(thr_half, thr, -0.5, None, ALU.add))
            c(v_.tensor_copy(identb[:, :], ident[:, :]))
            c(v_.memset(ones, 1.0))
            c(v_.memset(zer, 0.0))
            c(v_.memset(small[:, :], 1.0))
            c(v_.memset(cnt, 0.0))
            c(v_.memset(cum, 0.0))
            dve.wait_ge(dst_loaded, 16)
            v_.tensor_copy(DSTF, DSTI).then_inc(counted, 1)
            with dve.Fori(0, half) as b:
                dve.wait_ge(counted, b + 1)
                v_.tensor_scalar(JUNK, DSTF, thr[:, bass.ds(b, 1)], 0.0, ALU.is_lt, ALU.add,
                                 accum_out=cnt[:, bass.ds(b, 1)]).then_inc(counted, 1)
            dve.wait_ge(totals, 1)
            c(v_.tensor_copy(bf[:, 0:half], PB[0][:, 0:half]))
            c(v_.tensor_scalar(bf[:, half:NE], PB[0][:, half:NE], 0.5, float(P * TC) / 2, ALU.mult, ALU.add))
            c(v_.tensor_copy(bi, bf))
            c(v_.tensor_scalar(bi, bi, 4, 4, ALU.logical_shift_right, ALU.logical_shift_left))
            c(v_.tensor_copy(b16f, bi))
            c(v_.tensor_tensor(tiles_f[:, 0:NB], bf[:, 1:NE], b16f[:, 0:NB], ALU.subtract))
            c(v_.tensor_scalar(tiles_f[:, 0:NB], tiles_f[:, 0:NB], float(P - 1), None, ALU.add))
            c(v_.tensor_copy(ti32[:, 0:NB], tiles_f[:, 0:NB]))
            c(v_.tensor_scalar(ti32[:, 0:NB], ti32[:, 0:NB], 7, None, ALU.logical_shift_right))
            c(v_.tensor_copy(tiles_f[:, 0:NB], ti32[:, 0:NB]))
            c(v_.tensor_tensor_scan(cum[:, 1:NE], tiles_f[:, 0:NB], zer[:, 0:NB], 0.0, ALU.add, ALU.add))
            c(v_.scalar_tensor_tensor(rel0, cum, -float(P), b16f, ALU.mult, ALU.add))
            c(v_.tensor_copy(delta[:, 0:1], rel0[:, 0:1]))
            c(v_.tensor_tensor(delta[:, 1:NE], rel0[:, 1:NE], rel0[:, 0:NE - 1], ALU.subtract))
            c(v_.tensor_scalar(p15, pI, GROUP - 1, None, ALU.bitwise_and))
            c(v_.tensor_scalar(p4, pI, 4, None, ALU.logical_shift_right))
            c(v_.tensor_copy(p15f, p15))
            c(v_.tensor_copy(p4f, p4))
            c(v_.tensor_copy(grp, cI))
            c(v_.tensor_scalar(grp, grp, p4f, None, ALU.add))
            c(v_.tensor_scalar(tp, p15f, float(sz.chunk), None, ALU.mult))
            c(v_.tensor_scalar(tpos, grp, tp, None, ALU.add))
            for m in range(1, PARTS):
                c(v_.tensor_scalar(off, grp, float(m * sz.chunk), float((GROUP - 1) * sz.chunk), ALU.is_ge, ALU.mult))
                c(v_.tensor_tensor(tpos, tpos, off, ALU.add))
            c(v_.tensor_tensor(M, bc(cum, [P, NC, NE], 1), tpos.unsqueeze(2).to_broadcast([P, NC, NE]), ALU.is_le))
            c(v_.tensor_reduce(bt, M, AX.X, ALU.add))
            c(v_.tensor_scalar(bt, bt, -1.0, None, ALU.add))
            c(v_.tensor_tensor(MD, M, bc(delta, [P, NC, NE], 1), ALU.mult))
            c(v_.tensor_reduce(st, MD, AX.X, ALU.add))
            c(v_.scalar_tensor_tensor(st, tpos, float(P), st, ALU.mult, ALU.add))
            c(v_.tensor_scalar(st, st, float(sz.edge_end), None, ALU.min))
            c(v_.tensor_copy(bI, bt))
            c(v_.tensor_copy(sI, st))
            c(v_.tensor_scalar(wI, sI, 4, None, ALU.logical_shift_right))
            dve.sem_inc(windows_known, 1)
            c(v_.tensor_scalar(off, bt, -float(P), None, ALU.mult))
            dve.wait_ge(w_loaded, 16 * 13)
            dve.sem_inc(sig_in, 1)
            c(v_.tensor_copy(CTXB, CTXC.to_broadcast([CTX, P])))
            dve.sem_inc(film_in, 1)
            ntf = st1
            c(v_.tensor_copy(ntf[:, :], NTI))
            dve.wait_ge(sig_out, 1)
            c(v_.memset(ALPHA[:, :], 0.0))
            for t in range(TYPES):
                c(v_.tensor_scalar(MASK[:, :, t], ntf[:, :], float(t), None, ALU.is_equal))
                c(v_.scalar_tensor_tensor(ALPHA[:, :], MASK[:, :, t], SIG[:, t:t + 1], ALPHA[:, :], ALU.mult, ALU.add))
            c(v_.tensor_scalar(PRI.rearrange("p (h d) -> p h d", h=HEADS), PRI8.unsqueeze(2).to_broadcast([P, HEADS, DH]),
                               float(DH) ** -0.5, None, ALU.mult))
            dve.wait_ge(w_combined, 1)
            c(v_.tensor_copy(W3[:, :, 0:D], PB[1][:, 0:3 * D].rearrange("p (t d) -> p t d", t=3)))
            c(v_.tensor_copy(W3[:, :, D:2 * D], PB[2][:, 0:3 * D].rearrange("p (t d) -> p t d", t=3)))
            c(v_.tensor_tensor(ROWS[:, 3:5, :].rearrange("p a d -> p (a d)"), ROWS[:, 3:5, :].rearrange("p a d -> p (a d)"),
                               PB[3][:, 0:2 * D], ALU.add))
            dve.wait_ge(x_loaded, 16)
            layer_norm(X, H)
            dve.wait_ge(windows_in, 32 * NC)
            c(v_.tensor_copy(SRCF, SRCW))
            c(v_.tensor_copy(DKF, DSTW[:, :, 1:P + 1]))
            c(v_.tensor_tensor(RELF, DKF, off.unsqueeze(2).to_broadcast([P, NC, P]), ALU.add))
            c(v_.tensor_scalar(VAL, RELF, 0.0, None, ALU.is_ge))
            c(v_.scalar_tensor_tensor(VAL, RELF, float(P), VAL, ALU.is_lt, ALU.mult))
            c(v_.scalar_tensor_tensor(KEYW, DKF, 1.0, VAL, ALU.add, ALU.mult))
            c(v_.tensor_scalar(KEYW, KEYW, -1.0, None, ALU.add))
            c(v_.tensor_copy(prev.unsqueeze(2), DSTW[:, :, 0:1]))
            c(v_.tensor_tensor(STARTS[:, :, 1:P], KEYW[:, :, 1:P], KEYW[:, :, 0:P - 1], ALU.not_equal))
            c(v_.tensor_tensor(STARTS[:, :, 0:1], KEYW[:, :, 0:1], prev.unsqueeze(2), ALU.not_equal))
            c(v_.tensor_scalar(STARTS, STARTS, NEG, None, ALU.mult))
            c(v_.tensor_copy(kI.unsqueeze(2), KEYW[:, :, P - 1:P]))
            c(v_.memset(flags[:, :, sz.span:sz.span + 1], NEG))
            dve.sem_inc(tiles_masked, 1)
            dve.wait_ge(tiles_turned, 1)
            for k, dst in enumerate((REL, SRC)):
                for h in range(-(-NC // 4)):
                    n = min(4, NC - 4 * h) * P
                    c(v_.tensor_copy(dst[:, 4 * h * P:4 * h * P + n], PB[2 * k + h][:, 0:n]))
            dve.wait_ge(tiles_stored, 64)

            dve_proj(dve, 0)
            c(v_.tensor_tensor(MASK[:, :, :], MASK[:, :, :], ALPHA[:, :].unsqueeze(2).to_broadcast([P, NS, TYPES]), ALU.mult))
            c(v_.tensor_scalar(ALPHA[:, :], ALPHA[:, :], -1.0, 1.0, ALU.mult, ALU.add))
            c(v_.tensor_tensor(ROWS[:, 1, :], ROWS[:, 1, :], ROWS[:, 3, :], ALU.mult))
            c(v_.tensor_tensor(ROWS[:, 2, :], ROWS[:, 2, :], ROWS[:, 3, :], ALU.mult))
            c(v_.tensor_tensor(ROWS[:, 2, :], ROWS[:, 2, :], ROWS[:, 4, :], ALU.add))
            s, w = scored, weighted
            c(v_.memset(WM[:, :, :, D + HEADS:D + HEADS + 1], 1.0))
            hops = [0]

            def hop():
                dve.sem_inc(hop_in, 1)
                hops[0] += 1
                dve.wait_ge(hop_out, hops[0])

            def to_row(column, dst):
                c(v_.tensor_copy(small[:, 0:1], column))
                hop()
                c(v_.tensor_copy(dst, HOP[0:1, :].rearrange("o (t h) -> o h t", h=HEADS)))

            hc = lambda r: CLINE(r).rearrange("o (h t) -> o h t", h=HEADS)
            th = lambda r: CLINE(r).rearrange("o (t h) -> o h t", h=HEADS)
            carry = CLINE(4)[:, 0:HEADS].unsqueeze(2)
            before = CLINE(4)[:, 8:8 + HEADS]
            shift = CLINE(4)[:, 16:16 + HEADS]
            c(v_.memset(CLINE(4), 2 * NEG))

            def maxima(m):
                if m == 0:
                    dve.wait_ge(flags_in, 16 * flag_dmas)
                    dve.wait_ge(acc_cleared, 1)
                dve.wait_ge(s["grp_copied"], (m + 1) * sz.chunk)
                wait(dve, exp_out, m)
                at_m = AT[:, m % 2, :, :].rearrange("p g e -> p (g e)")
                ahead, behind = flags[:, m, 0:sz.span], flags[:, m, 1:sz.span + 1]
                c(v_.tensor_tensor_scan(FMAX, ahead, at_m, 2 * NEG, ALU.add, ALU.max))
                to_row(FMAX[:, sz.span - 1:sz.span], hc(0))
                c(v_.tensor_reduce(small[:, 1:2], ahead, AX.X, ALU.min))
                to_row(small[:, 1:2], hc(1))
                c(v_.tensor_copy(before, carry.rearrange("o h x -> o (h x)")))
                c(v_.tensor_tensor(hc(1)[:, :, 0:1], hc(1)[:, :, 0:1], carry, ALU.add))
                c(v_.tensor_tensor(hc(0)[:, :, 0:1], hc(0)[:, :, 0:1], hc(1)[:, :, 0:1], ALU.max))
                c(v_.memset(hc(1)[:, :, 0:1], 2 * NEG))
                c(v_.tensor_tensor_scan(CLINE(2), CLINE(1), CLINE(0), 4 * NEG, ALU.add, ALU.max))
                c(v_.tensor_copy(th(3)[:, :, 1:GROUP], hc(2)[:, :, 0:GROUP - 1]))
                c(v_.tensor_copy(th(3)[:, :, 0:1], carry))
                c(v_.tensor_copy(carry, hc(2)[:, :, GROUP - 1:GROUP]))
                hop()
                c(v_.tensor_copy(small[:, 2:3], HOP[:, 0:1]))
                c(v_.tensor_tensor_scan(FMAX, ahead, FMAX, small[:, 2:3], ALU.add, ALU.max))
                fb, bb = FMAX[:, ::-1], behind[:, ::-1]
                c(v_.tensor_tensor_scan(fb, bb, fb, 2 * NEG, ALU.add, ALU.max))
                to_row(FMAX[:, 0:1], hc(0))
                c(v_.tensor_reduce(small[:, 1:2], behind, AX.X, ALU.min))
                to_row(small[:, 1:2], hc(1))
                c(v_.memset(hc(1)[:, :, GROUP - 1:GROUP], 2 * NEG))
                c(v_.tensor_tensor_scan(CLINE(2)[:, ::-1], CLINE(1)[:, ::-1], CLINE(0)[:, ::-1], 4 * NEG, ALU.add, ALU.max))
                c(v_.memset(CLINE(3), 2 * NEG))
                c(v_.tensor_copy(th(3)[:, :, 0:GROUP - 1], hc(2)[:, :, 1:GROUP]))
                hop()
                c(v_.tensor_copy(small[:, 2:3], HOP[:, 0:1]))
                c(v_.tensor_tensor_scan(fb, bb, fb, small[:, 2:3], ALU.add, ALU.max))
                if m:
                    to_row(FMAX[:, 0:1], hc(0))
                    c(v_.tensor_tensor(shift, before, hc(0)[:, :, 0:1].rearrange("o h x -> o (h x)"), ALU.subtract))
                    c(v_.tensor_scalar(CLINE(4)[:, 32:33], flags[0:1, m, 0:1], -1.0, None, ALU.is_ge))
                    c(v_.tensor_scalar(shift, shift, CLINE(4)[:, 32:33], None, ALU.mult))
                    dve.sem_inc(scale_in, 1)
                c(v_.tensor_tensor(FMAX, at_m, FMAX, ALU.subtract))
                dve.sem_inc(exp_in, 1)

            def rescale(m):
                k = m * sz.chunk * GROUP - 1
                block_col = BROW[0:1, k:k + 1]
                c(v_.tensor_copy(CLINE(4)[:, 33:34], block_col))
                c(v_.tensor_copy(CLINE(4)[:, 35:36], LASTK[0:1, m:m + 1]))
                c(v_.scalar_tensor_tensor(CLINE(4)[:, 34:35], CLINE(4)[:, 33:34], -float(P), CLINE(4)[:, 35:36], ALU.mult, ALU.add))
                c(v_.tensor_scalar(CLINE(5), iota[0:1, :], CLINE(4)[:, 34:35], None, ALU.is_equal))
                dve.wait_ge(scale_out, m)
                c(v_.tensor_scalar(CLINE(4)[:, 24:24 + HEADS], CLINE(4)[:, 24:24 + HEADS], -1.0, None, ALU.add))
                hop()
                c(v_.tensor_scalar(small[:, 4:4 + HEADS], HOP[:, 0:HEADS], 1.0, None, ALU.add))
                b = nc.values_load(block_col, engines=[dve.engine], min_val=0, max_val=NB,
                                   skip_runtime_bounds_check_because=reg_note)
                row = acc0[:, bass.ds(b, 1), :].rearrange("p o d -> p (o d)")
                sums = row[:, 0:D].rearrange("p (h d) -> p h d", h=HEADS)
                c(v_.tensor_tensor(sums, sums, small[:, 4:4 + HEADS].unsqueeze(2).to_broadcast([P, HEADS, DH]), ALU.mult))
                c(v_.tensor_tensor(row[:, D:D + HEADS], row[:, D:D + HEADS], small[:, 4:4 + HEADS], ALU.mult))

            def step(i, u, scores, messages):
                q, slot, turn, v = at(i, u, 0)
                if scores and valid(q):
                    onehot(0, q, v % 2)
                q, slot, turn, v = at(i - LAG, u, -4)
                add = row_adder(1, acc0, WMW, q, v % 2, messages)
                add(0)
                qm, mslot, mturn, mv = at(i - LAG, u, -2)
                weigh = messages and valid(qm)
                if weigh:
                    onehot(1, qm, 2 + mv % 2)
                add(1)
                q, slot, turn, v = at(i, u, -2)
                score = scores and valid(q)
                if score:
                    dve.wait_ge(s["q_spread"], q + 1)
                    dve.wait_ge(ps[0]["gathered"][slot], (turn + 1) * 64)
                    wait(dve, s["reduced"], q - 1)
                    v_.tensor_tensor(PROD[:, v % 2, :, :], G2[:, slot, :, 0:D], QD[v % 2], ALU.mult).then_inc(s["multiplied"], 1)
                add(2)
                if weigh:
                    dve.wait_ge(mv_loaded[mslot], (mturn + 1) * 16)
                    dve.wait_ge(w["prob_put"], qm + 1)
                    wait(dve, ps[1]["agg_done"], qm - 1)
                    probs = AE[:, (mv // 4) % 2, (mv % 4) * 32:(mv % 4) * 32 + 32]
                    v_.tensor_tensor(
                        WM[:, mv % 2, :, 0:D].rearrange("p j (h d) -> p j h d", h=HEADS),
                        MV[:, mslot, :, :].rearrange("p j (h d) -> p j h d", h=HEADS),
                        probs.rearrange("p (j h) -> p j h", j=QUAD).unsqueeze(3).to_broadcast([P, QUAD, HEADS, DH]),
                        ALU.mult).then_inc(w["weighted"], 1)
                add(3)
                if score:
                    dve.wait_ge(s["multiplied"], q + 1)
                    if v % 4 == 0:
                        wait(dve, s["grp_turned"], group_of(i, u, -2) - 1)
                    v_.tensor_reduce(ABUF[:, (v // 4) % 2, (v % 4) * 32:(v % 4) * 32 + 32].rearrange("p (j h) -> p j h", j=QUAD),
                                     PROD[:, v % 2, :, :].rearrange("p j (h d) -> p j h d", h=HEADS), AX.X, ALU.add
                                     ).then_inc(s["reduced"], 1)
                if isinstance(i, int) and i in hooks[1:] and u == 3:
                    dve.wait_ge(ps[1]["rows_added"], hooks.index(i) * sz.chunk * GROUP)
                    rescale(hooks.index(i))
                    dve.sem_inc(rescaled, 1)
            layer0_steps(dve, step, maxima)
            dve.sem_inc(w_free, 1)
            dve.wait_ge(ps[1]["rows_added"], T)
            c(v_.tensor_copy(DEG[:, :], acc0[:, :, D + HEADS:D + HEADS + 1].rearrange("p b o -> p (b o)")))
            probs = acc0[:, :, D:D + HEADS]
            c(v_.tensor_scalar(probs, probs, 0.5, None, ALU.max))
            c(v_.reciprocal(probs, probs))
            for h in range(HEADS):
                c(v_.tensor_tensor(acc0[:, :, h * DH:(h + 1) * DH], acc0[:, :, h * DH:(h + 1) * DH],
                                   acc0[:, :, D + h:D + h + 1].to_broadcast([P, NS, DH]), ALU.mult))
            dve.wait_ge(w_next, 16)
            dve.wait_ge(pool_added, 4)
            dve_proj(dve, 1)
            layer_norm(QT, QT, relu=False)
            c(v_.tensor_tensor(QT, QT, vec(1), ALU.mult))
            c(v_.tensor_tensor(X[:, :, :], X[:, :, :], QT, ALU.add))

            c(v_.tensor_scalar(ALPHA[:, :], DEG[:, :], 1.0, 1.0, ALU.add, ALU.max))
            root(ALPHA)
            layer_norm(X, H, by=ALPHA)
            dve.sem_inc(table_made, 1)
            c(v_.tensor_copy(acc1, H[:, :, :]))
            dve.wait_ge(hist_in, 16)
            c(v_.tensor_scalar(SRCTMP, SRCPM, P - 1, None, ALU.bitwise_and))
            c(v_.tensor_copy(LO, SRCTMP))
            c(v_.tensor_scalar(SRCTMP, SRCPM, 7, None, ALU.logical_shift_right))
            c(v_.tensor_copy(HI, SRCTMP))
            plain(dve, 2, onehot, row_adder)
            c(v_.tensor_scalar(OUTDEG[:, :], HISTP, 1.0, 1.0, ALU.add, ALU.max))
            root(OUTDEG)
            c(v_.tensor_tensor(acc1, acc1, over(OUTDEG[:, :]), ALU.mult))
            c(v_.tensor_tensor(X[:, :, :], X[:, :, :], acc1, ALU.add))

            layer_norm(X, H)
            dve.wait_ge(w_next, 16 * 7)
            dve_proj(dve, 2)
            dve.wait_ge(acc_cleared, 2)
            s = gated

            def step(i, u):
                q, slot, turn, v = at(i, u, -4)
                add = row_adder(3, acc2, 2 * D, q, v % 2)
                q, slot, turn, v = at(i, u, -3)
                if valid(q):
                    dve.wait_ge(s["gate_done"], q + 1)
                    v_.tensor_tensor(RHS[:, v % 2, :, 0:D], G2[:, slot, :, D:2 * D], RHS[:, v % 2, :, D:2 * D],
                                     ALU.mult).then_inc(s["multiplied"], 1)
                add(0)
                q, slot, turn, v = at(i, u, -2)
                if valid(q):
                    dve.wait_ge(s["pre_done"], q + 1)
                    dve.wait_ge(ps[3]["gathered"][slot], (turn + 1) * 64)
                    wait(dve, s["gate_done"], q - 1)
                    v_.tensor_tensor(PRE[:, v % 2, :, :], QD[v % 2], G2[:, slot, :, 0:D], ALU.add).then_inc(s["summed"], 1)
                add(1)
                q, slot, turn, v = at(i, u, 0)
                if valid(q):
                    onehot(3, q, slot)
                add(2)
                add(3)
            steps(dve, step, 4)
            dve.wait_ge(ps[3]["rows_added"], T)
            dve.wait_ge(pool_added, 5)
            norm, summed = acc2[:, :, D:2 * D], acc2[:, :, 0:D]
            c(v_.tensor_scalar(norm, norm, 1e-6, None, ALU.max))
            c(v_.reciprocal(norm, norm))
            c(v_.tensor_tensor(summed, summed, norm, ALU.mult))
            c(v_.tensor_tensor(summed, summed, H[:, :, :], ALU.add))
            c(v_.tensor_tensor(X[:, :, :], X[:, :, :], summed, ALU.add))

            layer_norm(X, H)
            dve.sem_inc(table_made, 1)
            c(v_.memset(acc1, 0.0))
            plain(dve, 4, onehot, row_adder)
            c(v_.tensor_scalar(st1[:, :], DEG[:, :], 1.0, None, ALU.max))
            c(v_.reciprocal(st1[:, :], st1[:, :]))
            c(v_.tensor_tensor(QT, acc1, over(st1[:, :]), ALU.mult))
            dve.wait_ge(w_next, 16 * 12)
            dve_proj(dve, 3)
            c(v_.tensor_tensor(QT, QT, vec(0), ALU.add))
            layer_norm(QT, QT, relu=False)
            c(v_.tensor_tensor(QT, QT, vec(1), ALU.mult))
            c(v_.tensor_tensor(QT, QT, vec(2), ALU.add))
            dve.sem_inc(gelu_in, 1)
            dve.wait_ge(gelu_out, 1)
            c(v_.tensor_tensor(X[:, :, :], X[:, :, :], QT, ALU.add))
            dve.sem_inc(x_final, 1)


def kernel(x, src, dst, edge_attr_128, node_type_3, **w):
    import concourse.bacc as _bacc
    from concourse.bass_utils import run_bass_kernel_spmd as _run

    x, src, dst, ea, ntype = (np.asarray(v) for v in (x, src, dst, edge_attr_128, node_type_3))
    w = {k: np.asarray(v) for k, v in w.items()}
    sz = Sizes(x.shape[0], src.shape[0])
    rows = sz.slots * P
    cont = np.ascontiguousarray

    def padded(v, n, value):
        out = np.full((n,) + v.shape[1:], value, v.dtype)
        out[:v.shape[0]] = v
        return out

    def windows(v, value, before=0):
        v = np.concatenate([np.full(before, value, v.dtype), padded(v, sz.edge_end + P, value)])
        return cont(np.lib.stride_tricks.sliding_window_view(v, P + before)[::ALIGN])

    def by_head(m):
        out = np.zeros((D, D), m.dtype)
        for h in range(HEADS):
            out[h * DH:(h + 1) * DH, h * DH:(h + 1) * DH] = m[h]
        return out

    arrays = {
        "x": padded(x, rows, 0),
        "src_win": windows(src, 0), "dst_win": windows(dst, PAD_NODE, 1),
        "src_pm": padded(src, P * sz.tiles, sz.blocks * P).reshape(P, sz.tiles),
        "dst_pm": padded(dst, P * (-(-sz.edges // P)), PAD_NODE).reshape(P, -1),
        "ea_t": cont(padded(ea, sz.edge_end + P, 0).T),
        "ntype": cont(padded(ntype, rows, 0).reshape(sz.slots, P).T),
        "ctx": w["L0_gnn_global_context"],
        "wk_t": cont(w["L0_gnn_Wk"].transpose(0, 2, 1)), "wv_t": cont(w["L0_gnn_Wv"].transpose(0, 2, 1)),
        "wq": w["L0_gnn_Wq"], "att": by_head(w["L0_gnn_rel_att"]), "msg": by_head(w["L0_gnn_rel_msg"]),
        "pri": w["L0_gnn_rel_pri"], "wa": w["L0_gnn_Wa"], "skip": w["L0_gnn_skip"],
        "ln_g": w["L0_gnn_ln_g"], "ln_b": w["L0_gnn_ln_b"], "film_w": w["L0_gnn_film_w"], "film_b": w["L0_gnn_film_b"],
        "w_root": w["L2_gnn_W_root"], "b_root": w["L2_gnn_b_root"], "w_msg": w["L2_gnn_W_msg"],
        "w_src": w["L2_gnn_W_src"], "w_dst": w["L2_gnn_W_dst"], "w_edge": w["L2_gnn_W_edge"],
        "w_l": w["L3_gnn_W_l"], "b_l": w["L3_gnn_b_l"], "w_r": w["L3_gnn_W_r"],
        "gamma": w["L3_gnn_gamma"], "beta": w["L3_gnn_beta"],
    }
    nc = _bacc.Bacc("TRN2", target_bir_lowering=False, num_devices=1)
    a, feeds = {}, {}
    for name, v in arrays.items():
        feeds[f"in_{name}"] = cont(v)
        a[name] = nc.dram_tensor(f"in_{name}", v.shape, mybir.dt.from_np(v.dtype), kind="ExternalInput").ap()
    a["out"] = nc.dram_tensor("out_x", (sz.nodes, D), F32, kind="ExternalOutput").ap()
    build(nc, sz, a)
    return _run(nc, [feeds], core_ids=[0]).results[0]["out_x"]
```
